# Optimizing a Trainium2 kernel written in Bass

```python
import numpy as np
import jax
import jax.numpy as jnp

def _softmax(x, axis=-1):
    return jax.nn.softmax(x, axis=axis)

def _gelu(x):
    return jax.nn.gelu(x, approximate=True)

def _silu(x):
    return jax.nn.silu(x)

def _sigmoid(x):
    return jax.nn.sigmoid(x)

def _layernorm(x, axis=-1, eps=1e-05):
    m = jnp.mean(x, axis=axis, keepdims=True)
    v = jnp.var(x, axis=axis, keepdims=True)
    return (x - m) / jnp.sqrt(v + eps)

def _scatter_add(tgt, idx, src, axis=0):
    return tgt.at[idx].add(src)

def _segment_sum(src, seg, n):
    return jax.ops.segment_sum(src, seg, n)
kernel_name = 'mk_gps_d2_gnn_r32_75126b'

def setup_inputs(seed: int=0):
    np.random.seed(seed)
    _w = jnp.asarray

    def _rec_inputs():
        import jax
        import jax.numpy as jnp
        _gk = jax.random.key(seed)
        x = -0.0002928 + 1 * jax.random.normal(jax.random.fold_in(_gk, 1), (256, 512), jnp.float32)
        src = jax.random.randint(jax.random.fold_in(_gk, 2), (8192,), 0, 256, jnp.int32)
        dst = jax.random.randint(jax.random.fold_in(_gk, 3), (8192,), 0, 256, jnp.int32)
        _o = jnp.argsort(dst, stable=True)
        src = src[_o]
        dst = dst[_o]
        return (x, src, dst)
    x, src, dst = _rec_inputs()

    def _L0_gnn_setup():
        import jax, jax.numpy as jnp
        import numpy as np
        N = 256
        D = 512
        E = 8192
        STEPS = 3
        key = jax.random.key(seed)
        k1, k2, k3 = jax.random.split(key, 3)
        x = jax.random.normal(k1, (N, D), dtype=jnp.float32)
        edge_index = jax.random.randint(k2, (2, E), 0, N, dtype=jnp.int32)
        W = jax.random.normal(k3, (D, D), dtype=jnp.float32) / np.sqrt(D)
        b = jnp.zeros((D,), dtype=jnp.float32)
        diffusion_weights = jnp.ones((STEPS + 1,), dtype=jnp.float32) / (STEPS + 1)
        return {'x': x, 'edge_index': edge_index, 'W': W, 'b': b, 'diffusion_weights': diffusion_weights}
    _L0_gnn_all = _L0_gnn_setup()
    _L0_gnn_in = {k: v for k, v in _L0_gnn_all.items() if k in ('W', 'b', 'diffusion_weights')}
    del _L0_gnn_all

    def _L0_mix_setup():
        import jax, jax.numpy as jnp
        import numpy as np
        EPS = 1e-05

        def gamma_layer_norm(x, gamma):
            mu = jnp.mean(x, axis=-1, keepdims=True)
            var = jnp.var(x, axis=-1, keepdims=True)
            return (x - mu) * jax.lax.rsqrt(var + EPS) * gamma
        key = jax.random.key(seed)
        k1, k2, k3, k4 = jax.random.split(key, 4)
        b, n, dim = (8, 128, 512)
        heads, head_size = (8, 64)
        hidden = heads * head_size
        x = jax.random.normal(k1, (b, n, dim), dtype=jnp.float32)
        w_qkv = jax.random.normal(k2, (3 * hidden, dim), dtype=jnp.float32) * dim ** (-0.5)
        w_out = jax.random.normal(k3, (dim, hidden), dtype=jnp.float32) * hidden ** (-0.5)
        gamma = 1.0 + 0.02 * jax.random.normal(k4, (dim,), dtype=jnp.float32)
        return {'x': x, 'w_qkv': w_qkv, 'w_out': w_out, 'gamma': gamma}
    _L0_mix_all = _L0_mix_setup()
    _L0_mix_in = {k: v for k, v in _L0_mix_all.items() if k in ('w_qkv', 'w_out', 'gamma')}
    del _L0_mix_all

    def _L0_ffn_setup():
        import jax, jax.numpy as jnp
        import numpy as np
        MIN_EXPERT_CAPACITY = 4
        EPS = 1e-09
        CAPACITY_FACTOR = 2.0

        def cumsum_exclusive(t, axis):
            return jnp.cumsum(t, axis=axis) - t

        def safe_one_hot(idx, depth):
            return jax.nn.one_hot(idx, depth + 1)[..., :depth]

        def top2_gating(x, w_gating):
            b, n, d = x.shape
            e = w_gating.shape[-1]
            raw_gates = jax.nn.softmax(jnp.einsum('bnd,de->bne', x, w_gating), axis=-1)
            gate_1 = jnp.max(raw_gates, axis=-1)
            index_1 = jnp.argmax(raw_gates, axis=-1)
            mask_1 = jax.nn.one_hot(index_1, e, dtype=raw_gates.dtype)
            gates_without_top1 = raw_gates * (1.0 - mask_1)
            gate_2 = jnp.max(gates_without_top1, axis=-1)
            index_2 = jnp.argmax(gates_without_top1, axis=-1)
            mask_2 = jax.nn.one_hot(index_2, e, dtype=raw_gates.dtype)
            denom = gate_1 + gate_2 + EPS
            gate_1 = gate_1 / denom
            gate_2 = gate_2 / denom
            density_1 = jnp.mean(mask_1, axis=-2)
            density_1_proxy = jnp.mean(raw_gates, axis=-2)
            loss = jnp.mean(density_1_proxy * density_1) * float(e * e)
            capacity = max(min(n, int(n * 2 * CAPACITY_FACTOR / e)), MIN_EXPERT_CAPACITY)
            cap_f = float(capacity)
            pos1 = cumsum_exclusive(mask_1, axis=-2) * mask_1
            mask_1 = mask_1 * (pos1 < cap_f).astype(mask_1.dtype)
            mask_1_count = jnp.sum(mask_1, axis=-2, keepdims=True)
            mask_1_flat = jnp.sum(mask_1, axis=-1)
            pos1 = jnp.sum(pos1, axis=-1)
            gate_1 = gate_1 * mask_1_flat
            pos2 = (cumsum_exclusive(mask_2, axis=-2) + mask_1_count) * mask_2
            mask_2 = mask_2 * (pos2 < cap_f).astype(mask_2.dtype)
            mask_2_flat = jnp.sum(mask_2, axis=-1)
            pos2 = jnp.sum(pos2, axis=-1)
            gate_2 = gate_2 * mask_2_flat
            combine = gate_1[..., None, None] * mask_1_flat[..., None, None] * jax.nn.one_hot(index_1, e, dtype=x.dtype)[..., None] * safe_one_hot(pos1.astype(jnp.int32), capacity)[..., None, :] + gate_2[..., None, None] * mask_2_flat[..., None, None] * jax.nn.one_hot(index_2, e, dtype=x.dtype)[..., None] * safe_one_hot(pos2.astype(jnp.int32), capacity)[..., None, :]
            dispatch = (combine > 0).astype(combine.dtype)
            return (dispatch, combine, loss)
        key = jax.random.key(seed)
        k_x, k_g, k_w1, k_w2 = jax.random.split(key, 4)
        b, n, d, e, h = (2, 128, 512, 16, 64)
        x = jax.random.normal(k_x, (b, n, d), dtype=jnp.float32)
        w_gating = jax.random.normal(k_g, (d, e), dtype=jnp.float32) / np.sqrt(d)
        w1 = jax.random.normal(k_w1, (e, d, h), dtype=jnp.float32) / np.sqrt(d)
        w2 = jax.random.normal(k_w2, (e, h, d), dtype=jnp.float32) / np.sqrt(h)
        return {'x': x, 'w_gating': w_gating, 'w1': w1, 'w2': w2}
    _L0_ffn_all = _L0_ffn_setup()
    _L0_ffn_in = {k: v for k, v in _L0_ffn_all.items() if k in ('w_gating', 'w1', 'w2')}
    del _L0_ffn_all

    def _L1_gnn_setup():
        import jax, jax.numpy as jnp
        import numpy as np
        N = 625
        E = 10000
        LN_EPS = 1e-05
        NEG_SLOPE = 0.2

        def _segment_softmax(logits, seg, num_segments):
            m = jax.ops.segment_max(logits, seg, num_segments=num_segments)
            e = jnp.exp(logits - m[seg])
            s = jax.ops.segment_sum(e, seg, num_segments=num_segments)
            return e / s[seg]

        def _gat_conv(x, src, dst, W, a_s, a_d, b, concat):
            H, C = a_s.shape
            n = x.shape[0]
            h = (x @ W).reshape(n, H, C)
            alpha_s = jnp.einsum('nhc,hc->nh', h, a_s)
            alpha_d = jnp.einsum('nhc,hc->nh', h, a_d)
            logits = jax.nn.leaky_relu(alpha_s[src] + alpha_d[dst], NEG_SLOPE)
            alpha = _segment_softmax(logits, dst, n)
            msg = h[src] * alpha[:, :, None]
            out = jax.ops.segment_sum(msg, dst, num_segments=n)
            out = out.reshape(n, H * C) if concat else out.mean(axis=1)
            return out + b

        def _layer_norm(x, g, beta):
            mu = jnp.mean(x, axis=-1, keepdims=True)
            var = jnp.var(x, axis=-1, keepdims=True)
            return (x - mu) * jax.lax.rsqrt(var + LN_EPS) * g + beta

        def _forward(x, edge_index, W1, a_src1, a_dst1, b1, g1, beta1, W2, a_src2, a_dst2, b2, g2, beta2):
            n = x.shape[0]
            loops = jnp.arange(n, dtype=edge_index.dtype)
            src = jnp.concatenate([edge_index[0], loops])
            dst = jnp.concatenate([edge_index[1], loops])
            x_new = _gat_conv(x, src, dst, W1, a_src1, a_dst1, b1, concat=True)
            x_new = jax.nn.elu(_layer_norm(x_new, g1, beta1))
            x = x + x_new
            x_new = _gat_conv(x, src, dst, W2, a_src2, a_dst2, b2, concat=False)
            x_new = jax.nn.elu(_layer_norm(x_new, g2, beta2))
            return x + x_new
        key = jax.random.key(seed)
        ks = jax.random.split(key, 12)
        d = {}
        d['x'] = jax.random.normal(ks[0], (N, 512), dtype=jnp.float32)
        d['edge_index'] = jax.random.randint(ks[1], (2, E), 0, N, dtype=jnp.int64)
        s = 1.0 / np.sqrt(512.0)
        d['W1'] = jax.random.normal(ks[2], (512, 512), dtype=jnp.float32) * s
        d['a_src1'] = jax.random.normal(ks[3], (8, 64), dtype=jnp.float32) * s
        d['a_dst1'] = jax.random.normal(ks[4], (8, 64), dtype=jnp.float32) * s
        d['b1'] = jnp.zeros((512,), jnp.float32)
        d['g1'] = jnp.ones((512,), jnp.float32)
        d['beta1'] = jnp.zeros((512,), jnp.float32)
        d['W2'] = jax.random.normal(ks[5], (512, 512), dtype=jnp.float32) * s
        d['a_src2'] = jax.random.normal(ks[6], (1, 512), dtype=jnp.float32) * s
        d['a_dst2'] = jax.random.normal(ks[7], (1, 512), dtype=jnp.float32) * s
        d['b2'] = jnp.zeros((512,), jnp.float32)
        d['g2'] = jnp.ones((512,), jnp.float32)
        d['beta2'] = jnp.zeros((512,), jnp.float32)
        return d
    _L1_gnn_all = _L1_gnn_setup()
    _L1_gnn_in = {k: v for k, v in _L1_gnn_all.items() if k in ('W1', 'a_src1', 'a_dst1', 'b1', 'g1', 'beta1', 'W2', 'a_src2', 'a_dst2', 'b2', 'g2', 'beta2')}
    del _L1_gnn_all

    def _L1_mix_setup():
        import jax, jax.numpy as jnp
        import numpy as np
        DIM = 512
        HEADS = 8
        DIM_HEAD = 64
        INNER = HEADS * DIM_HEAD
        B, N = (4, 256)
        key = jax.random.key(seed)
        k1, k2, k3, k4 = jax.random.split(key, 4)
        x = jax.random.normal(k1, (B, N, DIM), dtype=jnp.float32)
        W_qkv = jax.random.normal(k2, (DIM, 3 * INNER), dtype=jnp.float32) / np.sqrt(DIM)
        W_out = jax.random.normal(k3, (INNER, DIM), dtype=jnp.float32) / np.sqrt(INNER)
        b_out = jax.random.normal(k4, (DIM,), dtype=jnp.float32) * 0.01
        return {'x': x, 'W_qkv': W_qkv, 'W_out': W_out, 'b_out': b_out}
    _L1_mix_all = _L1_mix_setup()
    _L1_mix_in = {k: v for k, v in _L1_mix_all.items() if k in ('W_qkv', 'W_out', 'b_out')}
    del _L1_mix_all

    def _L1_ffn_setup():
        import jax, jax.numpy as jnp
        import numpy as np
        import math
        E, K, CAPF = (8, 2, 1.25)
        D, DFF = (512, 64)

        def _moe(x, Wr, br, W1, b1, W2, b2):
            orig = x.shape
            d = orig[-1]
            xf = x.reshape(-1, d)
            N = xf.shape[0]
            logits = xf @ Wr + br
            probs = jax.nn.softmax(logits, axis=-1)
            topk_p, topk_i = jax.lax.top_k(probs, K)
            topk_w = topk_p / (jnp.sum(topk_p, axis=-1, keepdims=True) + 1e-09)
            cap = max(1, int(math.ceil(CAPF * float(N * K) / float(E))))
            flat_e = topk_i.reshape(-1)
            flat_w = topk_w.reshape(-1)
            tok = jnp.repeat(jnp.arange(N), K)
            one_hot = jax.nn.one_hot(flat_e, E, dtype=xf.dtype)
            pos = (jnp.cumsum(one_hot, axis=0) - one_hot)[jnp.arange(N * K), flat_e]
            pos = pos.astype(jnp.int32)
            keep = pos < cap
            w_k = jnp.where(keep, flat_w, 0.0)
            sum_w = jnp.zeros((N,), xf.dtype).at[tok].add(w_k)
            w_norm = w_k / (sum_w[tok] + 1e-09)
            slot = flat_e * cap + pos
            slot_safe = jnp.where(keep, slot, E * cap)
            expert_in = jnp.zeros((E * cap, d), xf.dtype).at[slot_safe].set(xf[tok], mode='drop').reshape(E, cap, d)
            h = jax.nn.gelu(jnp.einsum('ecd,edf->ecf', expert_in, W1) + b1[:, None, :], approximate=False)
            expert_out = (jnp.einsum('ecf,efd->ecd', h, W2) + b2[:, None, :]).reshape(E * cap, d)
            contrib = expert_out[jnp.where(keep, slot, 0)]
            y = jnp.zeros((N, d), xf.dtype).at[tok].add(contrib * w_norm[:, None])
            return y.reshape(orig)
        key = jax.random.key(seed)
        ks = jax.random.split(key, 5)
        s = lambda k, sh, sc: jax.random.normal(k, sh, jnp.float32) * sc
        return {'x': jax.random.normal(ks[0], (8, 128, D), jnp.float32), 'Wr': s(ks[1], (D, E), 1.0 / math.sqrt(D)), 'br': jnp.zeros((E,), jnp.float32), 'W1': s(ks[2], (E, D, DFF), 1.0 / math.sqrt(D)), 'b1': jnp.zeros((E, DFF), jnp.float32), 'W2': s(ks[3], (E, DFF, D), 1.0 / math.sqrt(DFF)), 'b2': jnp.zeros((E, D), jnp.float32)}
    _L1_ffn_all = _L1_ffn_setup()
    _L1_ffn_in = {k: v for k, v in _L1_ffn_all.items() if k in ('Wr', 'br', 'W1', 'b1', 'W2', 'b2')}
    del _L1_ffn_all
    return {'x': x, 'src': src, 'dst': dst, 'L0_gnn_W': _L0_gnn_in['W'], 'L0_gnn_b': _L0_gnn_in['b'], 'L0_gnn_diffusion_weights': _L0_gnn_in['diffusion_weights'], 'L0_mix_w_qkv': _L0_mix_in['w_qkv'], 'L0_mix_w_out': _L0_mix_in['w_out'], 'L0_mix_gamma': _L0_mix_in['gamma'], 'L0_ffn_w_gating': _L0_ffn_in['w_gating'], 'L0_ffn_w1': _L0_ffn_in['w1'], 'L0_ffn_w2': _L0_ffn_in['w2'], 'L1_gnn_W1': _L1_gnn_in['W1'], 'L1_gnn_a_src1': _L1_gnn_in['a_src1'], 'L1_gnn_a_dst1': _L1_gnn_in['a_dst1'], 'L1_gnn_b1': _L1_gnn_in['b1'], 'L1_gnn_g1': _L1_gnn_in['g1'], 'L1_gnn_beta1': _L1_gnn_in['beta1'], 'L1_gnn_W2': _L1_gnn_in['W2'], 'L1_gnn_a_src2': _L1_gnn_in['a_src2'], 'L1_gnn_a_dst2': _L1_gnn_in['a_dst2'], 'L1_gnn_b2': _L1_gnn_in['b2'], 'L1_gnn_g2': _L1_gnn_in['g2'], 'L1_gnn_beta2': _L1_gnn_in['beta2'], 'L1_mix_W_qkv': _L1_mix_in['W_qkv'], 'L1_mix_W_out': _L1_mix_in['W_out'], 'L1_mix_b_out': _L1_mix_in['b_out'], 'L1_ffn_Wr': _L1_ffn_in['Wr'], 'L1_ffn_br': _L1_ffn_in['br'], 'L1_ffn_W1': _L1_ffn_in['W1'], 'L1_ffn_b1': _L1_ffn_in['b1'], 'L1_ffn_W2': _L1_ffn_in['W2'], 'L1_ffn_b2': _L1_ffn_in['b2']}

def reference(x, src, dst, L0_gnn_W, L0_gnn_b, L0_gnn_diffusion_weights, L0_mix_w_qkv, L0_mix_w_out, L0_mix_gamma, L0_ffn_w_gating, L0_ffn_w1, L0_ffn_w2, L1_gnn_W1, L1_gnn_a_src1, L1_gnn_a_dst1, L1_gnn_b1, L1_gnn_g1, L1_gnn_beta1, L1_gnn_W2, L1_gnn_a_src2, L1_gnn_a_dst2, L1_gnn_b2, L1_gnn_g2, L1_gnn_beta2, L1_mix_W_qkv, L1_mix_W_out, L1_mix_b_out, L1_ffn_Wr, L1_ffn_br, L1_ffn_W1, L1_ffn_b1, L1_ffn_W2, L1_ffn_b2):
    import jax
    import jax.numpy as jnp

    def _L0_gnn_ref(x, edge_index, W, b, diffusion_weights):
        import jax, jax.numpy as jnp
        import numpy as np
        N = 256
        D = 512
        E = 8192
        STEPS = 3
        h = x @ W + b
        row, col = (edge_index[0], edge_index[1])
        adj = jnp.zeros((N, N), dtype=h.dtype)
        adj = adj.at[row, col].set(1.0)
        adj = adj.at[col, row].set(1.0)
        adj = adj + jnp.eye(N, dtype=h.dtype)
        row_sum = adj.sum(axis=1, keepdims=True)
        adj = adj / jnp.maximum(row_sum, 1.0)
        out = diffusion_weights[0] * h
        cur = h
        for i in range(STEPS):
            cur = adj @ cur
            out = out + diffusion_weights[i + 1] * cur
        return jax.nn.relu(out)

    def _L0_mix_ref(x, w_qkv, w_out, gamma):
        import jax, jax.numpy as jnp
        import numpy as np
        EPS = 1e-05

        def gamma_layer_norm(x, gamma):
            mu = jnp.mean(x, axis=-1, keepdims=True)
            var = jnp.var(x, axis=-1, keepdims=True)
            return (x - mu) * jax.lax.rsqrt(var + EPS) * gamma
        b, n, dim = x.shape
        heads, head_size = (8, 64)
        scale = head_size ** (-0.5)
        qkv = jnp.einsum('bnd,hd->bnh', x, w_qkv)
        q, k, v = jnp.split(qkv, 3, axis=-1)

        def to_heads(t):
            return t.reshape(b, n, heads, head_size).transpose(0, 2, 1, 3)
        q, k, v = (to_heads(q), to_heads(k), to_heads(v))
        q = jax.nn.softmax(q, axis=-1) * scale
        k = jax.nn.softmax(k, axis=-2)
        context = jnp.einsum('bhnd,bhne->bhde', k, v)
        out = jnp.einsum('bhde,bhnd->bhne', context, q)
        out = out.transpose(0, 2, 1, 3).reshape(b, n, heads * head_size)
        out = jnp.einsum('bnh,dh->bnd', out, w_out)
        out = gamma_layer_norm(out, gamma)
        return out

    def _L0_ffn_ref(x, w_gating, w1, w2):
        import jax, jax.numpy as jnp
        import numpy as np
        MIN_EXPERT_CAPACITY = 4
        EPS = 1e-09
        CAPACITY_FACTOR = 2.0

        def cumsum_exclusive(t, axis):
            return jnp.cumsum(t, axis=axis) - t

        def safe_one_hot(idx, depth):
            return jax.nn.one_hot(idx, depth + 1)[..., :depth]

        def top2_gating(x, w_gating):
            b, n, d = x.shape
            e = w_gating.shape[-1]
            raw_gates = jax.nn.softmax(jnp.einsum('bnd,de->bne', x, w_gating), axis=-1)
            gate_1 = jnp.max(raw_gates, axis=-1)
            index_1 = jnp.argmax(raw_gates, axis=-1)
            mask_1 = jax.nn.one_hot(index_1, e, dtype=raw_gates.dtype)
            gates_without_top1 = raw_gates * (1.0 - mask_1)
            gate_2 = jnp.max(gates_without_top1, axis=-1)
            index_2 = jnp.argmax(gates_without_top1, axis=-1)
            mask_2 = jax.nn.one_hot(index_2, e, dtype=raw_gates.dtype)
            denom = gate_1 + gate_2 + EPS
            gate_1 = gate_1 / denom
            gate_2 = gate_2 / denom
            density_1 = jnp.mean(mask_1, axis=-2)
            density_1_proxy = jnp.mean(raw_gates, axis=-2)
            loss = jnp.mean(density_1_proxy * density_1) * float(e * e)
            capacity = max(min(n, int(n * 2 * CAPACITY_FACTOR / e)), MIN_EXPERT_CAPACITY)
            cap_f = float(capacity)
            pos1 = cumsum_exclusive(mask_1, axis=-2) * mask_1
            mask_1 = mask_1 * (pos1 < cap_f).astype(mask_1.dtype)
            mask_1_count = jnp.sum(mask_1, axis=-2, keepdims=True)
            mask_1_flat = jnp.sum(mask_1, axis=-1)
            pos1 = jnp.sum(pos1, axis=-1)
            gate_1 = gate_1 * mask_1_flat
            pos2 = (cumsum_exclusive(mask_2, axis=-2) + mask_1_count) * mask_2
            mask_2 = mask_2 * (pos2 < cap_f).astype(mask_2.dtype)
            mask_2_flat = jnp.sum(mask_2, axis=-1)
            pos2 = jnp.sum(pos2, axis=-1)
            gate_2 = gate_2 * mask_2_flat
            combine = gate_1[..., None, None] * mask_1_flat[..., None, None] * jax.nn.one_hot(index_1, e, dtype=x.dtype)[..., None] * safe_one_hot(pos1.astype(jnp.int32), capacity)[..., None, :] + gate_2[..., None, None] * mask_2_flat[..., None, None] * jax.nn.one_hot(index_2, e, dtype=x.dtype)[..., None] * safe_one_hot(pos2.astype(jnp.int32), capacity)[..., None, :]
            dispatch = (combine > 0).astype(combine.dtype)
            return (dispatch, combine, loss)
        dispatch, combine, loss = top2_gating(x, w_gating)
        expert_inputs = jnp.einsum('bnd,bnec->ebcd', x, dispatch)
        hidden = jax.nn.relu(jnp.einsum('ebcd,edh->ebch', expert_inputs, w1))
        expert_outputs = jnp.einsum('ebch,ehd->ebcd', hidden, w2)
        output = jnp.einsum('ebcd,bnec->bnd', expert_outputs, combine)
        return output

    def _L1_gnn_ref(x, edge_index, W1, a_src1, a_dst1, b1, g1, beta1, W2, a_src2, a_dst2, b2, g2, beta2):
        import jax, jax.numpy as jnp
        import numpy as np
        N = 625
        E = 10000
        LN_EPS = 1e-05
        NEG_SLOPE = 0.2

        def _segment_softmax(logits, seg, num_segments):
            m = jax.ops.segment_max(logits, seg, num_segments=num_segments)
            e = jnp.exp(logits - m[seg])
            s = jax.ops.segment_sum(e, seg, num_segments=num_segments)
            return e / s[seg]

        def _gat_conv(x, src, dst, W, a_s, a_d, b, concat):
            H, C = a_s.shape
            n = x.shape[0]
            h = (x @ W).reshape(n, H, C)
            alpha_s = jnp.einsum('nhc,hc->nh', h, a_s)
            alpha_d = jnp.einsum('nhc,hc->nh', h, a_d)
            logits = jax.nn.leaky_relu(alpha_s[src] + alpha_d[dst], NEG_SLOPE)
            alpha = _segment_softmax(logits, dst, n)
            msg = h[src] * alpha[:, :, None]
            out = jax.ops.segment_sum(msg, dst, num_segments=n)
            out = out.reshape(n, H * C) if concat else out.mean(axis=1)
            return out + b

        def _layer_norm(x, g, beta):
            mu = jnp.mean(x, axis=-1, keepdims=True)
            var = jnp.var(x, axis=-1, keepdims=True)
            return (x - mu) * jax.lax.rsqrt(var + LN_EPS) * g + beta

        def _forward(x, edge_index, W1, a_src1, a_dst1, b1, g1, beta1, W2, a_src2, a_dst2, b2, g2, beta2):
            n = x.shape[0]
            loops = jnp.arange(n, dtype=edge_index.dtype)
            src = jnp.concatenate([edge_index[0], loops])
            dst = jnp.concatenate([edge_index[1], loops])
            x_new = _gat_conv(x, src, dst, W1, a_src1, a_dst1, b1, concat=True)
            x_new = jax.nn.elu(_layer_norm(x_new, g1, beta1))
            x = x + x_new
            x_new = _gat_conv(x, src, dst, W2, a_src2, a_dst2, b2, concat=False)
            x_new = jax.nn.elu(_layer_norm(x_new, g2, beta2))
            return x + x_new
        return _forward(x, edge_index, W1, a_src1, a_dst1, b1, g1, beta1, W2, a_src2, a_dst2, b2, g2, beta2)

    def _L1_mix_ref(x, W_qkv, W_out, b_out):
        import jax, jax.numpy as jnp
        import numpy as np
        DIM = 512
        HEADS = 8
        DIM_HEAD = 64
        INNER = HEADS * DIM_HEAD
        B, N = (4, 256)
        b, n, _ = x.shape
        qkv = x @ W_qkv
        q, k, v = jnp.split(qkv, 3, axis=-1)

        def heads(t):
            return t.reshape(b, n, HEADS, DIM_HEAD).transpose(0, 2, 1, 3)
        q, k, v = (heads(q), heads(k), heads(v))
        q = jax.nn.softmax(q, axis=-1)
        k = jax.nn.softmax(k, axis=2)
        context = jnp.einsum('bhnd,bhne->bhde', k, v)
        out = jnp.einsum('bhnd,bhde->bhne', q, context)
        out = out.transpose(0, 2, 1, 3).reshape(b, n, INNER)
        return out @ W_out + b_out

    def _L1_ffn_ref(x, Wr, br, W1, b1, W2, b2):
        import jax, jax.numpy as jnp
        import numpy as np
        import math
        E, K, CAPF = (8, 2, 1.25)
        D, DFF = (512, 64)

        def _moe(x, Wr, br, W1, b1, W2, b2):
            orig = x.shape
            d = orig[-1]
            xf = x.reshape(-1, d)
            N = xf.shape[0]
            logits = xf @ Wr + br
            probs = jax.nn.softmax(logits, axis=-1)
            topk_p, topk_i = jax.lax.top_k(probs, K)
            topk_w = topk_p / (jnp.sum(topk_p, axis=-1, keepdims=True) + 1e-09)
            cap = max(1, int(math.ceil(CAPF * float(N * K) / float(E))))
            flat_e = topk_i.reshape(-1)
            flat_w = topk_w.reshape(-1)
            tok = jnp.repeat(jnp.arange(N), K)
            one_hot = jax.nn.one_hot(flat_e, E, dtype=xf.dtype)
            pos = (jnp.cumsum(one_hot, axis=0) - one_hot)[jnp.arange(N * K), flat_e]
            pos = pos.astype(jnp.int32)
            keep = pos < cap
            w_k = jnp.where(keep, flat_w, 0.0)
            sum_w = jnp.zeros((N,), xf.dtype).at[tok].add(w_k)
            w_norm = w_k / (sum_w[tok] + 1e-09)
            slot = flat_e * cap + pos
            slot_safe = jnp.where(keep, slot, E * cap)
            expert_in = jnp.zeros((E * cap, d), xf.dtype).at[slot_safe].set(xf[tok], mode='drop').reshape(E, cap, d)
            h = jax.nn.gelu(jnp.einsum('ecd,edf->ecf', expert_in, W1) + b1[:, None, :], approximate=False)
            expert_out = (jnp.einsum('ecf,efd->ecd', h, W2) + b2[:, None, :]).reshape(E * cap, d)
            contrib = expert_out[jnp.where(keep, slot, 0)]
            y = jnp.zeros((N, d), xf.dtype).at[tok].add(contrib * w_norm[:, None])
            return y.reshape(orig)
        return _moe(x, Wr, br, W1, b1, W2, b2)
    edge_index = jnp.stack([src, dst])
    xn = _layernorm(x, axis=-1)
    x = x + _L0_gnn_ref(xn, edge_index, L0_gnn_W, L0_gnn_b, L0_gnn_diffusion_weights) + _L0_mix_ref(xn[None], L0_mix_w_qkv, L0_mix_w_out, L0_mix_gamma)[0]
    x = x + _L0_ffn_ref(_layernorm(x, axis=-1)[None], L0_ffn_w_gating, L0_ffn_w1, L0_ffn_w2)[0]
    xn = _layernorm(x, axis=-1)
    x = x + _L1_gnn_ref(xn, edge_index, L1_gnn_W1, L1_gnn_a_src1, L1_gnn_a_dst1, L1_gnn_b1, L1_gnn_g1, L1_gnn_beta1, L1_gnn_W2, L1_gnn_a_src2, L1_gnn_a_dst2, L1_gnn_b2, L1_gnn_g2, L1_gnn_beta2) + _L1_mix_ref(xn[None], L1_mix_W_qkv, L1_mix_W_out, L1_mix_b_out)[0]
    x = x + _L1_ffn_ref(_layernorm(x, axis=-1)[None], L1_ffn_Wr, L1_ffn_br, L1_ffn_W1, L1_ffn_b1, L1_ffn_W2, L1_ffn_b2)[0]
    return x

_drawn_inputs = setup_inputs


def setup_inputs(seed=0):
    import zlib

    import numpy as np

    out = dict(_drawn_inputs(seed))
    spreads = {'L0_gnn_b': (0.0, 0.1),
     'L0_gnn_diffusion_weights': (0.25, 0.6),
     'L1_gnn_b1': (0.0, 0.1),
     'L1_gnn_g1': (1.0, 0.2),
     'L1_gnn_beta1': (0.0, 0.1),
     'L1_gnn_b2': (0.0, 0.1),
     'L1_gnn_g2': (1.0, 0.2),
     'L1_gnn_beta2': (0.0, 0.1),
     'L1_ffn_br': (0.0, 0.1),
     'L1_ffn_b1': (0.0, 0.451),
     'L1_ffn_b2': (0.0, 0.289)}
    factors = {'L1_gnn_a_dst1': 3.442, 'L1_gnn_a_dst2': 6.494, 'L1_mix_b_out': 3.934}
    for name, (base, spread) in spreads.items():
        noise = np.random.default_rng([zlib.crc32(name.encode()), seed]).standard_normal(out[name].shape)
        drawn = base * np.exp(spread * noise) if base else spread * noise
        out[name] = jnp.asarray(drawn.astype(out[name].dtype))
    for name, factor in factors.items():
        out[name] = (out[name] * factor).astype(out[name].dtype)
    return out
```

```python
import concourse.bass as bass
from concourse import mybir
from contextlib import ExitStack



def gps_two_layers(nc, A, out):
    f32, bf16 = mybir.dt.float32, mybir.dt.bfloat16
    i32, u32 = mybir.dt.int32, mybir.dt.uint32
    ALU, ACT, AX = mybir.AluOpType, mybir.ActivationFunctionType, mybir.AxisListType

    P = 128
    N, D = A["x"].shape
    T = N // P
    C = D // P
    EDGES = A["src"].shape[0]
    ET = EDGES // P
    H, HD = 8, 64
    STEPS = A["diffusion"].shape[0] - 1
    EXPERTS = (16, 8)
    FF = 64
    CAP0 = max(min(N, int(N * 2 * 2.0 / EXPERTS[0])), 4)
    CAP1 = max(1, -int(-1.25 * N * 2 // EXPERTS[1]))
    EPS, GATE_EPS = 1e-5, 1e-9
    SLOPE = 0.2
    BIG = 3.0e38
    FAR = 1.0e30

    ctx = ExitStack()
    with ctx:
        def sb(name, shape, dt=f32):
            return ctx.enter_context(nc.sbuf_tensor(name, shape, dt))

        def sem(name):
            return ctx.enter_context(nc.semaphore(name))

        region_a = sb("region_a", [P, 10 * 1024])
        region_b = sb("region_b", [P, 16 * 1024])

        def part(region, kib, rows, cols):
            return region[:, kib * 256:kib * 256 + rows * cols].rearrange("p (c n) -> p c n", c=rows)

        w_k0, w_q0, w_v0 = (part(region_a, 8 * i, C, D) for i in range(3))
        w_gnn0 = part(region_a, 24, C, D)
        w_out0 = part(region_a, 32, C, D)
        w1t = part(region_a, 0, C, D)
        w2t = part(region_a, 8, C, D)
        hid = part(region_a, 16, 8, N)
        w_out1 = part(region_a, 24, C, D)
        w_gat2 = part(region_a, 32, C, D)
        w_gat1 = part(region_b, 0, C, D)
        w_k1, w_q1, w_v1 = (part(region_b, 8 + 8 * i, C, D) for i in range(3))
        w_up0 = part(region_b, 32, C, 2 * D)
        w_down0 = part(region_b, 48, 2 * C, D)
        onehot = region_b[:, :].bitcast(bf16).rearrange("p (j a n) -> p j a n", j=ET, a=2)
        logit = region_b[:, 8192:12288].rearrange("p (s h n) -> p s h n", s=T, h=H)
        w_up1 = part(region_b, 48, C, D)
        w_down1 = part(region_b, 56, C, D)
        w_gate = sb("w_gate", [P, C, EXPERTS[0]])
        w_router = sb("w_router", [P, C, EXPERTS[1]])

        row_names = ["b_gnn0", "gamma0", "b1", "g1", "beta1", "b2", "g2", "beta2", "b_out1"]
        rows = sb("rows", [P, len(row_names), D])
        row = {n: rows[:, i, :] for i, n in enumerate(row_names)}
        diffusion = sb("diffusion", [P, STEPS + 1])
        b_router = sb("b_router", [P, EXPERTS[1]])
        b_up1 = sb("b_up1", [P, C])
        b_down1 = sb("b_down1", [EXPERTS[1], D])
        att1 = sb("att1", [P, 2, C])
        att2 = sb("att2", [P, 2, C])

        ident = sb("ident", [P, P])
        ones = sb("ones", [P, P])
        before = sb("before", [P, P])
        pick = sb("pick", [EXPERTS[0], H, P])
        spread = sb("spread", [EXPERTS[0], 8, 2, FF])
        headmask = sb("headmask", [P, C, H])
        iota_i = sb("iota_i", [P, N], i32)
        iota_bf = sb("iota_bf", [P, N], bf16)
        iota_f = sb("iota_f", [P, EXPERTS[0]])
        minus_half = sb("minus_half", [P, T])
        edges_i = sb("edges_i", [P, 2, ET], i32)
        edges = sb("edges", [P, 2, ET])

        xa = sb("xa", [P, T, D])
        xb = sb("xb", [P, T, D])
        xn = sb("xn", [P, T, D])
        xT = sb("xT", [P, C, N])
        q = sb("q", [P, T, D])
        v = sb("v", [P, T, D])
        ek = sb("ek", [P, T, D])
        ekT = sb("ekT", [P, C, N])
        qT = sb("qT", [P, C, N])
        yT = ekT
        ctxbd = sb("ctxbd", [P, C, P])
        cur = sb("cur", [P, 2, T, D])
        diffused = sb("diffused", [P, T, D])
        mixed = v
        count = sb("count", [P, T, N])
        countT = sb("countT", [P, T, N])
        linked = sb("linked", [P, T, N])
        far = sb("far", [P, T, N])
        hx = sb("hx", [P, T, H, HD + 1])
        h2 = cur[:, 0, :, :]
        g_a = cur[:, 1, :, :]
        g_b = diffused
        x1g = q
        wa = sb("wa", [P, C, 2 * H + 2])
        al = sb("al", [P, T, 2 * H])
        alT = sb("alT", [H, 2, N])
        mx = sb("mx", [P, T, H])
        mz = sb("mz", [P, T, H])
        mT = sb("mT", [H, N])
        junk = cur[:, 1, :, :].rearrange("p t (a n) -> p (t a) n", a=2)
        attblk = sb("attblk", [P, C, 2 * H])
        stats = sb("stats", [P, T, 6])
        mv = sb("mv", [P, T, 2])
        veps = sb("veps", [P, T])
        rstd = sb("rstd", [P, T])
        kmax = sb("kmax", [P, C])
        ksum = sb("ksum", [P, C])
        kinv = sb("kinv", [P, C])
        qmax = sb("qmax", [P, T, H])
        qsum = sb("qsum", [P, T, H])
        degree = sb("degree", [P, T])
        E0 = EXPERTS[0]
        lg = sb("lg", [P, T, E0])
        prob = sb("prob", [P, T, E0])
        prob2 = sb("prob2", [P, T, E0])
        gsm = sb("gsm", [P, 8, T])
        top = sb("top", [P, 2, T, 8])
        top_i = sb("top_i", [P, 2, T, 8], u32)
        top_f = sb("top_f", [P, 2, T])
        mask = sb("mask", [P, T, 2 * E0])
        kept = sb("kept", [P, T, 2 * E0])
        poss = sb("poss", [P, T, 2 * E0])
        gate = sb("gate", [P, T, E0])
        gateT = sb("gateT", [E0, N])

        bank = [ctx.enter_context(nc.psum_tensor(f"bank{i}", [P, 512], f32)) for i in range(8)]

        x_in, edges_in, small_in = sem("x_in"), sem("edges_in"), sem("small_in")
        win = {n: sem("in_" + n) for n in
               ["k0", "q0", "v0", "gnn0", "out0", "gate", "up0", "down0", "w1t", "w2t", "gat1",
                "k1", "q1", "v1", "out1", "gat2", "up1", "down1"]}
        consts, iota_ready = sem("consts"), sem("iota_ready")
        var_ready, rstd_ready, xn_ready = sem("var_ready"), sem("rstd_ready"), sem("xn_ready")
        xT_full, xT_ready = sem("xT_full"), sem("xT_ready")
        k_full, kmax_ready, ekT_ready, ek_full, ek_ready = (sem(n) for n in
            ["k_full", "kmax_ready", "ekT_ready", "ek_full", "ek_ready"])
        q_full, q_shifted, q_exp, q_ready, qT_full, qT_ready = (sem(n) for n in
            ["q_full", "q_shifted", "q_exp", "q_ready", "qT_full", "qT_ready"])
        v_full, v_ready, ctx_full, ctx_ready = (sem(n) for n in
            ["v_full", "v_ready", "ctx_full", "ctx_ready"])
        yT_full, yT_ready, o_full, mix_ready = (sem(n) for n in
            ["yT_full", "yT_ready", "o_full", "mix_ready"])
        onehot_ready, count_full, count_ready, countT_full, linked_ready, countT_ready = (sem(n) for n in
            ["onehot_ready", "count_full", "count_ready", "countT_full", "linked_ready", "countT_ready"])
        h_full, cur_ready, step_full = sem("h_full"), sem("cur_ready"), sem("step_full")
        logits_full, shift_ready, gexp_ready, masks_ready, pos_full = (sem(n) for n in
            ["logits_full", "shift_ready", "gexp_ready", "masks_ready", "pos_full"])
        gate_ready, gateT_full, gateT_ready, spread_full = (sem(n) for n in
            ["gate_ready", "gateT_full", "gateT_ready", "spread_full"])
        up_full, up_ready, hid_ready, down_full, x_ready = (sem(n) for n in
            ["up_full", "up_ready", "hid_ready", "down_full", "x_ready"])
        wa_full, wa_ready, al_full, al_ready, alT_full, alT_ready = (sem(n) for n in
            ["wa_full", "wa_ready", "al_full", "al_ready", "alT_full", "alT_ready"])
        src_full, max_ready, mT_full, mT_ready, hx_full, hx_ready = (sem(n) for n in
            ["src_full", "max_ready", "mT_full", "mT_ready", "hx_full", "hx_ready"])
        dst_full, z_ready, max_full, shifted, exp_ready, weight_ready = (sem(n) for n in
            ["dst_full", "z_ready", "max_full", "shifted", "exp_ready", "weight_ready"])
        agg_full, elu_min, elu_exp, out_ready, stored = (sem(n) for n in
            ["agg_full", "elu_min", "elu_exp", "out_ready", "stored"])
        attblk_ready, agg_ready = sem("attblk_ready"), sem("agg_ready")
        dve_step, pool_step = sem("dve_step"), sem("pool_step")

        xT_read = {1: (h_full, 2), 2: (up_full, 4), 3: (v_full, 4), 4: (hx_full, 4)}

        block = ctx.enter_context(nc.Block())

        def half(b, i, n=N):
            return bank[b][:, i * n:(i + 1) * n]

        @block.sync
        def _(sp):
            for t in range(T):
                sp.dma_start(xa[:, t, :], A["x"][t * P:(t + 1) * P, :]).then_inc(x_in, 16)
            for a, n in enumerate(("src", "dst")):
                sp.dma_start(edges_i[:, a, :], A[n].rearrange("(p j) -> p j", p=P)).then_inc(edges_in, 16)

            def load(dst, name):
                sp.dma_start(dst, A[name]).then_inc(win[name], 16)

            load(w_k0, "k0")
            load(w_q0, "q0")
            load(w_v0, "v0")
            load(w_gnn0, "gnn0")
            sp.dma_start(diffusion[:, :], A["diffusion"].partition_broadcast(P)).then_inc(small_in, 16)
            for n in row_names:
                sp.dma_start(row[n], A[n].partition_broadcast(P)).then_inc(small_in, 16)
            sp.dma_start(b_router[:, :], A["b_router"].partition_broadcast(P)).then_inc(small_in, 16)
            sp.dma_start(b_up1[:, :], A["b_up1"]).then_inc(small_in, 16)
            sp.dma_start(b_down1[:, :], A["b_down1"]).then_inc(small_in, 16)
            sp.dma_start(w_router[:, :, :], A["router"]).then_inc(small_in, 16)
            for a, n in enumerate(("a_src1", "a_dst1")):
                sp.dma_start(att1[:, a, :], A[n]).then_inc(small_in, 16)
            for a, n in enumerate(("a_src2", "a_dst2")):
                sp.dma_start(att2[:, a, :], A[n]).then_inc(small_in, 16)
            load(w_out0, "out0")
            load(w_gate[:, :, :], "gate")
            sp.wait_ge(count_full, 1)
            load(w_up0, "up0")
            load(w_down0, "down0")
            sp.wait_ge(k_full, 2)
            load(w1t, "w1t")
            sp.wait_ge(q_full, 2)
            load(w2t, "w2t")
            load(w_gat1, "gat1")
            load(w_k1, "k1")
            load(w_q1, "q1")
            load(w_v1, "v1")
            sp.wait_ge(h_full, 2)
            load(w_out1, "out1")
            sp.wait_ge(o_full, 2)
            load(w_gat2, "gat2")
            sp.wait_ge(down_full, 2)
            load(w_up1, "up1")
            load(w_down1, "down1")
            for t in range(T):
                sp.wait_ge(out_ready, t + 1)
                sp.dma_start(out[t * P:(t + 1) * P, :], xa[:, t, :]).then_inc(stored, 16)
            sp.wait_ge(stored, 16 * T)

        SMALLS = 16 * (1 + len(row_names) + 8)

        @block.gpsimd
        def _(pool):
            n = [0]

            def then(ins):
                n[0] += 1
                ins.then_inc(pool_step, 1)
                pool.wait_ge(pool_step, n[0])

            def fill(dst, base, pattern, cm):
                then(nc.gpsimd.affine_select(out=dst, in_=dst, compare_op=ALU.not_equal, fill=1.0,
                                             base=base, pattern=pattern, channel_multiplier=cm))

            nc.gpsimd.iota(iota_i[:, :], pattern=[[1, N]], base=0, channel_multiplier=0).then_inc(iota_ready, 1)
            then(nc.gpsimd.memset(minus_half[:, :], -0.5))
            then(nc.gpsimd.memset(ident[:, :], 0.0))
            fill(ident[:, :], 0, [[-1, P]], 1)
            nc.gpsimd.memset(ctxbd[:, :, :], 0.0).then_inc(consts, 1)

            def root(i):
                pool.wait_ge(var_ready, i + 1)
                nc.gpsimd.tensor_tensor(rstd[:, :], veps[:, :], minus_half[:, :], ALU.pow)\
                    .then_inc(rstd_ready, 1)

            root(0)
            then(nc.gpsimd.memset(ones[:, :], 1.0))
            then(nc.gpsimd.affine_select(out=before[:, :], in_=ones[:, :], compare_op=ALU.is_gt, fill=0.0,
                                         base=0, pattern=[[1, P]], channel_multiplier=-1))
            then(nc.gpsimd.memset(pick[:, :, :], 0.0))
            fill(pick[:, :, :], 0, [[-1, H], [0, P]], 1)
            then(nc.gpsimd.memset(spread[:, :, :, :], 0.0))
            fill(spread[:, :, :, :], 0, [[-2, 8], [-1, 2], [0, FF]], 1)
            then(nc.gpsimd.memset(headmask[:, :, :], 0.0))
            fill(headmask[0:64, :, :], 0, [[2, C], [-1, H]], 0)
            fill(headmask[64:128, :, :], 1, [[2, C], [-1, H]], 0)
            pool.wait_ge(small_in, SMALLS)
            for a in range(2):
                then(nc.gpsimd.tensor_tensor(attblk[:, :, a * H:(a + 1) * H], headmask[:, :, :],
                                             att1[:, a, :].unsqueeze(2).broadcast_to([P, C, H]), ALU.mult))
            nc.gpsimd.memset(hx[:, :, :, HD:HD + 1], 1.0).then_inc(consts, 1)
            for i in range(1, 7):
                root(i)

        @block.scalar
        def _(act):
            def copy(dst, src):
                return nc.scalar.activation(dst, src, ACT.Copy)

            def xT_part(i, b):
                act.wait_ge(xT_full, 2 * i + 1)
                if i:
                    act.wait_ge(*xT_read[i])
                copy(xT[:, 0:2, :], bank[b][:, :].rearrange("p (c n) -> p c n", c=2)).then_inc(xT_ready, 1)

            def mix_exps(L):
                for m in range(C):
                    act.wait_ge(kmax_ready, 2 * L + m // 2 + 1)
                    if L:
                        act.wait_ge(yT_full, 2)
                        act.wait_ge(o_full, 2)
                    nc.scalar.activation(ekT[:, m, :], half(4 + m // 2, m % 2), ACT.Exp,
                                         bias=kmax[:, m:m + 1], accum_out=ksum[:, m:m + 1]).then_inc(ekT_ready, 1)

            def mix_q(L):
                for t in range(T):
                    act.wait_ge(q_shifted, 2 * L + t + 1)
                    nc.scalar.activation(q[:, t, :], q[:, t, :], ACT.Exp).then_inc(q_exp, 1)

            def mix_v(L, banks):
                for t in range(T):
                    act.wait_ge(v_full, 2 * L + t + 1)
                    if L:
                        act.wait_ge(ctx_full, 1)
                    copy(v[:, t, :], bank[banks[t]][:, :]).then_inc(v_ready, 1)

            def mix_rest(L, ekb, qTb, yTb):
                for t in range(T):
                    act.wait_ge(ek_full, 2 * L + t + 1)
                    if L:
                        act.wait_ge(ctx_full, 1)
                    copy(ek[:, t, :], bank[ekb[t]][:, :]).then_inc(ek_ready, 1)
                for j in range(2):
                    act.wait_ge(qT_full, 2 * L + j + 1)
                    if L:
                        act.wait_ge(yT_full, 2)
                    copy(qT[:, 2 * j:2 * j + 2, :], bank[qTb[j]][:, :].rearrange("p (c n) -> p c n", c=2))\
                        .then_inc(qT_ready, 1)
                for j in range(2):
                    act.wait_ge(yT_full, 2 * L + j + 1)
                    act.wait_ge(ek_full, 2 * L + 2)
                    copy(yT[:, 2 * j:2 * j + 2, :], bank[yTb[j]][:, :].rearrange("p (c n) -> p c n", c=2))\
                        .then_inc(yT_ready, 1)

            def gate_exp(L):
                act.wait_ge(shift_ready, L + 1)
                nc.scalar.activation(prob[:, :, 0:EXPERTS[L]], lg[:, :, 0:EXPERTS[L]], ACT.Exp)\
                    .then_inc(gexp_ready, 1)

            def elu(g):
                act.wait_ge(elu_min, g + 1)
                nc.scalar.activation(g_b[:, :, :], g_b[:, :, :], ACT.Exp).then_inc(elu_exp, 1)

            xT_part(0, 0)
            mix_exps(0)
            mix_v(0, (6, 7))
            mix_q(0)
            act.wait_ge(ek_full, 1)
            copy(ek[:, 0, :], bank[4][:, :]).then_inc(ek_ready, 1)
            act.wait_ge(ek_full, 2)
            copy(ek[:, 1, :], bank[5][:, :]).then_inc(ek_ready, 1)
            for j in range(2):
                act.wait_ge(qT_full, j + 1)
                copy(qT[:, 2 * j:2 * j + 2, :], bank[j][:, :].rearrange("p (c n) -> p c n", c=2)).then_inc(qT_ready, 1)
            for t in range(T):
                act.wait_ge(count_full, 1)
                copy(count[:, t, :], half(2 + t, 0)).then_inc(count_ready, 1)
            act.wait_ge(countT_full, 1)
            copy(countT[:, :, :], bank[7][:, :].rearrange("p (c n) -> p c n", c=T)).then_inc(countT_ready, 1)
            for j in range(2):
                act.wait_ge(yT_full, j + 1)
                copy(yT[:, 2 * j:2 * j + 2, :], bank[4 + j][:, :].rearrange("p (c n) -> p c n", c=2)).then_inc(yT_ready, 1)
            xT_part(1, 4)
            gate_exp(0)
            act.wait_ge(v_full, 2)
            for m in range(8):
                act.wait_ge(up_full, m // 2 + 1)
                nc.scalar.activation(hid[:, m, :], half(m // 2, m % 2), ACT.Relu).then_inc(up_ready, 1)
            act.wait_ge(gateT_full, 1)
            copy(gateT[0:E0, :], bank[6][0:E0, 0:N]).then_inc(gateT_ready, 1)

            act.wait_ge(wa_full, 1)
            copy(wa[:, :, :], bank[5][:, 0:C * (2 * H + 2)].rearrange("p (c n) -> p c n", c=C)).then_inc(wa_ready, 1)
            xT_part(2, 2)
            act.wait_ge(al_full, 1)
            copy(al[:, :, :], bank[4][:, 0:T * 2 * H].rearrange("p (t n) -> p t n", t=T)).then_inc(al_ready, 1)
            act.wait_ge(alT_full, 1)
            copy(alT[:, :, :], bank[5][0:H, :].rearrange("p (a n) -> p a n", a=2)).then_inc(alT_ready, 1)
            for t in range(T):
                act.wait_ge(hx_full, t + 1)
                copy(hx[:, t, :, 0:HD], bank[2 + t][:, :].rearrange("p (h n) -> p h n", h=H)).then_inc(hx_ready, 1)
            mix_exps(1)
            PAIR = (0, 1, 6, 7)
            act.wait_ge(al_ready, 1)
            act.wait_ge(down_full, 2)
            for j in range(4):
                act.wait_ge(dst_full, j + 1)
                for s in range(T):
                    for h in range(2):
                        hh = 2 * j + h
                        nc.scalar.activation(logit[:, s, hh, :], half(PAIR[j], h), ACT.Identity,
                                             bias=al[:, s, hh:hh + 1]).then_inc(z_ready, 1)
            act.wait_ge(mT_full, 1)
            copy(mT[:, :], bank[4][0:H, 0:N]).then_inc(mT_ready, 1)
            mix_q(1)
            mix_v(1, (2, 3))
            for t in range(T):
                act.wait_ge(ek_full, 2 + t + 1)
                copy(ek[:, t, :], bank[4 + t][:, :]).then_inc(ek_ready, 1)
            for j in range(4):
                for s in range(T):
                    act.wait_ge(shifted, 2 * j + s + 1)
                    nc.scalar.activation(logit[:, s, 2 * j:2 * j + 2, :], logit[:, s, 2 * j:2 * j + 2, :],
                                         ACT.Exp).then_inc(exp_ready, 1)
            for j in range(2):
                act.wait_ge(qT_full, 2 + j + 1)
                copy(qT[:, 2 * j:2 * j + 2, :], bank[2 + j][:, :].rearrange("p (c n) -> p c n", c=2)).then_inc(qT_ready, 1)
            for j, b in enumerate((5, 2)):
                act.wait_ge(yT_full, 2 + j + 1)
                copy(yT[:, 2 * j:2 * j + 2, :], bank[b][:, :].rearrange("p (c n) -> p c n", c=2)).then_inc(yT_ready, 1)
            elu(0)
            xT_part(3, 0)
            act.wait_ge(al_full, 2)
            copy(al[:, :, 0:2], bank[6][:, 0:2 * T].rearrange("p (t n) -> p t n", t=T)).then_inc(al_ready, 1)
            act.wait_ge(alT_full, 2)
            copy(alT[0:1, :, :], bank[7][0:1, :].rearrange("p (a n) -> p a n", a=2)).then_inc(alT_ready, 1)
            act.wait_ge(al_ready, 2)
            act.wait_ge(src_full, 5)
            for s in range(T):
                nc.scalar.activation(logit[:, s, 0, :], half(6, 0), ACT.Identity,
                                     bias=al[:, s, 0:1]).then_inc(z_ready, 1)
            act.wait_ge(mT_full, 2)
            copy(mT[0:1, :], bank[5][0:1, 0:N]).then_inc(mT_ready, 1)
            for s in range(T):
                act.wait_ge(shifted, 8 + s + 1)
                nc.scalar.activation(logit[:, s, 0, :], logit[:, s, 0, :], ACT.Exp).then_inc(exp_ready, 1)
            for t in range(T):
                act.wait_ge(hx_full, 2 + t + 1)
                copy(h2[:, t, :], bank[3 + t][:, :]).then_inc(hx_ready, 1)
            elu(1)
            xT_part(4, 3)
            gate_exp(1)
            act.wait_ge(gexp_ready, 2)
            for m in range(C):
                act.wait_ge(up_full, 4 + m // 2 + 1)
                nc.scalar.activation(hid[:, m, :], half(m // 2, m % 2), ACT.Gelu, bias=b_up1[:, m:m + 1])\
                    .then_inc(up_ready, 1)
            act.wait_ge(gateT_full, 2)
            copy(gateT[0:EXPERTS[1], :], bank[7][0:EXPERTS[1], 0:N]).then_inc(gateT_ready, 1)

        @block.vector
        def _(dve):
            n = [0]
            V = nc.vector

            def go(ins):
                n[0] += 1
                ins.then_inc(dve_step, 1)
                return ins

            def settle():
                dve.wait_ge(dve_step, n[0])

            def norm(i, srcs, dst=None, first=None):
                for t in range(T):
                    go(V.bn_stats(stats[:, t, :], srcs[t]))
                settle()
                for t in range(T):
                    go(V.bn_aggr(mv[:, t, :], stats[:, t, :]))
                settle()
                V.tensor_scalar(veps[:, :], mv[:, :, 1], EPS, None, ALU.add).then_inc(var_ready, 1)
                dve.wait_ge(rstd_ready, i + 1)

            def norm_rows(dst, src, t, s=None):
                ins = V.tensor_scalar(dst, src, mv[:, t, 0:1], rstd[:, t:t + 1], ALU.subtract, ALU.mult)
                return ins.then_inc(s, 1) if s else go(ins)

            def xT_part(i, b):
                dve.wait_ge(xT_full, 2 * i + 2)
                if i:
                    dve.wait_ge(*xT_read[i])
                V.tensor_copy(xT[:, 2:4, :], bank[b][:, :].rearrange("p (c n) -> p c n", c=2)).then_inc(xT_ready, 1)

            def k_max(L):
                for j in range(2):
                    dve.wait_ge(k_full, 2 * L + j + 1)
                    V.tensor_reduce(kmax[:, 2 * j:2 * j + 2], bank[4 + j][:, :].rearrange("p (c n) -> p c n", c=2),
                                    AX.X, ALU.max, negate=True).then_inc(kmax_ready, 1)

            def bc(a, shape):
                return a.unsqueeze(len(a.shape)).broadcast_to(shape)

            def q_shift(L, banks):
                for t in range(T):
                    dve.wait_ge(q_full, 2 * L + t + 1)
                    src = bank[banks[t]][:, :].rearrange("p (h n) -> p h n", h=H)
                    go(V.tensor_reduce(qmax[:, t, :], src, AX.X, ALU.max))
                    settle()
                    V.tensor_tensor(q[:, t, :].rearrange("p (h n) -> p h n", h=H), src,
                                    bc(qmax[:, t, :], [P, H, HD]), ALU.subtract).then_inc(q_shifted, 1)

            def q_norm(L):
                for t in range(T):
                    dve.wait_ge(q_exp, 2 * L + t + 1)
                    qh = q[:, t, :].rearrange("p (h n) -> p h n", h=H)
                    go(V.tensor_reduce(qsum[:, t, :], qh, AX.X, ALU.add))
                    settle()
                    go(V.reciprocal(qsum[:, t, :], qsum[:, t, :]))
                    settle()
                    if L == 0:
                        go(V.tensor_scalar(qsum[:, t, :], qsum[:, t, :], float(HD) ** -0.5, None, ALU.mult))
                        settle()
                    V.tensor_tensor(qh, qh, bc(qsum[:, t, :], [P, H, HD]), ALU.mult).then_inc(q_ready, 1)

            def context(L, b):
                dve.wait_ge(ekT_ready, 4 * L + 4)
                go(V.reciprocal(kinv[:, :], ksum[:, :]))
                settle()
                dve.wait_ge(ctx_full, L + 1)
                if L == 0:
                    dve.wait_ge(consts, 1)
                for r in range(2):
                    p0, p1 = r * HD, (r + 1) * HD
                    src = bank[b][p0:p1, :].rearrange("p (m n) -> p m n", m=C)[:, :, p0:p1]
                    V.tensor_tensor(ctxbd[p0:p1, :, p0:p1], src, bc(kinv[p0:p1, :], [HD, C, HD]), ALU.mult)\
                        .then_inc(ctx_ready, 1)

            def gates(L, b, pb):
                E = EXPERTS[L]
                dve.wait_ge(logits_full, L + 1)
                src = bank[b][:, 0:T * E].rearrange("p (t e) -> p t e", t=T)
                lgE, pE = lg[:, :, 0:E], prob[:, :, 0:E]
                if L:
                    go(V.tensor_tensor(lgE, src, b_router[:, :].unsqueeze(1).broadcast_to([P, T, E]), ALU.add))
                else:
                    go(V.tensor_copy(lgE, src))
                settle()
                go(V.tensor_reduce(gsm[:, 0, :], lgE, AX.X, ALU.max))
                settle()
                V.tensor_tensor(lgE, lgE, bc(gsm[:, 0, :], [P, T, E]), ALU.subtract).then_inc(shift_ready, 1)
                dve.wait_ge(gexp_ready, L + 1)
                go(V.tensor_reduce(gsm[:, 1, :], pE, AX.X, ALU.add))
                settle()
                go(V.reciprocal(gsm[:, 1, :], gsm[:, 1, :]))
                settle()
                go(V.tensor_tensor(pE, pE, bc(gsm[:, 1, :], [P, T, E]), ALU.mult))
                settle()
                for t in range(T):
                    go(V.max(top[:, 0, t, :], prob[:, t, 0:E]))
                settle()
                for t in range(T):
                    go(V.max_index(top_i[:, 0, t, :], top[:, 0, t, :], prob[:, t, 0:E]))
                settle()
                go(V.tensor_copy(top_f[:, 0, :], top_i[:, 0, :, 0]))
                if L:
                    go(V.tensor_copy(top_f[:, 1, :], top_i[:, 0, :, 1]))
                settle()
                io = iota_f[:, 0:E].unsqueeze(1).broadcast_to([P, T, E])
                m1, m2 = mask[:, :, 0:E], mask[:, :, E:2 * E]
                go(V.tensor_tensor(m1, io, bc(top_f[:, 0, :], [P, T, E]), ALU.is_equal))
                if L == 0:
                    settle()
                    go(V.tensor_scalar(prob2[:, :, :], m1, -1.0, 1.0, ALU.mult, ALU.add))
                    settle()
                    go(V.tensor_tensor(prob2[:, :, :], prob2[:, :, :], pE, ALU.mult))
                    settle()
                    for t in range(T):
                        go(V.max(top[:, 1, t, :], prob2[:, t, :]))
                    settle()
                    for t in range(T):
                        go(V.max_index(top_i[:, 1, t, :], top[:, 1, t, :], prob2[:, t, :]))
                    settle()
                    go(V.tensor_copy(top_f[:, 1, :], top_i[:, 1, :, 0]))
                    settle()
                    v2 = top[:, 1, :, 0]
                else:
                    v2 = top[:, 0, :, 1]
                v1 = top[:, 0, :, 0]
                V.tensor_tensor(m2, io, bc(top_f[:, 1, :], [P, T, E]), ALU.is_equal).then_inc(masks_ready, 1)
                go(V.tensor_tensor(gsm[:, 2, :], v1, v2, ALU.add))
                settle()
                go(V.tensor_scalar(gsm[:, 2, :], gsm[:, 2, :], GATE_EPS, None, ALU.add))
                settle()
                go(V.reciprocal(gsm[:, 2, :], gsm[:, 2, :]))
                settle()
                go(V.tensor_tensor(gsm[:, 3, :], v1, gsm[:, 2, :], ALU.mult))
                go(V.tensor_tensor(gsm[:, 4, :], v2, gsm[:, 2, :], ALU.mult))
                dve.wait_ge(masks_ready, L + 1)
                dve.wait_ge(pos_full, L + 1)
                pos = bank[pb][:, 0:T * 2 * E].rearrange("p (t e) -> p t e", t=T)
                total = bank[pb][:, T * 2 * E:T * 2 * E + E]
                k1, k2 = kept[:, :, 0:E], kept[:, :, E:2 * E]
                if L == 0:
                    go(V.tensor_scalar(poss[:, 0, 0:E], total, float(CAP0), None, ALU.min))
                    go(V.scalar_tensor_tensor(k1, pos[:, :, 0:E], float(CAP0), m1, ALU.is_lt, ALU.mult))
                    settle()
                    go(V.tensor_tensor(poss[:, :, E:2 * E], pos[:, :, E:2 * E],
                                       poss[:, 0:1, 0:E].broadcast_to([P, T, E]), ALU.add))
                    settle()
                    go(V.scalar_tensor_tensor(k2, poss[:, :, E:2 * E], float(CAP0), m2, ALU.is_lt, ALU.mult))
                    settle()
                else:
                    go(V.tensor_copy(poss[:, :, E:2 * E], pos[:, :, E:2 * E]))
                    settle()
                    go(V.tensor_tensor(poss[:, :, 0:E], pos[:, :, 0:E], poss[:, :, E:2 * E], ALU.add))
                    settle()
                    go(V.scalar_tensor_tensor(k1, poss[:, :, 0:E], float(CAP1), m1, ALU.is_lt, ALU.mult))
                    go(V.scalar_tensor_tensor(k2, poss[:, :, 0:E], float(CAP1), m2, ALU.is_lt, ALU.mult))
                    settle()
                    go(V.tensor_reduce(gsm[:, 5, :], k1, AX.X, ALU.add))
                    go(V.tensor_reduce(gsm[:, 6, :], k2, AX.X, ALU.add))
                    settle()
                    go(V.tensor_tensor(gsm[:, 3, :], gsm[:, 3, :], gsm[:, 5, :], ALU.mult))
                    go(V.tensor_tensor(gsm[:, 4, :], gsm[:, 4, :], gsm[:, 6, :], ALU.mult))
                    settle()
                    go(V.tensor_tensor(gsm[:, 7, :], gsm[:, 3, :], gsm[:, 4, :], ALU.add))
                    settle()
                    go(V.tensor_scalar(gsm[:, 7, :], gsm[:, 7, :], GATE_EPS, None, ALU.add))
                    settle()
                    go(V.reciprocal(gsm[:, 7, :], gsm[:, 7, :]))
                    settle()
                    go(V.tensor_tensor(gsm[:, 3, :], gsm[:, 3, :], gsm[:, 7, :], ALU.mult))
                    go(V.tensor_tensor(gsm[:, 4, :], gsm[:, 4, :], gsm[:, 7, :], ALU.mult))
                    settle()
                go(V.tensor_tensor(k1, k1, bc(gsm[:, 3, :], [P, T, E]), ALU.mult))
                go(V.tensor_tensor(k2, k2, bc(gsm[:, 4, :], [P, T, E]), ALU.mult))
                settle()
                V.tensor_tensor(gate[:, :, 0:E], k1, k2, ALU.add).then_inc(gate_ready, 1)

            def gate_hidden(L, banks):
                for m in range(8 if L == 0 else C):
                    dve.wait_ge(up_ready, 8 * L + m + 1)
                    dve.wait_ge(spread_full, 4 * L + m // 2 + 1)
                    V.tensor_tensor(hid[:, m, :], hid[:, m, :], half(banks[m // 2], m % 2), ALU.mult)\
                        .then_inc(hid_ready, 1)

            dve.wait_ge(x_in, 16 * T)
            norm(0, [xa[:, t, :] for t in range(T)])
            for t in range(T):
                norm_rows(xn[:, t, :], xa[:, t, :], t, xn_ready)
            dve.wait_ge(iota_ready, 1)
            go(V.tensor_copy(iota_bf[:, :], iota_i[:, :]))
            go(V.tensor_copy(iota_f[:, :], iota_i[:, 0:E0]))
            dve.wait_ge(edges_in, 32)
            go(V.tensor_copy(edges[:, :, :], edges_i[:, :, :]))
            settle()
            xT_part(0, 1)

            def onehots(j0, j1):
                for j in range(j0, j1):
                    for a in range(2):
                        ins = V.tensor_scalar(onehot[:, j, a, :], iota_bf[:, :], edges[:, a, j:j + 1], None,
                                              ALU.is_equal)
                    ins.then_inc(onehot_ready, 1)

            onehots(0, 16)
            k_max(0)
            onehots(16, 32)
            q_shift(0, (2, 3))
            onehots(32, 48)
            q_norm(0)
            onehots(48, 64)
            dve.wait_ge(small_in, SMALLS)
            for t in range(T):
                dve.wait_ge(h_full, t + 1)
                V.tensor_tensor(cur[:, 0, t, :], bank[t][:, :], row["b_gnn0"], ALU.add).then_inc(cur_ready, 1)
            dve.wait_ge(cur_ready, 2)
            for t in range(T):
                go(V.tensor_scalar(diffused[:, t, :], cur[:, 0, t, :], diffusion[:, 0:1], None, ALU.mult))
            context(0, 6)
            dve.wait_ge(count_ready, 2)
            dve.wait_ge(countT_full, 1)
            dve.wait_ge(countT_ready, 1)
            go(V.tensor_tensor(linked[:, :, :], count[:, :, :], countT[:, :, :], ALU.add))
            settle()
            go(V.tensor_scalar(linked[:, :, :], linked[:, :, :], 1.0, None, ALU.min))
            settle()
            for t in range(T):
                sl = linked[:, t, t * P:(t + 1) * P]
                V.tensor_tensor(sl, sl, ident[:, :], ALU.add).then_inc(linked_ready, 1)
            dve.wait_ge(linked_ready, 2)
            go(V.tensor_reduce(degree[:, :], linked[:, :, :], AX.X, ALU.add))
            settle()
            go(V.tensor_scalar(degree[:, :], degree[:, :], 1.0, None, ALU.max))
            settle()
            go(V.reciprocal(degree[:, :], degree[:, :]))
            for t in range(T):
                for m in (count, countT):
                    sl = m[:, t, t * P:(t + 1) * P]
                    go(V.tensor_tensor(sl, sl, ident[:, :], ALU.add))
            settle()
            go(V.tensor_scalar(far[:, :, :], count[:, :, :], 0.0, -FAR, ALU.is_equal, ALU.mult))
            settle()
            STEPB = ((2, 3), (6, 7), (2, 3))

            def diffuse(i):
                for t in range(T):
                    dve.wait_ge(step_full, 2 * i + t + 1)
                    V.tensor_scalar(cur[:, (i + 1) % 2, t, :], bank[STEPB[i][t]][:, :], degree[:, t:t + 1], None,
                                    ALU.mult).then_inc(cur_ready, 1)
                    dve.wait_ge(cur_ready, 2 * i + t + 3)
                    go(V.scalar_tensor_tensor(diffused[:, t, :], cur[:, (i + 1) % 2, t, :], diffusion[:, i + 1:i + 2],
                                              diffused[:, t, :], ALU.mult, ALU.add))

            diffuse(0)
            for t in range(T):
                dve.wait_ge(o_full, t + 1)
            norm(1, [bank[t][:, :] for t in range(T)])
            for t in range(T):
                norm_rows(mixed[:, t, :], bank[t][:, :], t, mix_ready)
            dve.wait_ge(mix_ready, 2)
            for t in range(T):
                go(V.tensor_tensor(mixed[:, t, :], mixed[:, t, :], row["gamma0"], ALU.mult))
            settle()
            go(V.tensor_tensor(mixed[:, :, :], mixed[:, :, :], xa[:, :, :], ALU.add))
            diffuse(1)
            diffuse(2)
            settle()
            for t in range(T):
                go(V.scalar_tensor_tensor(xb[:, t, :], diffused[:, t, :], 0.0, mixed[:, t, :], ALU.max, ALU.add))
            settle()
            dve.wait_ge(xT_full, 2)
            norm(2, [xb[:, t, :] for t in range(T)])
            for t in range(T):
                norm_rows(xn[:, t, :], xb[:, t, :], t, xn_ready)
            xT_part(1, 5)
            gates(0, 6, 7)
            gate_hidden(0, (4, 5, 7, 6))
            for t in range(T):
                dve.wait_ge(down_full, t + 1)
                go(V.tensor_tensor(xa[:, t, :], bank[t][:, :], xb[:, t, :], ALU.add))
            settle()

            norm(3, [xa[:, t, :] for t in range(T)])
            for t in range(T):
                norm_rows(xn[:, t, :], xa[:, t, :], t, xn_ready)
            xT_part(2, 3)
            PAIR = (0, 1, 6, 7)
            for j in range(4):
                dve.wait_ge(src_full, j + 1)
                settle()
                if j:
                    dve.wait_ge(max_ready, j)
                for h in range(2):
                    for t in range(T):
                        if h or t:
                            go(ins)
                        ins = V.tensor_tensor_reduce(out=junk[:, 2 * h + t, :], in0=half(PAIR[j], h), in1=far[:, t, :],
                                                     scale=1.0, scalar=-BIG, op0=ALU.add, op1=ALU.max,
                                                     accum_out=mx[:, t, 2 * j + h:2 * j + h + 1])
                ins.then_inc(max_ready, 1)
            dve.wait_ge(max_ready, 4)
            dve.wait_ge(al_ready, 1)
            go(V.tensor_tensor(mx[:, :, :], mx[:, :, :], al[:, :, H:2 * H], ALU.add))
            settle()
            V.scalar_tensor_tensor(mz[:, :, :], mx[:, :, :], SLOPE, mx[:, :, :], ALU.mult, ALU.max)\
                .then_inc(max_ready, 1)
            k_max(1)

            for j in range(4):
                dve.wait_ge(z_ready, 4 * j + 4)
                for s in range(T):
                    z = logit[:, s, 2 * j:2 * j + 2, :]
                    go(V.scalar_tensor_tensor(z, z, SLOPE, z, ALU.mult, ALU.max))
            settle()
            q_shift(1, (2, 3))
            for j in range(4):
                dve.wait_ge(max_full, j + 1)
                for s in range(T):
                    z = logit[:, s, 2 * j:2 * j + 2, :]
                    V.tensor_tensor(z, z, bank[PAIR[j]][:, :].rearrange("p (h n) -> p h n", h=2), ALU.subtract)\
                        .then_inc(shifted, 1)
            q_norm(1)
            for j in range(4):
                for s in range(T):
                    dve.wait_ge(exp_ready, 2 * j + s + 1)
                    z = logit[:, s, 2 * j:2 * j + 2, :]
                    V.scalar_tensor_tensor(z, z, BIG, countT[:, s:s + 1, :].broadcast_to([P, 2, N]), ALU.min, ALU.mult)\
                        .then_inc(weight_ready, 1)
            context(1, 4)

            def gat_norm(g, i, srcs_ready):
                b, gg, beta = (("b1", "g1", "beta1"), ("b2", "g2", "beta2"))[g]
                settle()
                for t in range(T):
                    go(V.tensor_tensor(g_a[:, t, :], g_a[:, t, :], row[b], ALU.add))
                settle()
                norm(i, [g_a[:, t, :] for t in range(T)])
                for t in range(T):
                    norm_rows(g_a[:, t, :], g_a[:, t, :], t)
                settle()
                for t in range(T):
                    go(V.tensor_tensor(g_a[:, t, :], g_a[:, t, :], row[gg], ALU.mult))
                settle()
                for t in range(T):
                    go(V.tensor_tensor(g_a[:, t, :], g_a[:, t, :], row[beta], ALU.add))
                settle()
                V.tensor_scalar(g_b[:, :, :], g_a[:, :, :], 0.0, None, ALU.min).then_inc(elu_min, 1)
                dve.wait_ge(elu_exp, g + 1)
                go(V.scalar_tensor_tensor(g_a[:, :, :], g_a[:, :, :], 0.0, g_b[:, :, :], ALU.max, ALU.add))
                settle()

            AGG = ((0, 1), (6, 7))
            for t in range(T):
                for u in range(2):
                    dve.wait_ge(agg_full, 2 * t + u + 1)
                    src = bank[AGG[t][u]][:, 0:4 * (HD + 1)].rearrange("p (h n) -> p h n", h=4)
                    go(V.reciprocal(mx[:, t, 4 * u:4 * u + 4], src[:, :, HD]))
                    settle()
                    dst = g_a[:, t, 4 * u * HD:4 * (u + 1) * HD].rearrange("p (h n) -> p h n", h=4)
                    V.tensor_tensor(dst, src[:, :, 0:HD], bc(mx[:, t, 4 * u:4 * u + 4], [P, 4, HD]), ALU.mult)\
                        .then_inc(agg_ready, 1)
            dve.wait_ge(agg_ready, 4)
            gat_norm(0, 4, None)
            dve.wait_ge(qT_full, 4)
            for t in range(T):
                V.scalar_tensor_tensor(x1g[:, t, :], g_a[:, t, :], -1.0, xn[:, t, :], ALU.add, ALU.add)\
                    .then_inc(xn_ready, 1)
            xT_part(3, 1)
            for t in range(T):
                dve.wait_ge(o_full, 2 + t + 1)
                V.tensor_tensor(mixed[:, t, :], bank[3 + t][:, :], row["b_out1"], ALU.add).then_inc(mix_ready, 1)
            dve.wait_ge(mix_ready, 4)
            go(V.tensor_tensor(mixed[:, :, :], mixed[:, :, :], xa[:, :, :], ALU.add))
            dve.wait_ge(src_full, 5)
            for t in range(T):
                go(V.tensor_tensor_reduce(out=junk[:, t, :], in0=half(2, 0), in1=far[:, t, :], scale=1.0, scalar=-BIG,
                                          op0=ALU.add, op1=ALU.max, accum_out=mx[:, t, 0:1]))
            dve.wait_ge(al_ready, 2)
            settle()
            go(V.tensor_tensor(mx[:, :, 0:1], mx[:, :, 0:1], al[:, :, 1:2], ALU.add))
            settle()
            V.scalar_tensor_tensor(mz[:, :, 0:1], mx[:, :, 0:1], SLOPE, mx[:, :, 0:1], ALU.mult, ALU.max)\
                .then_inc(max_ready, 1)
            dve.wait_ge(z_ready, 18)
            z = logit[:, :, 0, :]
            go(V.scalar_tensor_tensor(z, z, SLOPE, z, ALU.mult, ALU.max))
            settle()
            dve.wait_ge(max_full, 5)
            for s in range(T):
                V.tensor_tensor(logit[:, s, 0, :], logit[:, s, 0, :], half(7, 0), ALU.subtract).then_inc(shifted, 1)
            for s in range(T):
                dve.wait_ge(exp_ready, 8 + s + 1)
                V.scalar_tensor_tensor(logit[:, s, 0, :], logit[:, s, 0, :], BIG, countT[:, s, :], ALU.min, ALU.mult)\
                    .then_inc(weight_ready, 1)
            for t in range(T):
                dve.wait_ge(agg_full, 4 + t + 1)
                go(V.reciprocal(mx[:, t, 1:2], bank[(2, 5)[t]][:, 0:1]))
                settle()
                go(V.tensor_scalar(g_a[:, t, :], bank[t][:, :], mx[:, t, 1:2], None, ALU.mult))
            gat_norm(1, 5, None)
            go(V.scalar_tensor_tensor(g_a[:, :, :], g_a[:, :, :], -1.0, x1g[:, :, :], ALU.add, ALU.add))
            settle()
            go(V.tensor_tensor(xb[:, :, :], g_a[:, :, :], mixed[:, :, :], ALU.add))
            settle()
            norm(6, [xb[:, t, :] for t in range(T)])
            for t in range(T):
                norm_rows(xn[:, t, :], xb[:, t, :], t, xn_ready)
            xT_part(4, 4)
            gates(1, 5, 6)
            gate_hidden(1, (2, 5))
            for t in range(T):
                dve.wait_ge(down_full, 2 + t + 1)
                V.tensor_tensor(xa[:, t, :], bank[3 + t][:, :], xb[:, t, :], ALU.add).then_inc(out_ready, 1)

        @block.tensor
        def _(pe):
            mm = nc.tensor.matmul

            def product(dst, lhs, rhs, k):
                for c in range(k):
                    ins = mm(dst, lhs(c), rhs(c), start=c == 0, stop=c == k - 1)
                return ins

            def xT_made(i, src, banks, after):
                pe.wait_ge(xn_ready, 2 * i + 2)
                for s, nn in after:
                    pe.wait_ge(s, nn)
                for j in range(2):
                    for c in (2 * j, 2 * j + 1):
                        for t in range(T):
                            o = (c % 2) * N + t * P
                            ins = nc.tensor.transpose(bank[banks[j]][:, o:o + P], src[:, t, c * P:(c + 1) * P],
                                                      ident[:, :])
                    ins.then_inc(xT_full, 1)

            def rows_of(w, banks, full, waits=((), ())):
                for t in range(T):
                    for s, nn in waits[t]:
                        pe.wait_ge(s, nn)
                    product(bank[banks[t]][:, :], lambda c: xT[:, c, t * P:(t + 1) * P], lambda c: w[:, c, :], C)\
                        .then_inc(full, 1)

            def k_of(w, full):
                for m in range(C):
                    ins = product(half(4 + m // 2, m % 2), lambda c: w[:, c, m * P:(m + 1) * P],
                                  lambda c: xT[:, c, :], C)
                    if m % 2:
                        ins.then_inc(full, 1)

            def ek_made(L, banks):
                for t in range(T):
                    for m in range(C):
                        ins = nc.tensor.transpose(bank[banks[t]][:, m * P:(m + 1) * P], ekT[:, m, t * P:(t + 1) * P],
                                                  ident[:, :])
                    ins.then_inc(ek_full, 1)

            def qT_made(banks):
                for j in range(2):
                    for m in (2 * j, 2 * j + 1):
                        for t in range(T):
                            o = (m % 2) * N + t * P
                            ins = nc.tensor.transpose(bank[banks[j]][:, o:o + P], q[:, t, m * P:(m + 1) * P],
                                                      ident[:, :])
                    ins.then_inc(qT_full, 1)

            def context(b):
                for m in range(C):
                    cols = slice(m * P, (m + 1) * P)
                    ins = product(bank[b][:, cols], lambda t: ek[:, t, cols], lambda t: v[:, t, cols], T)
                ins.then_inc(ctx_full, 1)

            def yT_made(L, banks, waits):
                for m in range(C):
                    if m % 2 == 0:
                        for s, nn in waits[m // 2]:
                            pe.wait_ge(s, nn)
                    ins = mm(half(banks[m // 2], m % 2), ctxbd[:, m, :], qT[:, m, :], start=True, stop=True)
                    if m % 2:
                        ins.then_inc(yT_full, 1)

            def attn_out(w, banks):
                for t in range(T):
                    product(bank[banks[t]][:, :], lambda m: yT[:, m, t * P:(t + 1) * P], lambda m: w[:, m, :], C)\
                        .then_inc(o_full, 1)

            def positions(L, b):
                E2 = 2 * EXPERTS[L]
                E = EXPERTS[L]
                pe.wait_ge(masks_ready, L + 1)
                mm(bank[b][:, 0:E2], before[:, :], mask[:, 0, 0:E2], start=True, stop=True)
                mm(bank[b][:, E2:2 * E2], ones[:, :], mask[:, 0, 0:E2], start=True, stop=False)
                mm(bank[b][:, E2:2 * E2], before[:, :], mask[:, 1, 0:E2], start=False, stop=True)
                mm(bank[b][:, 2 * E2:2 * E2 + E], ones[:, :], mask[:, 0, 0:E], start=True, stop=False)
                mm(bank[b][:, 2 * E2:2 * E2 + E], ones[:, :], mask[:, 1, 0:E], start=False, stop=True)\
                    .then_inc(pos_full, 1)

            def gate_spread(L, b, banks, waits):
                E = EXPERTS[L]
                pe.wait_ge(gate_ready, L + 1)
                for t in range(T):
                    ins = nc.tensor.transpose(bank[b][0:E, t * P:(t + 1) * P], gate[:, t, 0:E], ident[:, :])
                ins.then_inc(gateT_full, 1)
                pe.wait_ge(gateT_ready, L + 1)
                for s, nn in waits:
                    pe.wait_ge(s, nn)
                for m in range(len(banks) * 2):
                    ins = mm(half(banks[m // 2], m % 2), spread[0:E, m, :, :].rearrange("p a f -> p (a f)"),
                             gateT[0:E, :], start=True, stop=True)
                    if m % 2:
                        ins.then_inc(spread_full, 1)

            def up(w, m_count, full):
                for m in range(m_count):
                    ins = product(half(m // 2, m % 2), lambda c: w[:, c, m * P:(m + 1) * P], lambda c: xT[:, c, :], C)
                    if m % 2:
                        ins.then_inc(full, 1)

            def logits(w, b, L):
                E = EXPERTS[L]
                for t in range(T):
                    ins = product(bank[b][:, t * E:(t + 1) * E], lambda c: xT[:, c, t * P:(t + 1) * P],
                                  lambda c: w[:, c, :], C)
                ins.then_inc(logits_full, 1)

            pe.wait_ge(consts, 1)
            xT_made(0, xn, (0, 1), ())
            pe.wait_ge(xT_ready, 2)
            pe.wait_ge(win["k0"], 16)
            k_of(w_k0, k_full)
            pe.wait_ge(win["q0"], 16)
            rows_of(w_q0, (2, 3), q_full)
            pe.wait_ge(win["v0"], 16)
            rows_of(w_v0, (6, 7), v_full)
            pe.wait_ge(win["gnn0"], 16)
            rows_of(w_gnn0, (0, 1), h_full)
            pe.wait_ge(ekT_ready, 4)
            ek_made(0, (4, 5))
            pe.wait_ge(q_shifted, 2)

            def counts(j0, j1):
                for j in range(j0, j1):
                    pe.wait_ge(onehot_ready, j + 1)
                    for t in range(T):
                        ins = mm(half(2 + t, 0), onehot[:, j, 1, t * P:(t + 1) * P], onehot[:, j, 0, :],
                                 start=j == 0, stop=j == ET - 1)
                return ins

            counts(0, 48)
            pe.wait_ge(v_ready, 2)
            pe.wait_ge(ek_ready, 2)
            context(6)
            counts(48, 64).then_inc(count_full, 1)
            pe.wait_ge(q_ready, 2)
            pe.wait_ge(cur_ready, 2)
            qT_made((0, 1))
            pe.wait_ge(count_ready, 2)
            for s in range(T):
                for t in range(T):
                    ins = nc.tensor.transpose(bank[7][:, s * N + t * P:s * N + (t + 1) * P],
                                              count[:, t, s * P:(s + 1) * P], ident[:, :])
            ins.then_inc(countT_full, 1)
            pe.wait_ge(ctx_ready, 2)
            pe.wait_ge(qT_ready, 2)
            yT_made(0, (4, 5), ((), ()))

            def diffuse(i, banks):
                for t in range(T):
                    product(bank[banks[t]][:, :], lambda s: linked[:, s, t * P:(t + 1) * P],
                            lambda s: cur[:, i % 2, s, :], T).then_inc(step_full, 1)

            pe.wait_ge(linked_ready, 2)
            diffuse(0, (2, 3))
            pe.wait_ge(win["out0"], 16)
            pe.wait_ge(yT_ready, 2)
            attn_out(w_out0, (0, 1))
            pe.wait_ge(cur_ready, 4)
            diffuse(1, (6, 7))
            pe.wait_ge(cur_ready, 6)
            diffuse(2, (2, 3))
            xT_made(1, xn, (4, 5), ())
            pe.wait_ge(xT_ready, 4)
            pe.wait_ge(win["gate"], 16)
            logits(w_gate, 6, 0)
            pe.wait_ge(mix_ready, 2)
            pe.wait_ge(cur_ready, 8)
            pe.wait_ge(win["up0"], 16)
            pe.wait_ge(consts, 2)
            up(w_up0, 8, up_full)
            positions(0, 7)
            gate_spread(0, 6, (4, 5, 7, 6), ())
            pe.wait_ge(win["down0"], 16)
            for t in range(T):
                for m in range(8):
                    if t == 0:
                        pe.wait_ge(hid_ready, m + 1)
                    ins = mm(bank[t][:, :], hid[:, m, t * P:(t + 1) * P], w_down0[:, m, :],
                             start=m == 0, stop=m == 7)
                ins.then_inc(down_full, 1)

            pe.wait_ge(win["w1t"], 16)
            pe.wait_ge(win["w2t"], 16)
            A2 = 2 * H + 2
            for kc in range(C):
                product(bank[5][:, kc * A2:kc * A2 + 2 * H], lambda m: w1t[:, m, kc * P:(kc + 1) * P],
                        lambda m: attblk[:, m, :], C)
                ins = product(bank[5][:, kc * A2 + 2 * H:(kc + 1) * A2], lambda m: w2t[:, m, kc * P:(kc + 1) * P],
                              lambda m: att2[:, :, m], C)
            ins.then_inc(wa_full, 1)
            xT_made(2, xn, (2, 3), ())
            pe.wait_ge(xT_ready, 6)
            pe.wait_ge(wa_ready, 1)
            for t in range(T):
                ins = product(bank[4][:, t * 2 * H:(t + 1) * 2 * H], lambda c: xT[:, c, t * P:(t + 1) * P],
                              lambda c: wa[:, c, 0:2 * H], C)
            ins.then_inc(al_full, 1)
            for a in range(2):
                ins = product(bank[5][0:H, a * N:(a + 1) * N], lambda c: wa[:, c, a * H:(a + 1) * H],
                              lambda c: xT[:, c, :], C)
            ins.then_inc(alT_full, 1)
            PAIR = (0, 1, 6, 7)

            def broadcast(rows_ap, full):
                for h in range(H):
                    ins = mm(half(PAIR[h // 2], h % 2), pick[0:H, h, :], rows_ap, start=True, stop=True)
                    if h % 2:
                        ins.then_inc(full, 1)

            pe.wait_ge(alT_ready, 1)
            pe.wait_ge(xn_ready, 6)
            broadcast(alT[:, 0, :], src_full)
            pe.wait_ge(win["gat1"], 16)
            rows_of(w_gat1, (2, 3), hx_full)
            pe.wait_ge(win["k1"], 16)
            k_of(w_k1, k_full)
            pe.wait_ge(max_ready, 4)
            broadcast(alT[:, 1, :], dst_full)
            pe.wait_ge(win["q1"], 16)
            pe.wait_ge(hx_ready, 2)
            rows_of(w_q1, (2, 3), q_full)
            pe.wait_ge(max_ready, 5)
            pe.wait_ge(ekT_ready, 8)
            for t in range(T):
                ins = nc.tensor.transpose(bank[4][0:H, t * P:(t + 1) * P], mz[:, t, :], ident[:, :])
            ins.then_inc(mT_full, 1)
            pe.wait_ge(win["v1"], 16)
            pe.wait_ge(q_shifted, 4)
            rows_of(w_v1, (2, 3), v_full)
            pe.wait_ge(mT_ready, 1)
            pe.wait_ge(z_ready, 16)
            broadcast(mT[:, :], max_full)
            ek_made(1, (4, 5))
            pe.wait_ge(q_ready, 4)
            pe.wait_ge(v_ready, 4)
            qT_made((2, 3))
            pe.wait_ge(ek_ready, 4)
            context(4)
            pe.wait_ge(weight_ready, 8)
            AGG = ((0, 1), (6, 7))
            for t in range(T):
                for h in range(H):
                    o = (h % 4) * (HD + 1)
                    ins = product(bank[AGG[t][h // 4]][:, o:o + HD + 1],
                                  lambda s: logit[:, s, h, t * P:(t + 1) * P], lambda s: hx[:, s, h, :], T)
                    if h % 4 == 3:
                        ins.then_inc(agg_full, 1)
            pe.wait_ge(ctx_ready, 4)
            pe.wait_ge(qT_ready, 4)
            yT_made(1, (5, 2), ((), ()))
            pe.wait_ge(win["out1"], 16)
            pe.wait_ge(yT_ready, 4)
            attn_out(w_out1, (3, 4))
            xT_made(3, x1g, (0, 1), ())
            pe.wait_ge(xT_ready, 8)
            for t in range(T):
                ins = product(bank[6][:, t * 2:(t + 1) * 2], lambda c: xT[:, c, t * P:(t + 1) * P],
                              lambda c: wa[:, c, 2 * H:2 * H + 2], C)
            ins.then_inc(al_full, 1)
            for a in range(2):
                ins = product(bank[7][0:1, a * N:(a + 1) * N], lambda c: wa[:, c, 2 * H + a:2 * H + a + 1],
                              lambda c: xT[:, c, :], C)
            ins.then_inc(alT_full, 1)
            pe.wait_ge(alT_ready, 2)
            pe.wait_ge(al_ready, 2)
            for a in range(2):
                ins = mm(half((2, 6)[a], 0), ones[0:1, :], alT[0:1, a, :], start=True, stop=True)
            ins.then_inc(src_full, 1)
            pe.wait_ge(win["gat2"], 16)
            pe.wait_ge(mix_ready, 4)
            rows_of(w_gat2, (3, 4), hx_full)
            pe.wait_ge(max_ready, 6)
            for t in range(T):
                ins = nc.tensor.transpose(bank[5][0:1, t * P:(t + 1) * P], mz[:, t, 0:1], ident[:, :])
            ins.then_inc(mT_full, 1)
            pe.wait_ge(mT_ready, 2)
            mm(half(7, 0), ones[0:1, :], mT[0:1, :], start=True, stop=True).then_inc(max_full, 1)
            pe.wait_ge(hx_ready, 4)
            pe.wait_ge(weight_ready, 10)
            for t in range(T):
                product(bank[t][:, :], lambda s: logit[:, s, 0, t * P:(t + 1) * P], lambda s: h2[:, s, :], T)
                product(bank[(2, 5)[t]][:, 0:1], lambda s: logit[:, s, 0, t * P:(t + 1) * P],
                        lambda s: ones[:, 0:1], T).then_inc(agg_full, 1)
            xT_made(4, xn, (3, 4), ())
            pe.wait_ge(xT_ready, 10)
            logits(w_router, 5, 1)
            pe.wait_ge(win["up1"], 16)
            up(w_up1, C, up_full)
            positions(1, 6)
            gate_spread(1, 7, (2, 5), ())
            pe.wait_ge(win["down1"], 16)
            for t in range(T):
                mm(bank[3 + t][:, :], gateT[0:EXPERTS[1], t * P:(t + 1) * P], b_down1[:, :], start=True, stop=False)
                for m in range(C):
                    if t == 0:
                        pe.wait_ge(hid_ready, 8 + m + 1)
                    ins = mm(bank[3 + t][:, :], hid[:, m, t * P:(t + 1) * P], w_down1[:, m, :],
                             start=False, stop=m == C - 1)
                ins.then_inc(down_full, 1)


def _chunks(a):
    c = a.shape[0] // 128
    return a.reshape(c, 128, -1).transpose(1, 0, 2)


def kernel(**inputs):
    import numpy as np
    import concourse.bacc as bacc
    from concourse import mybir
    from concourse.bass_utils import run_bass_kernel_spmd

    a = {k: np.asarray(v) for k, v in inputs.items()}
    hidden = 512
    wq0, wk0, wv0 = (a["L0_mix_w_qkv"][i * hidden:(i + 1) * hidden].T for i in range(3))
    wq1, wk1, wv1 = (a["L1_mix_W_qkv"][:, i * hidden:(i + 1) * hidden] for i in range(3))

    def experts_in(w):
        return _chunks(w.transpose(1, 0, 2).reshape(w.shape[1], -1))

    def experts_out(w):
        return _chunks(w.reshape(-1, w.shape[2]))

    def column(v):
        return v.reshape(-1, 128).T

    arrays = {
        "x": a["x"], "src": a["src"], "dst": a["dst"],
        "k0": _chunks(wk0), "q0": _chunks(wq0), "v0": _chunks(wv0),
        "gnn0": _chunks(a["L0_gnn_W"]), "out0": _chunks(a["L0_mix_w_out"].T),
        "b_gnn0": a["L0_gnn_b"], "diffusion": a["L0_gnn_diffusion_weights"], "gamma0": a["L0_mix_gamma"],
        "gate": _chunks(a["L0_ffn_w_gating"]), "up0": experts_in(a["L0_ffn_w1"]),
        "down0": experts_out(a["L0_ffn_w2"]),
        "gat1": _chunks(a["L1_gnn_W1"]), "w1t": _chunks(a["L1_gnn_W1"].T),
        "gat2": _chunks(a["L1_gnn_W2"]), "w2t": _chunks(a["L1_gnn_W2"].T),
        "a_src1": column(a["L1_gnn_a_src1"]), "a_dst1": column(a["L1_gnn_a_dst1"]),
        "a_src2": column(a["L1_gnn_a_src2"]), "a_dst2": column(a["L1_gnn_a_dst2"]),
        "b1": a["L1_gnn_b1"], "g1": a["L1_gnn_g1"], "beta1": a["L1_gnn_beta1"],
        "b2": a["L1_gnn_b2"], "g2": a["L1_gnn_g2"], "beta2": a["L1_gnn_beta2"],
        "k1": _chunks(wk1), "q1": _chunks(wq1), "v1": _chunks(wv1),
        "out1": _chunks(a["L1_mix_W_out"]), "b_out1": a["L1_mix_b_out"],
        "router": _chunks(a["L1_ffn_Wr"]), "b_router": a["L1_ffn_br"],
        "up1": experts_in(a["L1_ffn_W1"]), "b_up1": column(a["L1_ffn_b1"]),
        "down1": experts_out(a["L1_ffn_W2"]), "b_down1": a["L1_ffn_b2"],
    }
    arrays = {k: np.ascontiguousarray(v) for k, v in arrays.items()}
    nc = bacc.Bacc("TRN2", target_bir_lowering=False, num_devices=1)
    aps = {k: nc.dram_tensor("in_" + k, v.shape, mybir.dt.from_np(v.dtype), kind="ExternalInput").ap()
           for k, v in arrays.items()}
    out = nc.dram_tensor("out", a["x"].shape, mybir.dt.from_np(a["x"].dtype), kind="ExternalOutput").ap()
    gps_two_layers(nc, aps, out)
    r = run_bass_kernel_spmd(nc, [{"in_" + k: v for k, v in arrays.items()}], core_ids=[0])
    return r.results[0]["out"]
```

```python
import concourse.bass as bass
from concourse import mybir
from contextlib import ExitStack



def gps_two_layers(nc, A, out):
    f32, bf16, f32r = mybir.dt.float32, mybir.dt.bfloat16, mybir.dt.float32r
    i32, u32 = mybir.dt.int32, mybir.dt.uint32
    ALU, ACT, AX = mybir.AluOpType, mybir.ActivationFunctionType, mybir.AxisListType

    P = 128
    N, D = A["x"].shape
    T = N // P
    C = D // P
    EDGES = A["src"].shape[0]
    ET = EDGES // P
    H, HD = 8, 64
    STEPS = A["diffusion"].shape[0] - 1
    EXPERTS = (16, 8)
    FF = 64
    CAP0 = max(min(N, int(N * 2 * 2.0 / EXPERTS[0])), 4)
    CAP1 = max(1, -int(-1.25 * N * 2 // EXPERTS[1]))
    EPS, GATE_EPS = 1e-5, 1e-9
    SLOPE = 0.2
    BIG = 3.0e38
    FAR = 1.0e30

    ctx = ExitStack()
    with ctx:
        def sb(name, shape, dt=f32):
            return ctx.enter_context(nc.sbuf_tensor(name, shape, dt))

        def sem(name):
            return ctx.enter_context(nc.semaphore(name))

        UNIT, RAWS, SLOTS = 2 * D, 4, 6
        raw = sb("raw", [P, RAWS, UNIT])
        w_hi = sb("w_hi", [P, SLOTS, UNIT], f32r)
        w_lo = sb("w_lo", [P, SLOTS, UNIT], f32r)
        ORDER = ["k0", "q0", "v0", "gnn0", "out0", "up0", "down0",
                 "gat1", "k1", "q1", "v1", "out1", "gat2", "up1", "down1"]
        unit_of, units = {}, []
        for name in ORDER:
            unit_of[name] = len(units)
            parts = A[name].shape[1] * A[name].shape[2] // UNIT
            flat = A[name].rearrange("p c n -> p (c n)")
            units += [(name, flat[:, i * UNIT:(i + 1) * UNIT]) for i in range(parts)]
        U = len(units)

        class Weight:

            def __init__(self, name):
                self.first, self.width = unit_of[name], A[name].shape[2]
                self.units = A[name].shape[1] * self.width // UNIT

            def at(self, c, c0=0, c1=None):
                o = c * self.width + c0
                slot = (self.first + o // UNIT) % SLOTS
                n = (self.width if c1 is None else c1) - c0
                return tuple(w[:, slot, o % UNIT:o % UNIT + n] for w in (w_hi, w_lo))

        ring = sb("ring", [P, 4 * 1024])
        RING = 16
        onehot = ring[:, :].bitcast(bf16).rearrange("p (j a n) -> p j a n", j=RING, a=2)
        w1t = ring[:, 2048:4096].rearrange("p (c n) -> p c n", c=C)
        w2t = ring[:, 0:2048].rearrange("p (c n) -> p c n", c=C)
        hid = ring[:, 0:2048].rearrange("p (c n) -> p c n", c=8)
        logit = ring[:, :].rearrange("p (s h n) -> p s h n", s=T, h=H)
        w_gate = sb("w_gate", [P, C, EXPERTS[0]])
        w_router = sb("w_router", [P, C, EXPERTS[1]])
        narrow_hi = sb("narrow_hi", [P, 2, C, EXPERTS[0]], f32r)
        narrow_lo = sb("narrow_lo", [P, 2, C, EXPERTS[0]], f32r)

        row_names = ["b_gnn0", "gamma0", "b1", "g1", "beta1", "b2", "g2", "beta2", "b_out1"]
        rows = sb("rows", [P, len(row_names), D])
        row = {n: rows[:, i, :] for i, n in enumerate(row_names)}
        diffusion = sb("diffusion", [P, STEPS + 1])
        b_router = sb("b_router", [P, EXPERTS[1]])
        b_up1 = sb("b_up1", [P, C])
        b_down1 = sb("b_down1", [EXPERTS[1], D])
        b_down_hi = sb("b_down_hi", [EXPERTS[1], D], f32r)
        b_down_lo = sb("b_down_lo", [EXPERTS[1], D], f32r)
        att1 = sb("att1", [P, 2, C])
        att2 = sb("att2", [P, 2, C])

        ident = sb("ident", [P, P])
        ones = sb("ones", [P, P])
        before = sb("before", [P, P])
        pick = sb("pick", [H, H, P], f32r)
        spread = sb("spread", [EXPERTS[0], 8, 2, FF], f32r)
        headmask = sb("headmask", [P, C, H])
        iota_i = sb("iota_i", [P, N], i32)
        iota_bf = sb("iota_bf", [P, N], bf16)
        iota_f = sb("iota_f", [P, EXPERTS[0]])
        minus_half = sb("minus_half", [P, T])
        edges_i = sb("edges_i", [P, 2, ET], i32)
        edges = sb("edges", [P, 2, ET])

        xa = sb("xa", [P, T, D])
        xb = sb("xb", [P, T, D])
        xn = sb("xn", [P, T, D])
        xT_hi = sb("xT_hi", [P, C, N], f32r)
        xT_lo = sb("xT_lo", [P, C, N], f32r)
        q = sb("q", [P, T, D])
        v = sb("v", [P, T, D])
        ek = sb("ek", [P, T, D])
        ekT = sb("ekT", [P, C, N])
        qT = ekT
        yT_hi = sb("yT_hi", [P, C, N], f32r)
        yT_lo = sb("yT_lo", [P, C, N], f32r)
        ctxbd = sb("ctxbd", [P, C, P])
        hr = sb("hr", [P, T, D])
        both_hi = sb("both_hi", [P, 2, T * D], f32r)
        both_lo = sb("both_lo", [P, 2, T * D], f32r)
        cur_hi = both_hi[:, :, :].rearrange("p i (t n) -> p i t n", t=T)
        cur_lo = both_lo[:, :, :].rearrange("p i (t n) -> p i t n", t=T)
        hid_hi = both_hi[:, :, :].rearrange("p i (c n) -> p (i c) n", n=N)
        hid_lo = both_lo[:, :, :].rearrange("p i (c n) -> p (i c) n", n=N)
        diffused = sb("diffused", [P, T, D])
        mixed = v
        count = sb("count", [P, T, N])
        countT = sb("countT", [P, T, N])
        linked = sb("linked", [P, T, N], f32r)
        far = sb("far", [P, T, N])
        hx = sb("hx", [P, T, H, HD + 1])
        h2 = ek
        g_a = hr
        g_b = diffused
        x1g = q
        A2 = 2 * H + 2
        wa = sb("wa", [P, C, A2])
        wa_hi = sb("wa_hi", [P, C, A2], f32r)
        wa_lo = sb("wa_lo", [P, C, A2], f32r)
        al = sb("al", [P, T, 2 * H])
        rows_hi = sb("rows_hi", [EXPERTS[0], 2, N], f32r)
        rows_lo = sb("rows_lo", [EXPERTS[0], 2, N], f32r)
        alT_hi, alT_lo = rows_hi[0:H, :, :], rows_lo[0:H, :, :]
        mT_hi, mT_lo = rows_hi[0:H, 0, :], rows_lo[0:H, 0, :]
        gateT_hi, gateT_lo = rows_hi[:, 1, :], rows_lo[:, 1, :]
        mx = sb("mx", [P, T, H])
        mz = sb("mz", [P, T, H])
        junk = g_a[:, :, :].rearrange("p t (a n) -> p (t a) n", a=2)
        attblk = sb("attblk", [P, C, 2 * H])
        stats = sb("stats", [P, T, 6])
        mv = sb("mv", [P, T, 2])
        veps = sb("veps", [P, T])
        rstd = sb("rstd", [P, T])
        kmax = sb("kmax", [P, C])
        ksum = sb("ksum", [P, C])
        kinv = sb("kinv", [P, C])
        qmax = sb("qmax", [P, T, H])
        qsum = sb("qsum", [P, T, H])
        degree = sb("degree", [P, T])
        degree_w = sb("degree_w", [P, STEPS, T])
        E0 = EXPERTS[0]
        lg = sb("lg", [P, T, E0])
        prob = sb("prob", [P, T, E0])
        prob2 = sb("prob2", [P, T, E0])
        gsm = sb("gsm", [P, 8, T])
        top = sb("top", [P, 2, T, 8])
        top_i = sb("top_i", [P, 2, T, 8], u32)
        top_f = sb("top_f", [P, 2, T])
        mask = sb("mask", [P, T, 2 * E0])
        kept = sb("kept", [P, T, 2 * E0])
        poss = sb("poss", [P, T, 2 * E0])
        gate = sb("gate", [P, T, E0])

        bank = [ctx.enter_context(nc.psum_tensor(f"bank{i}", [P, 512], f32)) for i in range(8)]

        x_in, edges_in, small_in = sem("x_in"), sem("edges_in"), sem("small_in")
        raw_in = [sem(f"raw_in{i}") for i in range(RAWS)]
        hi_ready, lo_ready = sem("hi_ready"), sem("lo_ready")
        w1t_in, w2t_in, narrow_ready = sem("w1t_in"), sem("w2t_in"), sem("narrow_ready")
        consts, iota_ready = sem("consts"), sem("iota_ready")
        var_ready, rstd_ready, xn_ready = sem("var_ready"), sem("rstd_ready"), sem("xn_ready")
        xT_full, xT_rounded, xT_ready = sem("xT_full"), sem("xT_rounded"), sem("xT_ready")
        k_full, kmax_ready, ekT_ready, ek_full, ek_ready = (sem(n) for n in
            ["k_full", "kmax_ready", "ekT_ready", "ek_full", "ek_ready"])
        q_full, q_shifted, q_exp, q_ready, qT_full, qT_ready = (sem(n) for n in
            ["q_full", "q_shifted", "q_exp", "q_ready", "qT_full", "qT_ready"])
        v_full, v_ready, ctx_full, ctx_ready = (sem(n) for n in
            ["v_full", "v_ready", "ctx_full", "ctx_ready"])
        yT_full, yT_rounded, yT_ready, o_full, mix_ready = (sem(n) for n in
            ["yT_full", "yT_rounded", "yT_ready", "o_full", "mix_ready"])
        onehot_used = sem("onehot_used")
        onehot_ready, count_full, count_ready, countT_full, linked_ready, countT_ready = (sem(n) for n in
            ["onehot_ready", "count_full", "count_ready", "countT_full", "linked_ready", "countT_ready"])
        h_full, hr_ready, cur_rounded, cur_ready, step_full, step_read = (sem(n) for n in
            ["h_full", "hr_ready", "cur_rounded", "cur_ready", "step_full", "step_read"])
        logits_full, shift_ready, gexp_ready, masks_ready, pos_full = (sem(n) for n in
            ["logits_full", "shift_ready", "gexp_ready", "masks_ready", "pos_full"])
        gate_ready, gateT_full, gateT_rounded, gateT_ready, spread_full = (sem(n) for n in
            ["gate_ready", "gateT_full", "gateT_rounded", "gateT_ready", "spread_full"])
        up_full, up_ready, gated, hid_rounded, hid_ready, down_full = (sem(n) for n in
            ["up_full", "up_ready", "gated", "hid_rounded", "hid_ready", "down_full"])
        wa_full, wa_read, wa_ready, al_full, al_ready, alT_full, alT_rounded, alT_ready = (sem(n) for n in
            ["wa_full", "wa_read", "wa_ready", "al_full", "al_ready", "alT_full", "alT_rounded", "alT_ready"])
        src_full, max_ready, mT_full, mT_rounded, mT_ready, hx_full, hx_ready = (sem(n) for n in
            ["src_full", "max_ready", "mT_full", "mT_rounded", "mT_ready", "hx_full", "hx_ready"])
        dst_full, z_ready, max_full, shifted, exp_ready, weight_ready = (sem(n) for n in
            ["dst_full", "z_ready", "max_full", "shifted", "exp_ready", "weight_ready"])
        agg_full, y_ready, elu_exp, out_ready, stored = (sem(n) for n in
            ["agg_full", "y_ready", "elu_exp", "out_ready", "stored"])
        degree_ready = sem("degree_ready")
        agg_ready, xn_less_one = sem("agg_ready"), sem("xn_less_one")
        dve_step, pool_step = sem("dve_step"), sem("pool_step")

        xT_read = {1: (h_full, 2), 2: (up_full, 4), 3: (v_full, 4), 4: (hx_full, 4)}
        last_read = {"k0": (k_full, 2), "q0": (q_full, 2), "v0": (v_full, 2), "gnn0": (h_full, 2),
                     "out0": (o_full, 2), "up0": (up_full, 4), "down0": (down_full, 2), "gat1": (hx_full, 2),
                     "k1": (k_full, 4), "q1": (q_full, 4), "v1": (v_full, 4), "out1": (o_full, 4),
                     "gat2": (hx_full, 4)}

        block = ctx.enter_context(nc.Block())

        def half(b, i, n=N):
            return bank[b][:, i * n:(i + 1) * n]

        @block.sync
        def _(sp):
            for t in range(T):
                sp.dma_start(xa[:, t, :], A["x"][t * P:(t + 1) * P, :]).then_inc(x_in, 16)

            def load(u0, u1):
                for u in range(u0, u1):
                    if u >= RAWS:
                        sp.wait_ge(lo_ready, u - RAWS + 1)
                    sp.dma_start(raw[:, u % RAWS, :], units[u][1]).then_inc(raw_in[u % RAWS], 16)

            load(0, 2)
            for a, n in enumerate(("src", "dst")):
                sp.dma_start(edges_i[:, a, :], A[n].rearrange("(p j) -> p j", p=P)).then_inc(edges_in, 16)
            load(2, 8)
            sp.dma_start(w_gate[:, :, :], A["gate"]).then_inc(small_in, 16)
            sp.dma_start(diffusion[:, :], A["diffusion"].partition_broadcast(P)).then_inc(small_in, 16)
            for n in row_names:
                sp.dma_start(row[n], A[n].partition_broadcast(P)).then_inc(small_in, 16)
            sp.dma_start(b_router[:, :], A["b_router"].partition_broadcast(P)).then_inc(small_in, 16)
            sp.dma_start(b_up1[:, :], A["b_up1"]).then_inc(small_in, 16)
            sp.dma_start(b_down1[:, :], A["b_down1"]).then_inc(small_in, 16)
            sp.dma_start(w_router[:, :, :], A["router"]).then_inc(small_in, 16)
            for a, n in enumerate(("a_src1", "a_dst1")):
                sp.dma_start(att1[:, a, :], A[n]).then_inc(small_in, 16)
            for a, n in enumerate(("a_src2", "a_dst2")):
                sp.dma_start(att2[:, a, :], A[n]).then_inc(small_in, 16)
            load(8, 14)
            sp.wait_ge(count_full, 1)
            sp.dma_start(w1t, A["w1t"]).then_inc(w1t_in, 16)
            sp.dma_start(w2t, A["w2t"]).then_inc(w2t_in, 16)
            load(14, U)
            for t in range(T):
                sp.wait_ge(out_ready, t + 1)
                sp.dma_start(out[t * P:(t + 1) * P, :], xa[:, t, :]).then_inc(stored, 16)
            sp.wait_ge(stored, 16 * T)

        SMALLS = 16 * (2 + len(row_names) + 8)

        @block.gpsimd
        def _(pool):
            n = [0]

            def then(ins):
                n[0] += 1
                ins.then_inc(pool_step, 1)
                pool.wait_ge(pool_step, n[0])

            def fill(dst, base, pattern, cm):
                then(nc.gpsimd.affine_select(out=dst, in_=dst.bitcast(f32), compare_op=ALU.not_equal, fill=1.0,
                                             base=base, pattern=pattern, channel_multiplier=cm))

            nc.gpsimd.iota(iota_i[:, :], pattern=[[1, N]], base=0, channel_multiplier=0).then_inc(iota_ready, 1)
            then(nc.gpsimd.memset(minus_half[:, :], -0.5))
            then(nc.gpsimd.memset(ident[:, :], 0.0))
            fill(ident[:, :], 0, [[-1, P]], 1)
            nc.gpsimd.memset(ctxbd[:, :, :], 0.0).then_inc(consts, 1)

            def roots(i):
                for t in range(T):
                    pool.wait_ge(var_ready, T * i + t + 1)
                    nc.gpsimd.tensor_tensor(rstd[:, t:t + 1], veps[:, t:t + 1], minus_half[:, t:t + 1], ALU.pow)\
                        .then_inc(rstd_ready, 1)

            def split(u0, u1):
                for u in range(u0, u1):
                    pool.wait_ge(hi_ready, u + 1)
                    nc.gpsimd.tensor_tensor(w_lo[:, u % SLOTS, :], raw[:, u % RAWS, :],
                                            w_hi[:, u % SLOTS, :].bitcast(f32), ALU.subtract).then_inc(lo_ready, 1)

            roots(0)
            split(0, 8)
            then(nc.gpsimd.memset(ones[:, :], 1.0))
            then(nc.gpsimd.affine_select(out=before[:, :], in_=ones[:, :], compare_op=ALU.is_gt, fill=0.0,
                                         base=0, pattern=[[1, P]], channel_multiplier=-1))
            then(nc.gpsimd.memset(pick[:, :, :].bitcast(f32), 0.0))
            fill(pick[:, :, :], 0, [[-1, H], [0, P]], 1)
            then(nc.gpsimd.memset(spread[:, :, :, :].bitcast(f32), 0.0))
            fill(spread[:, :, :, :], 0, [[-2, 8], [-1, 2], [0, FF]], 1)
            then(nc.gpsimd.memset(headmask[:, :, :], 0.0))
            fill(headmask[0:64, :, :], 0, [[2, C], [-1, H]], 0)
            fill(headmask[64:128, :, :], 1, [[2, C], [-1, H]], 0)
            pool.wait_ge(small_in, SMALLS)
            for a in range(2):
                then(nc.gpsimd.tensor_tensor(attblk[:, :, a * H:(a + 1) * H], headmask[:, :, :],
                                             att1[:, a, :].unsqueeze(2).broadcast_to([P, C, H]), ALU.mult))
            nc.gpsimd.memset(hx[:, :, :, HD:HD + 1], 1.0).then_inc(consts, 1)
            split(8, 14)
            roots(1)
            split(14, 16)
            roots(2)
            split(16, 20)
            roots(3)
            split(20, 26)
            pool.wait_ge(xT_full, 6)
            nc.gpsimd.tensor_scalar(xn[:, :, :], xn[:, :, :], -1.0, None, ALU.add).then_inc(xn_less_one, 1)
            split(26, 32)
            roots(4)
            split(32, 34)
            roots(5)
            roots(6)

        @block.scalar
        def _(act):
            def copy(dst, src):
                return nc.scalar.activation(dst, src, ACT.Copy)

            def hi(u0, u1):
                for u in range(u0, u1):
                    act.wait_ge(raw_in[u % RAWS], 16 * (u // RAWS + 1))
                    if u >= SLOTS:
                        act.wait_ge(*last_read[units[u - SLOTS][0]])
                    copy(w_hi[:, u % SLOTS, :], raw[:, u % RAWS, :]).then_inc(hi_ready, 1)

            def xT_part(i, banks):
                for t in range(T):
                    act.wait_ge(xT_full, T * i + t + 1)
                    if i and t == 0:
                        act.wait_ge(*xT_read[i])
                    copy(xT_hi[:, :, t * P:(t + 1) * P], bank[banks[t]][:, :].rearrange("p (c n) -> p c n", c=C))\
                        .then_inc(xT_rounded, 1)

            def mix_exps(L):
                for m in range(C):
                    act.wait_ge(kmax_ready, 2 * L + m // 2 + 1)
                    if L:
                        act.wait_ge(yT_full, 2)
                    nc.scalar.activation(ekT[:, m, :], half(4 + m // 2, m % 2), ACT.Exp,
                                         bias=kmax[:, m:m + 1], accum_out=ksum[:, m:m + 1]).then_inc(ekT_ready, 1)

            def mix_q(L):
                for t in range(T):
                    act.wait_ge(q_shifted, 2 * L + t + 1)
                    nc.scalar.activation(q[:, t, :], q[:, t, :], ACT.Exp).then_inc(q_exp, 1)

            def mix_v(L, banks):
                for t in range(T):
                    act.wait_ge(v_full, 2 * L + t + 1)
                    if L:
                        act.wait_ge(ctx_full, 1)
                    copy(v[:, t, :], bank[banks[t]][:, :]).then_inc(v_ready, 1)

            def yT_part(L, banks):
                for j in range(2):
                    act.wait_ge(yT_full, 2 * L + j + 1)
                    if L:
                        act.wait_ge(o_full, 2)
                    copy(yT_hi[:, 2 * j:2 * j + 2, :], bank[banks[j]][:, :].rearrange("p (c n) -> p c n", c=2))\
                        .then_inc(yT_rounded, 1)

            def gate_exp(L):
                act.wait_ge(shift_ready, L + 1)
                nc.scalar.activation(prob[:, :, 0:EXPERTS[L]], lg[:, :, 0:EXPERTS[L]], ACT.Exp)\
                    .then_inc(gexp_ready, 1)

            def elu(g):
                for t in range(T):
                    act.wait_ge(y_ready, T * g + t + 1)
                    nc.scalar.activation(g_b[:, t, :], g_a[:, t, :], ACT.Exp).then_inc(elu_exp, 1)

            def diffuse(i, banks):
                for t in range(T):
                    act.wait_ge(step_full, T * i + t + 1)
                    nc.scalar.activation(cur_hi[:, (i + 1) % 2, t, :], bank[banks[t]][:, :], ACT.Copy,
                                         scale=degree[:, t:t + 1]).then_inc(cur_rounded, 1)

            def gateT_part(L, b):
                act.wait_ge(gateT_full, L + 1)
                copy(gateT_hi[0:EXPERTS[L], :], bank[b][0:EXPERTS[L], 0:N]).then_inc(gateT_rounded, 1)

            def hid_part(L, pairs):
                for j in range(pairs):
                    act.wait_ge(gated, 4 * L + j + 1)
                    copy(hid_hi[:, 2 * j:2 * j + 2, :], hid[:, 2 * j:2 * j + 2, :]).then_inc(hid_rounded, 1)

            def wa_part(g):
                act.wait_ge(wa_full, g + 1)
                w = slice(0, 2 * H) if g == 0 else slice(2 * H, A2)
                copy(wa[:, :, w], bank[4 + g][:, 0:C * A2].rearrange("p (c n) -> p c n", c=C)[:, :, w]).then_inc(wa_read, 1)

            hi(0, 2)
            xT_part(0, (0, 1))
            hi(2, 6)
            mix_exps(0)
            hi(6, 8)
            mix_q(0)
            hi(8, 10)
            mix_v(0, (6, 7))
            hi(10, 12)
            for t in range(T):
                act.wait_ge(hr_ready, t + 1)
                copy(cur_hi[:, 0, t, :], hr[:, t, :]).then_inc(cur_rounded, 1)
            hi(12, 14)
            for t in range(T):
                act.wait_ge(ek_full, t + 1)
                copy(ek[:, t, :], bank[4 + t][:, :]).then_inc(ek_ready, 1)
            for j in range(2):
                act.wait_ge(qT_full, j + 1)
                copy(qT[:, 2 * j:2 * j + 2, :], bank[j][:, :].rearrange("p (c n) -> p c n", c=2)).then_inc(qT_ready, 1)
            for t in range(T):
                act.wait_ge(count_full, 1)
                copy(count[:, t, :], half(2 + t, 0)).then_inc(count_ready, 1)
            act.wait_ge(linked_ready, 2)
            copy(countT[:, :, :], bank[7][:, :].rearrange("p (c n) -> p c n", c=T)).then_inc(countT_ready, 1)
            yT_part(0, (4, 5))
            act.wait_ge(degree_ready, 1)
            diffuse(0, (2, 3))
            hi(14, 16)
            diffuse(1, (6, 7))
            wa_part(0)
            wa_part(1)
            xT_part(1, (4, 5))
            gate_exp(0)
            act.wait_ge(wa_full, 2)
            for m in range(8):
                act.wait_ge(up_full, m // 2 + 1)
                nc.scalar.activation(hid[:, m, :], half(m // 2, m % 2), ACT.Relu).then_inc(up_ready, 1)
            hi(16, 18)
            gateT_part(0, 6)
            hid_part(0, 4)
            hi(18, 20)

            hi(20, 24)
            xT_part(2, (2, 3))
            act.wait_ge(al_full, 1)
            copy(al[:, :, :], bank[4][:, 0:T * 2 * H].rearrange("p (t n) -> p t n", t=T)).then_inc(al_ready, 1)
            act.wait_ge(alT_full, 1)
            copy(alT_hi[:, :, :], bank[5][0:H, :].rearrange("p (a n) -> p a n", a=2)).then_inc(alT_rounded, 1)
            for t in range(T):
                act.wait_ge(hx_full, t + 1)
                copy(hx[:, t, :, 0:HD], bank[2 + t][:, :].rearrange("p (h n) -> p h n", h=H)).then_inc(hx_ready, 1)
            hi(24, 26)
            mix_exps(1)
            hi(26, 28)
            PAIR = (0, 1, 6, 7)
            act.wait_ge(al_ready, 1)
            act.wait_ge(hid_ready, 4)
            act.wait_ge(wa_full, 2)
            for j in range(4):
                act.wait_ge(dst_full, j + 1)
                for s in range(T):
                    for h in range(2):
                        hh = 2 * j + h
                        nc.scalar.activation(logit[:, s, hh, :], half(PAIR[j], h), ACT.Identity,
                                             bias=al[:, s, hh:hh + 1]).then_inc(z_ready, 1)
                if j == 1:
                    act.wait_ge(mT_full, 1)
                    copy(mT_hi[:, :], bank[4][0:H, 0:N]).then_inc(mT_rounded, 1)
            mix_q(1)
            mix_v(1, (5, 4))
            for t in range(T):
                act.wait_ge(ek_full, 2 + t + 1)
                copy(ek[:, t, :], bank[2 + t][:, :]).then_inc(ek_ready, 1)
            for j in range(4):
                for s in range(T):
                    act.wait_ge(shifted, 2 * j + s + 1)
                    nc.scalar.activation(logit[:, s, 2 * j:2 * j + 2, :], logit[:, s, 2 * j:2 * j + 2, :],
                                         ACT.Exp).then_inc(exp_ready, 1)
                if j == 1:
                    hi(28, 30)
                    for i in range(2):
                        act.wait_ge(qT_full, 2 + i + 1)
                        copy(qT[:, 2 * i:2 * i + 2, :], bank[4 + i][:, :].rearrange("p (c n) -> p c n", c=2))\
                            .then_inc(qT_ready, 1)
            hi(30, 32)
            yT_part(1, (5, 2))
            elu(0)
            hi(32, 34)
            xT_part(3, (0, 1))
            act.wait_ge(al_full, 2)
            copy(al[:, :, 0:2], bank[6][:, 0:2 * T].rearrange("p (t n) -> p t n", t=T)).then_inc(al_ready, 1)
            act.wait_ge(alT_full, 2)
            copy(alT_hi[0:1, :, :], bank[7][0:1, :].rearrange("p (a n) -> p a n", a=2)).then_inc(alT_rounded, 1)
            act.wait_ge(al_ready, 2)
            act.wait_ge(src_full, 5)
            for s in range(T):
                nc.scalar.activation(logit[:, s, 0, :], half(6, 0), ACT.Identity,
                                     bias=al[:, s, 0:1]).then_inc(z_ready, 1)
            act.wait_ge(mT_full, 2)
            copy(mT_hi[0:1, :], bank[5][0:1, 0:N]).then_inc(mT_rounded, 1)
            for t in range(T):
                act.wait_ge(hx_full, 2 + t + 1)
                copy(h2[:, t, :], bank[3 + t][:, :]).then_inc(hx_ready, 1)
            for s in range(T):
                act.wait_ge(shifted, 8 + s + 1)
                nc.scalar.activation(logit[:, s, 0, :], logit[:, s, 0, :], ACT.Exp).then_inc(exp_ready, 1)
            elu(1)
            xT_part(4, (3, 4))
            gate_exp(1)
            act.wait_ge(gexp_ready, 2)
            for m in range(C):
                act.wait_ge(up_full, 4 + m // 2 + 1)
                nc.scalar.activation(hid[:, m, :], half(m // 2, m % 2), ACT.Gelu, bias=b_up1[:, m:m + 1])\
                    .then_inc(up_ready, 1)
            gateT_part(1, 7)
            hid_part(1, 2)

        @block.vector
        def _(dve):
            n = [0]
            V = nc.vector

            def go(ins):
                n[0] += 1
                ins.then_inc(dve_step, 1)
                return ins

            def settle():
                dve.wait_ge(dve_step, n[0])

            def variance(i, t, src):
                go(V.bn_stats(stats[:, t, :], src))
                settle()
                go(V.bn_aggr(mv[:, t, :], stats[:, t, :]))
                settle()
                if i:
                    dve.wait_ge(rstd_ready, T * (i - 1) + t + 1)
                V.tensor_scalar(veps[:, t:t + 1], mv[:, t, 1:2], EPS, None, ALU.add).then_inc(var_ready, 1)

            def norm_rows(i, dst, src, t, s=None):
                dve.wait_ge(rstd_ready, T * i + t + 1)
                ins = V.tensor_scalar(dst, src, mv[:, t, 0:1], rstd[:, t:t + 1], ALU.subtract, ALU.mult)
                return ins.then_inc(s, 1) if s else go(ins)

            def xT_part(i, banks):
                for t in range(T):
                    dve.wait_ge(xT_rounded, T * i + t + 1)
                    cols = slice(t * P, (t + 1) * P)
                    V.tensor_tensor(xT_lo[:, :, cols], bank[banks[t]][:, :].rearrange("p (c n) -> p c n", c=C),
                                    xT_hi[:, :, cols].bitcast(f32), ALU.subtract).then_inc(xT_ready, 1)

            def yT_part(L, banks):
                for j in range(2):
                    dve.wait_ge(yT_rounded, 2 * L + j + 1)
                    V.tensor_tensor(yT_lo[:, 2 * j:2 * j + 2, :],
                                    bank[banks[j]][:, :].rearrange("p (c n) -> p c n", c=2),
                                    yT_hi[:, 2 * j:2 * j + 2, :].bitcast(f32), ALU.subtract).then_inc(yT_ready, 1)

            def small_split(hi, lo, src):
                go(V.tensor_copy(hi, src))
                settle()
                V.tensor_tensor(lo, src, hi.bitcast(f32), ALU.subtract).then_inc(narrow_ready, 1)

            def k_max(L):
                for j in range(2):
                    dve.wait_ge(k_full, 2 * L + j + 1)
                    V.tensor_reduce(kmax[:, 2 * j:2 * j + 2], bank[4 + j][:, :].rearrange("p (c n) -> p c n", c=2),
                                    AX.X, ALU.max, negate=True).then_inc(kmax_ready, 1)

            def bc(a, shape):
                return a.unsqueeze(len(a.shape)).broadcast_to(shape)

            def q_shift(L, banks):
                for t in range(T):
                    dve.wait_ge(q_full, 2 * L + t + 1)
                    src = bank[banks[t]][:, :].rearrange("p (h n) -> p h n", h=H)
                    go(V.tensor_reduce(qmax[:, t, :], src, AX.X, ALU.max))
                    settle()
                    V.tensor_tensor(q[:, t, :].rearrange("p (h n) -> p h n", h=H), src,
                                    bc(qmax[:, t, :], [P, H, HD]), ALU.subtract).then_inc(q_shifted, 1)

            def q_norm(L):
                for t in range(T):
                    dve.wait_ge(q_exp, 2 * L + t + 1)
                    qh = q[:, t, :].rearrange("p (h n) -> p h n", h=H)
                    go(V.tensor_reduce(qsum[:, t, :], qh, AX.X, ALU.add))
                    settle()
                    go(V.reciprocal(qsum[:, t, :], qsum[:, t, :]))
                    settle()
                    if L == 0:
                        go(V.tensor_scalar(qsum[:, t, :], qsum[:, t, :], float(HD) ** -0.5, None, ALU.mult))
                        settle()
                    V.tensor_tensor(qh, qh, bc(qsum[:, t, :], [P, H, HD]), ALU.mult).then_inc(q_ready, 1)

            def context(L, b):
                dve.wait_ge(ekT_ready, 4 * L + 4)
                go(V.reciprocal(kinv[:, :], ksum[:, :]))
                settle()
                dve.wait_ge(ctx_full, L + 1)
                if L == 0:
                    dve.wait_ge(consts, 1)
                for r in range(2):
                    p0, p1 = r * HD, (r + 1) * HD
                    src = bank[b][p0:p1, :].rearrange("p (m n) -> p m n", m=C)[:, :, p0:p1]
                    V.tensor_tensor(ctxbd[p0:p1, :, p0:p1], src, bc(kinv[p0:p1, :], [HD, C, HD]), ALU.mult)\
                        .then_inc(ctx_ready, 1)

            def gates(L, b, pb):
                E = EXPERTS[L]
                dve.wait_ge(logits_full, L + 1)
                src = bank[b][:, 0:T * E].rearrange("p (t e) -> p t e", t=T)
                lgE, pE = lg[:, :, 0:E], prob[:, :, 0:E]
                if L:
                    go(V.tensor_tensor(lgE, src, b_router[:, :].unsqueeze(1).broadcast_to([P, T, E]), ALU.add))
                else:
                    go(V.tensor_copy(lgE, src))
                settle()
                go(V.tensor_reduce(gsm[:, 0, :], lgE, AX.X, ALU.max))
                settle()
                V.tensor_tensor(lgE, lgE, bc(gsm[:, 0, :], [P, T, E]), ALU.subtract).then_inc(shift_ready, 1)
                dve.wait_ge(gexp_ready, L + 1)
                go(V.tensor_reduce(gsm[:, 1, :], pE, AX.X, ALU.add))
                settle()
                go(V.reciprocal(gsm[:, 1, :], gsm[:, 1, :]))
                settle()
                go(V.tensor_tensor(pE, pE, bc(gsm[:, 1, :], [P, T, E]), ALU.mult))
                settle()
                for t in range(T):
                    go(V.max(top[:, 0, t, :], prob[:, t, 0:E]))
                settle()
                for t in range(T):
                    go(V.max_index(top_i[:, 0, t, :], top[:, 0, t, :], prob[:, t, 0:E]))
                settle()
                go(V.tensor_copy(top_f[:, 0, :], top_i[:, 0, :, 0]))
                if L:
                    go(V.tensor_copy(top_f[:, 1, :], top_i[:, 0, :, 1]))
                settle()
                io = iota_f[:, 0:E].unsqueeze(1).broadcast_to([P, T, E])
                m1, m2 = mask[:, :, 0:E], mask[:, :, E:2 * E]
                go(V.tensor_tensor(m1, io, bc(top_f[:, 0, :], [P, T, E]), ALU.is_equal))
                if L == 0:
                    settle()
                    go(V.tensor_scalar(prob2[:, :, :], m1, -1.0, 1.0, ALU.mult, ALU.add))
                    settle()
                    go(V.tensor_tensor(prob2[:, :, :], prob2[:, :, :], pE, ALU.mult))
                    settle()
                    for t in range(T):
                        go(V.max(top[:, 1, t, :], prob2[:, t, :]))
                    settle()
                    for t in range(T):
                        go(V.max_index(top_i[:, 1, t, :], top[:, 1, t, :], prob2[:, t, :]))
                    settle()
                    go(V.tensor_copy(top_f[:, 1, :], top_i[:, 1, :, 0]))
                    settle()
                    v2 = top[:, 1, :, 0]
                else:
                    v2 = top[:, 0, :, 1]
                v1 = top[:, 0, :, 0]
                V.tensor_tensor(m2, io, bc(top_f[:, 1, :], [P, T, E]), ALU.is_equal).then_inc(masks_ready, 1)
                go(V.tensor_tensor(gsm[:, 2, :], v1, v2, ALU.add))
                settle()
                go(V.tensor_scalar(gsm[:, 2, :], gsm[:, 2, :], GATE_EPS, None, ALU.add))
                settle()
                go(V.reciprocal(gsm[:, 2, :], gsm[:, 2, :]))
                settle()
                go(V.tensor_tensor(gsm[:, 3, :], v1, gsm[:, 2, :], ALU.mult))
                go(V.tensor_tensor(gsm[:, 4, :], v2, gsm[:, 2, :], ALU.mult))
                dve.wait_ge(masks_ready, L + 1)
                dve.wait_ge(pos_full, L + 1)
                pos = bank[pb][:, 0:T * 2 * E].rearrange("p (t e) -> p t e", t=T)
                total = bank[pb][:, T * 2 * E:T * 2 * E + E]
                k1, k2 = kept[:, :, 0:E], kept[:, :, E:2 * E]
                if L == 0:
                    go(V.tensor_scalar(poss[:, 0, 0:E], total, float(CAP0), None, ALU.min))
                    go(V.scalar_tensor_tensor(k1, pos[:, :, 0:E], float(CAP0), m1, ALU.is_lt, ALU.mult))
                    settle()
                    go(V.tensor_tensor(poss[:, :, E:2 * E], pos[:, :, E:2 * E],
                                       poss[:, 0:1, 0:E].broadcast_to([P, T, E]), ALU.add))
                    settle()
                    go(V.scalar_tensor_tensor(k2, poss[:, :, E:2 * E], float(CAP0), m2, ALU.is_lt, ALU.mult))
                    settle()
                else:
                    go(V.tensor_copy(poss[:, :, E:2 * E], pos[:, :, E:2 * E]))
                    settle()
                    go(V.tensor_tensor(poss[:, :, 0:E], pos[:, :, 0:E], poss[:, :, E:2 * E], ALU.add))
                    settle()
                    go(V.scalar_tensor_tensor(k1, poss[:, :, 0:E], float(CAP1), m1, ALU.is_lt, ALU.mult))
                    go(V.scalar_tensor_tensor(k2, poss[:, :, 0:E], float(CAP1), m2, ALU.is_lt, ALU.mult))
                    settle()
                    go(V.tensor_reduce(gsm[:, 5, :], k1, AX.X, ALU.add))
                    go(V.tensor_reduce(gsm[:, 6, :], k2, AX.X, ALU.add))
                    settle()
                    go(V.tensor_tensor(gsm[:, 3, :], gsm[:, 3, :], gsm[:, 5, :], ALU.mult))
                    go(V.tensor_tensor(gsm[:, 4, :], gsm[:, 4, :], gsm[:, 6, :], ALU.mult))
                    settle()
                    go(V.tensor_tensor(gsm[:, 7, :], gsm[:, 3, :], gsm[:, 4, :], ALU.add))
                    settle()
                    go(V.tensor_scalar(gsm[:, 7, :], gsm[:, 7, :], GATE_EPS, None, ALU.add))
                    settle()
                    go(V.reciprocal(gsm[:, 7, :], gsm[:, 7, :]))
                    settle()
                    go(V.tensor_tensor(gsm[:, 3, :], gsm[:, 3, :], gsm[:, 7, :], ALU.mult))
                    go(V.tensor_tensor(gsm[:, 4, :], gsm[:, 4, :], gsm[:, 7, :], ALU.mult))
                    settle()
                go(V.tensor_tensor(k1, k1, bc(gsm[:, 3, :], [P, T, E]), ALU.mult))
                go(V.tensor_tensor(k2, k2, bc(gsm[:, 4, :], [P, T, E]), ALU.mult))
                settle()
                V.tensor_tensor(gate[:, :, 0:E], k1, k2, ALU.add).then_inc(gate_ready, 1)

            def gateT_part(L, b):
                E = EXPERTS[L]
                dve.wait_ge(gateT_rounded, L + 1)
                V.tensor_tensor(gateT_lo[0:E, :], bank[b][0:E, 0:N], gateT_hi[0:E, :].bitcast(f32), ALU.subtract)\
                    .then_inc(gateT_ready, 1)

            def gate_hidden(L, banks):
                pairs = 4 if L == 0 else 2

                def lo(j):
                    dve.wait_ge(hid_rounded, 4 * L + j + 1)
                    two = slice(2 * j, 2 * j + 2)
                    V.tensor_tensor(hid_lo[:, two, :], hid[:, two, :], hid_hi[:, two, :].bitcast(f32), ALU.subtract)\
                        .then_inc(hid_ready, 1)

                for j in range(pairs):
                    dve.wait_ge(up_ready, 8 * L + 2 * j + 2)
                    dve.wait_ge(spread_full, 4 * L + j + 1)
                    two = slice(2 * j, 2 * j + 2)
                    V.tensor_tensor(hid[:, two, :], hid[:, two, :],
                                    bank[banks[j]][:, :].rearrange("p (c n) -> p c n", c=2), ALU.mult)\
                        .then_inc(gated, 1)
                    if j:
                        lo(j - 1)
                lo(pairs - 1)

            for t in range(T):
                dve.wait_ge(x_in, 16 * T)
                variance(0, t, xa[:, t, :])
            for t in range(T):
                norm_rows(0, xn[:, t, :], xa[:, t, :], t, xn_ready)
            dve.wait_ge(iota_ready, 1)
            go(V.tensor_copy(iota_bf[:, :], iota_i[:, :]))
            go(V.tensor_copy(iota_f[:, :], iota_i[:, 0:E0]))
            xT_part(0, (0, 1))
            dve.wait_ge(edges_in, 32)
            go(V.tensor_copy(edges[:, :, :], edges_i[:, :, :]))
            settle()

            def onehots(j0, j1):
                for j in range(j0, j1):
                    if j >= RING:
                        dve.wait_ge(onehot_used, j - RING + 1)
                    for a in range(2):
                        ins = V.tensor_scalar(onehot[:, j % RING, a, :], iota_bf[:, :], edges[:, a, j:j + 1], None,
                                              ALU.is_equal)
                    ins.then_inc(onehot_ready, 1)

            onehots(0, 16)
            k_max(0)
            onehots(16, 32)
            q_shift(0, (0, 1))
            onehots(32, 48)
            q_norm(0)
            dve.wait_ge(small_in, SMALLS)
            for t in range(T):
                dve.wait_ge(h_full, t + 1)
                V.tensor_tensor(hr[:, t, :], bank[t][:, :], row["b_gnn0"], ALU.add).then_inc(hr_ready, 1)
            onehots(48, 64)
            for t in range(T):
                dve.wait_ge(cur_rounded, t + 1)
                V.tensor_tensor(cur_lo[:, 0, t, :], hr[:, t, :], cur_hi[:, 0, t, :].bitcast(f32), ALU.subtract)\
                    .then_inc(cur_ready, 1)
                go(V.tensor_scalar(diffused[:, t, :], hr[:, t, :], diffusion[:, 0:1], None, ALU.mult))
            context(0, 6)
            dve.wait_ge(count_ready, 2)
            go(V.tensor_scalar(far[:, :, :], count[:, :, :], 1.0, None, ALU.min))
            settle()
            dve.wait_ge(countT_full, 1)
            go(V.scalar_tensor_tensor(linked[:, :, :], bank[7][:, :].rearrange("p (c n) -> p c n", c=T), 1.0,
                                      far[:, :, :], ALU.min, ALU.max))
            settle()
            for t in range(T):
                sl = linked[:, t, t * P:(t + 1) * P]
                V.tensor_tensor(sl, sl.bitcast(f32), ident[:, :], ALU.add).then_inc(linked_ready, 1)
            dve.wait_ge(linked_ready, 2)
            go(V.tensor_reduce(degree[:, :], linked[:, :, :].bitcast(f32), AX.X, ALU.add))
            settle()
            go(V.tensor_scalar(degree[:, :], degree[:, :], 1.0, None, ALU.max))
            settle()
            V.reciprocal(degree[:, :], degree[:, :]).then_inc(degree_ready, 1)
            dve.wait_ge(degree_ready, 1)
            small_split(narrow_hi[:, 0, :, :], narrow_lo[:, 0, :, :], w_gate[:, :, :])
            for i in range(STEPS):
                go(V.tensor_scalar(degree_w[:, i, :], degree[:, :], diffusion[:, i + 1:i + 2], None, ALU.mult))
            yT_part(0, (4, 5))
            STEPB = ((2, 3), (6, 7), (2, 3))

            def diffuse(i):
                settle()
                for t in range(T):
                    src = bank[STEPB[i][t]][:, :]
                    if i < STEPS - 1:
                        dve.wait_ge(cur_rounded, T * (i + 1) + t + 1)
                        V.scalar_tensor_tensor(cur_lo[:, (i + 1) % 2, t, :], src, degree[:, t:t + 1],
                                               cur_hi[:, (i + 1) % 2, t, :].bitcast(f32), ALU.mult, ALU.subtract)\
                            .then_inc(cur_ready, 1)
                for t in range(T):
                    src = bank[STEPB[i][t]][:, :]
                    dve.wait_ge(step_full, T * i + t + 1)
                    V.scalar_tensor_tensor(diffused[:, t, :], src, degree_w[:, i, t:t + 1], diffused[:, t, :],
                                           ALU.mult, ALU.add).then_inc(step_read, 1)

            diffuse(0)
            small_split(narrow_hi[:, 1, :, 0:EXPERTS[1]], narrow_lo[:, 1, :, 0:EXPERTS[1]], w_router[:, :, :])
            small_split(b_down_hi[:, :], b_down_lo[:, :], b_down1[:, :])
            dve.wait_ge(countT_ready, 1)
            for t in range(T):
                for m in (count, countT):
                    sl = m[:, t, t * P:(t + 1) * P]
                    go(V.tensor_tensor(sl, sl, ident[:, :], ALU.add))
            settle()
            go(V.tensor_scalar(far[:, :, :], count[:, :, :], 0.0, -FAR, ALU.is_equal, ALU.mult))
            for t in range(T):
                dve.wait_ge(o_full, t + 1)
                variance(1, t, bank[t][:, :])
            dve.wait_ge(step_read, 2)
            diffuse(1)
            for t in range(T):
                norm_rows(1, mixed[:, t, :], bank[t][:, :], t, mix_ready)
            dve.wait_ge(mix_ready, 2)
            for t in range(T):
                go(V.tensor_tensor(mixed[:, t, :], mixed[:, t, :], row["gamma0"], ALU.mult))
            settle()
            go(V.tensor_tensor(mixed[:, :, :], mixed[:, :, :], xa[:, :, :], ALU.add))
            dve.wait_ge(step_read, 4)
            diffuse(2)
            settle()
            for t in range(T):
                dve.wait_ge(step_read, 4 + t + 1)
                go(V.scalar_tensor_tensor(xb[:, t, :], diffused[:, t, :], 0.0, mixed[:, t, :], ALU.max, ALU.add))
                settle()
                variance(2, t, xb[:, t, :])
            dve.wait_ge(xT_full, 2)
            for t in range(T):
                norm_rows(2, xn[:, t, :], xb[:, t, :], t, xn_ready)
            for g in range(2):
                w = slice(0, 2 * H) if g == 0 else slice(2 * H, A2)
                dve.wait_ge(wa_read, g + 1)
                go(V.tensor_copy(wa_hi[:, :, w], wa[:, :, w]))
                settle()
                V.tensor_tensor(wa_lo[:, :, w], wa[:, :, w], wa_hi[:, :, w].bitcast(f32), ALU.subtract)\
                    .then_inc(wa_ready, 1)
            xT_part(1, (4, 5))
            gates(0, 6, 7)
            gateT_part(0, 6)
            gate_hidden(0, (4, 5, 7, 6))
            dve.wait_ge(xT_full, 4)
            for t in range(T):
                dve.wait_ge(down_full, t + 1)
                go(V.tensor_tensor(xa[:, t, :], bank[t][:, :], xb[:, t, :], ALU.add))
                settle()
                variance(3, t, xa[:, t, :])
                norm_rows(3, xn[:, t, :], xa[:, t, :], t, xn_ready)

            xT_part(2, (2, 3))
            dve.wait_ge(alT_rounded, 1)
            V.tensor_tensor(alT_lo[:, :, :], bank[5][0:H, :].rearrange("p (a n) -> p a n", a=2),
                            alT_hi[:, :, :].bitcast(f32), ALU.subtract).then_inc(alT_ready, 1)
            PAIR = (0, 1, 6, 7)
            for j in range(4):
                dve.wait_ge(src_full, j + 1)
                settle()
                if j:
                    dve.wait_ge(max_ready, j)
                for h in range(2):
                    for t in range(T):
                        if h or t:
                            go(ins)
                        ins = V.tensor_tensor_reduce(out=junk[:, 2 * h + t, :], in0=half(PAIR[j], h), in1=far[:, t, :],
                                                     scale=1.0, scalar=-BIG, op0=ALU.add, op1=ALU.max,
                                                     accum_out=mx[:, t, 2 * j + h:2 * j + h + 1])
                ins.then_inc(max_ready, 1)
            dve.wait_ge(max_ready, 4)
            dve.wait_ge(al_ready, 1)
            go(V.tensor_tensor(mx[:, :, :], mx[:, :, :], al[:, :, H:2 * H], ALU.add))
            settle()
            V.scalar_tensor_tensor(mz[:, :, :], mx[:, :, :], SLOPE, mx[:, :, :], ALU.mult, ALU.max)\
                .then_inc(max_ready, 1)
            k_max(1)

            def leaky(j):
                dve.wait_ge(z_ready, 4 * j + 4)
                for s in range(T):
                    z = logit[:, s, 2 * j:2 * j + 2, :]
                    go(V.scalar_tensor_tensor(z, z, SLOPE, z, ALU.mult, ALU.max))

            def less_max(j):
                dve.wait_ge(max_full, j + 1)
                for s in range(T):
                    z = logit[:, s, 2 * j:2 * j + 2, :]
                    V.tensor_tensor(z, z, bank[PAIR[j]][:, :].rearrange("p (h n) -> p h n", h=2), ALU.subtract)\
                        .then_inc(shifted, 1)

            def edge_weights(j):
                for s in range(T):
                    dve.wait_ge(exp_ready, 2 * j + s + 1)
                    z = logit[:, s, 2 * j:2 * j + 2, :]
                    V.scalar_tensor_tensor(z, z, BIG, countT[:, s:s + 1, :].broadcast_to([P, 2, N]), ALU.min, ALU.mult)\
                        .then_inc(weight_ready, 1)

            leaky(0)
            leaky(1)
            dve.wait_ge(mT_rounded, 1)
            V.tensor_tensor(mT_lo[:, :], bank[4][0:H, 0:N], mT_hi[:, :].bitcast(f32), ALU.subtract)\
                .then_inc(mT_ready, 1)
            q_shift(1, (2, 3))
            leaky(2)
            leaky(3)
            settle()
            less_max(0)
            less_max(1)
            q_norm(1)
            edge_weights(0)
            edge_weights(1)
            less_max(2)
            less_max(3)
            context(1, 3)
            edge_weights(2)
            edge_weights(3)
            yT_part(1, (5, 2))

            def gat_norm(g, i, t):
                gg, beta = (("g1", "beta1"), ("g2", "beta2"))[g]
                y = g_a[:, t, :]
                settle()
                variance(i, t, y)
                go(V.scalar_tensor_tensor(y, y, mv[:, t, 0:1], row[gg], ALU.subtract, ALU.mult))
                settle()
                dve.wait_ge(rstd_ready, T * i + t + 1)
                V.scalar_tensor_tensor(y, y, rstd[:, t:t + 1], row[beta], ALU.mult, ALU.add).then_inc(y_ready, 1)

            def elu(g, t, dst, base, s=None):
                y = g_a[:, t, :]
                dve.wait_ge(y_ready, T * g + t + 1)
                go(V.scalar_tensor_tensor(base, y, 0.0, base, ALU.max, ALU.add))
                settle()
                dve.wait_ge(elu_exp, T * g + t + 1)
                ins = V.scalar_tensor_tensor(dst, g_b[:, t, :], 1.0, base, ALU.min, ALU.add)
                return ins.then_inc(s, 1) if s else go(ins)

            AGG = ((0, 6), (1, 7))
            for u in range(2):
                for t in range(T):
                    dve.wait_ge(agg_full, 2 * u + t + 1)
                    src = bank[AGG[t][u]][:, 0:4 * (HD + 1)].rearrange("p (h n) -> p h n", h=4)
                    go(V.reciprocal(mx[:, t, 4 * u:4 * u + 4], src[:, :, HD]))
                    settle()
                    dst = g_a[:, t, 4 * u * HD:4 * (u + 1) * HD].rearrange("p (h n) -> p h n", h=4)
                    V.tensor_tensor(dst, src[:, :, 0:HD], bc(mx[:, t, 4 * u:4 * u + 4], [P, 4, HD]), ALU.mult)\
                        .then_inc(agg_ready, 1)
                    dve.wait_ge(agg_ready, 2 * u + t + 1)
                    row_b1 = row["b1"][:, 4 * u * HD:4 * (u + 1) * HD].rearrange("p (h n) -> p h n", h=4)
                    go(V.tensor_tensor(dst, dst, row_b1, ALU.add))
            for t in range(T):
                gat_norm(0, 4, t)
            dve.wait_ge(qT_full, 4)
            dve.wait_ge(xn_less_one, 1)
            for t in range(T):
                elu(0, t, x1g[:, t, :], xn[:, t, :], xn_ready)
            for t in range(T):
                dve.wait_ge(o_full, 2 + t + 1)
                V.tensor_tensor(mixed[:, t, :], bank[3 + t][:, :], row["b_out1"], ALU.add).then_inc(mix_ready, 1)
            xT_part(3, (0, 1))
            dve.wait_ge(alT_rounded, 2)
            V.tensor_tensor(alT_lo[0:1, :, :], bank[7][0:1, :].rearrange("p (a n) -> p a n", a=2),
                            alT_hi[0:1, :, :].bitcast(f32), ALU.subtract).then_inc(alT_ready, 1)
            dve.wait_ge(src_full, 5)
            for t in range(T):
                go(V.tensor_tensor_reduce(out=junk[:, t, :], in0=half(2, 0), in1=far[:, t, :], scale=1.0, scalar=-BIG,
                                          op0=ALU.add, op1=ALU.max, accum_out=mx[:, t, 0:1]))
            dve.wait_ge(al_ready, 2)
            settle()
            go(V.tensor_tensor(mx[:, :, 0:1], mx[:, :, 0:1], al[:, :, 1:2], ALU.add))
            settle()
            V.scalar_tensor_tensor(mz[:, :, 0:1], mx[:, :, 0:1], SLOPE, mx[:, :, 0:1], ALU.mult, ALU.max)\
                .then_inc(max_ready, 1)
            dve.wait_ge(z_ready, 18)
            z = logit[:, :, 0, :]
            go(V.scalar_tensor_tensor(z, z, SLOPE, z, ALU.mult, ALU.max))
            settle()
            dve.wait_ge(mT_rounded, 2)
            V.tensor_tensor(mT_lo[0:1, :], bank[5][0:1, 0:N], mT_hi[0:1, :].bitcast(f32), ALU.subtract)\
                .then_inc(mT_ready, 1)
            dve.wait_ge(max_full, 5)
            for s in range(T):
                V.tensor_tensor(logit[:, s, 0, :], logit[:, s, 0, :], half(7, 0), ALU.subtract).then_inc(shifted, 1)
            for s in range(T):
                dve.wait_ge(exp_ready, 8 + s + 1)
                V.scalar_tensor_tensor(logit[:, s, 0, :], logit[:, s, 0, :], BIG, countT[:, s, :], ALU.min, ALU.mult)\
                    .then_inc(weight_ready, 1)
            dve.wait_ge(mix_ready, 4)
            go(V.tensor_tensor(mixed[:, :, :], mixed[:, :, :], xa[:, :, :], ALU.add))
            settle()
            go(V.scalar_tensor_tensor(mixed[:, :, :], x1g[:, :, :], -1.0, mixed[:, :, :], ALU.add, ALU.add))
            for t in range(T):
                dve.wait_ge(agg_full, 4 + t + 1)
                go(V.reciprocal(mx[:, t, 1:2], bank[(2, 5)[t]][:, 0:1]))
                settle()
                go(V.scalar_tensor_tensor(g_a[:, t, :], bank[t][:, :], mx[:, t, 1:2], row["b2"], ALU.mult, ALU.add))
            for t in range(T):
                gat_norm(1, 5, t)
            for t in range(T):
                elu(1, t, xb[:, t, :], mixed[:, t, :])
                settle()
                variance(6, t, xb[:, t, :])
            for t in range(T):
                norm_rows(6, xn[:, t, :], xb[:, t, :], t, xn_ready)
            xT_part(4, (3, 4))
            gates(1, 5, 6)
            gateT_part(1, 7)
            gate_hidden(1, (2, 5))
            for t in range(T):
                dve.wait_ge(down_full, 2 + t + 1)
                V.tensor_tensor(xa[:, t, :], bank[3 + t][:, :], xb[:, t, :], ALU.add).then_inc(out_ready, 1)

        @block.tensor
        def _(pe):
            mm = nc.tensor.matmul

            def product(dst, lhs, rhs, k):
                for c in range(k):
                    ins = mm(dst, lhs(c), rhs(c), start=c == 0, stop=c == k - 1)
                return ins

            def split_product(dst, lhs, rhs, k, waits=None):
                for c in range(k):
                    (l_hi, l_lo), (r_hi, r_lo) = lhs(c), rhs(c)
                    mm(dst, l_hi, r_hi, start=c == 0, stop=False)
                    mm(dst, l_hi, r_lo, start=False, stop=False)
                    ins = mm(dst, l_lo, r_hi, start=False, stop=c == k - 1)
                return ins

            def xT_at(c, t=None):
                cols = slice(0, N) if t is None else slice(t * P, (t + 1) * P)
                return xT_hi[:, c, cols], xT_lo[:, c, cols]

            def weights_in(w):
                pe.wait_ge(lo_ready, w.first + w.units)

            def xT_made(i, src, banks, after=()):
                for t in range(T):
                    pe.wait_ge(xn_ready, T * i + t + 1)
                    for s, nn in after:
                        pe.wait_ge(s, nn)
                    for c in range(C):
                        ins = nc.tensor.transpose(bank[banks[t]][:, c * P:(c + 1) * P], src[:, t, c * P:(c + 1) * P],
                                                  ident[:, :])
                    ins.then_inc(xT_full, 1)

            def rows_of(name, banks, full, i, read=lambda t: None):
                w = Weight(name)
                weights_in(w)
                for t in range(T):
                    pe.wait_ge(xT_ready, T * i + t + 1)
                    if read(t):
                        pe.wait_ge(*read(t))
                    split_product(bank[banks[t]][:, :], lambda c: xT_at(c, t), w.at, C).then_inc(full, 1)

            def k_of(name, full):
                w = Weight(name)
                weights_in(w)
                for m in range(C):
                    ins = split_product(half(4 + m // 2, m % 2), lambda c: w.at(c, m * P, (m + 1) * P), xT_at, C)
                    if m % 2:
                        ins.then_inc(full, 1)

            def ek_made(L, banks):
                for t in range(T):
                    for m in range(C):
                        ins = nc.tensor.transpose(bank[banks[t]][:, m * P:(m + 1) * P], ekT[:, m, t * P:(t + 1) * P],
                                                  ident[:, :])
                    ins.then_inc(ek_full, 1)

            def qT_made(banks):
                for j in range(2):
                    for m in (2 * j, 2 * j + 1):
                        for t in range(T):
                            o = (m % 2) * N + t * P
                            ins = nc.tensor.transpose(bank[banks[j]][:, o:o + P], q[:, t, m * P:(m + 1) * P],
                                                      ident[:, :])
                    ins.then_inc(qT_full, 1)

            def context(b):
                for m in range(C):
                    cols = slice(m * P, (m + 1) * P)
                    ins = product(bank[b][:, cols], lambda t: ek[:, t, cols], lambda t: v[:, t, cols], T)
                ins.then_inc(ctx_full, 1)

            def yT_made(L, banks):
                for m in range(C):
                    ins = mm(half(banks[m // 2], m % 2), ctxbd[:, m, :], qT[:, m, :], start=True, stop=True)
                    if m % 2:
                        ins.then_inc(yT_full, 1)

            def attn_out(name, banks):
                w = Weight(name)
                weights_in(w)
                for t in range(T):
                    cols = slice(t * P, (t + 1) * P)
                    split_product(bank[banks[t]][:, :], lambda m: (yT_hi[:, m, cols], yT_lo[:, m, cols]), w.at, C)\
                        .then_inc(o_full, 1)

            def selected(dst, selector, rows_hi, rows_lo):
                mm(dst, selector, rows_hi, start=True, stop=False)
                return mm(dst, selector, rows_lo, start=False, stop=True)

            def positions(L, b):
                E2 = 2 * EXPERTS[L]
                E = EXPERTS[L]
                pe.wait_ge(masks_ready, L + 1)
                mm(bank[b][:, 0:E2], before[:, :], mask[:, 0, 0:E2], start=True, stop=True)
                mm(bank[b][:, E2:2 * E2], ones[:, :], mask[:, 0, 0:E2], start=True, stop=False)
                mm(bank[b][:, E2:2 * E2], before[:, :], mask[:, 1, 0:E2], start=False, stop=True)
                mm(bank[b][:, 2 * E2:2 * E2 + E], ones[:, :], mask[:, 0, 0:E], start=True, stop=False)
                mm(bank[b][:, 2 * E2:2 * E2 + E], ones[:, :], mask[:, 1, 0:E], start=False, stop=True)\
                    .then_inc(pos_full, 1)

            def gate_rows(L, b):
                E = EXPERTS[L]
                pe.wait_ge(gate_ready, L + 1)
                for t in range(T):
                    ins = nc.tensor.transpose(bank[b][0:E, t * P:(t + 1) * P], gate[:, t, 0:E], ident[:, :])
                ins.then_inc(gateT_full, 1)

            def gate_spread(L, banks):
                E = EXPERTS[L]
                pe.wait_ge(gateT_ready, L + 1)
                for m in range(len(banks) * 2):
                    ins = selected(half(banks[m // 2], m % 2), spread[0:E, m, :, :].rearrange("p a f -> p (a f)"),
                                   gateT_hi[0:E, :], gateT_lo[0:E, :])
                    if m % 2:
                        ins.then_inc(spread_full, 1)

            def up(name, m0, m1):
                w = Weight(name)
                weights_in(w)
                for m in range(m0, m1):
                    ins = split_product(half(m // 2, m % 2), lambda c: w.at(c, m * P, (m + 1) * P), xT_at, C)
                    if m % 2:
                        ins.then_inc(up_full, 1)

            def down(name, t, dst, k, L, opened):
                w = Weight(name)
                cols = slice(t * P, (t + 1) * P)
                for m in range(k):
                    if t == 0:
                        pe.wait_ge(hid_ready, 4 * L + m // 2 + 1)
                        pe.wait_ge(lo_ready, w.first + m // 2 + 1)
                    h_hi, h_lo = hid_hi[:, m, cols], hid_lo[:, m, cols]
                    r_hi, r_lo = w.at(m)
                    mm(dst, h_hi, r_hi, start=m == 0 and not opened, stop=False)
                    mm(dst, h_hi, r_lo, start=False, stop=False)
                    ins = mm(dst, h_lo, r_hi, start=False, stop=m == k - 1)
                ins.then_inc(down_full, 1)

            def logits(b, L, i):
                E = EXPERTS[L]
                for t in range(T):
                    pe.wait_ge(xT_ready, T * i + t + 1)
                    ins = split_product(bank[b][:, t * E:(t + 1) * E], lambda c: xT_at(c, t),
                                        lambda c: (narrow_hi[:, L, c, 0:E], narrow_lo[:, L, c, 0:E]), C)
                ins.then_inc(logits_full, 1)

            def attention_weights(g):
                wt = w2t if g else w1t
                pe.wait_ge(w2t_in if g else w1t_in, 16)
                for kc in range(C):
                    o = kc * A2 + (2 * H if g else 0)
                    ins = product(bank[4 + g][:, o:o + (2 if g else 2 * H)], lambda m: wt[:, m, kc * P:(kc + 1) * P],
                                  (lambda m: att2[:, :, m]) if g else (lambda m: attblk[:, m, :]), C)
                ins.then_inc(wa_full, 1)

            pe.wait_ge(consts, 1)
            xT_made(0, xn, (0, 1))
            pe.wait_ge(xT_ready, 2)
            k_of("k0", k_full)

            def counts(j0, j1):
                for j in range(j0, j1):
                    pe.wait_ge(onehot_ready, j + 1)
                    for t in range(T):
                        ins = mm(half(COUNTB[t], 0), onehot[:, j % RING, 1, t * P:(t + 1) * P],
                                 onehot[:, j % RING, 0, :], start=j == 0, stop=j == ET - 1)
                    if j < ET - 1:
                        ins.then_inc(onehot_used, 1)
                return ins

            COUNTB = (2, 3)
            rows_of("q0", (0, 1), q_full, 0)
            counts(0, 16)
            rows_of("v0", (6, 7), v_full, 0)
            counts(16, 32)
            pe.wait_ge(q_shifted, 2)
            rows_of("gnn0", (0, 1), h_full, 0)
            counts(32, 48)
            pe.wait_ge(ekT_ready, 4)
            ek_made(0, (4, 5))
            pe.wait_ge(hr_ready, 2)
            pe.wait_ge(q_ready, 2)
            qT_made((0, 1))
            pe.wait_ge(v_ready, 2)
            pe.wait_ge(ek_ready, 2)
            context(6)
            counts(48, 64).then_inc(count_full, 1)
            pe.wait_ge(ctx_ready, 2)
            pe.wait_ge(qT_ready, 2)
            yT_made(0, (4, 5))
            pe.wait_ge(count_ready, 2)
            for s in range(T):
                for t in range(T):
                    ins = nc.tensor.transpose(bank[7][:, s * N + t * P:s * N + (t + 1) * P],
                                              count[:, t, s * P:(s + 1) * P], ident[:, :])
            ins.then_inc(countT_full, 1)

            def diffuse(i, banks):
                for t in range(T):
                    for s in range(T):
                        adj = linked[:, s, t * P:(t + 1) * P]
                        mm(bank[banks[t]][:, :], adj, cur_hi[:, i % 2, s, :], start=s == 0, stop=False)
                        ins = mm(bank[banks[t]][:, :], adj, cur_lo[:, i % 2, s, :], start=False, stop=s == T - 1)
                    ins.then_inc(step_full, 1)

            pe.wait_ge(linked_ready, 2)
            pe.wait_ge(cur_ready, 2)
            diffuse(0, (2, 3))
            pe.wait_ge(yT_ready, 2)
            attn_out("out0", (0, 1))
            pe.wait_ge(cur_ready, 4)
            diffuse(1, (6, 7))
            pe.wait_ge(consts, 2)
            attention_weights(0)
            pe.wait_ge(cur_ready, 6)
            pe.wait_ge(step_read, 2)
            diffuse(2, (2, 3))
            attention_weights(1)
            pe.wait_ge(wa_read, 2)
            xT_made(1, xn, (4, 5))
            pe.wait_ge(step_read, 4)
            pe.wait_ge(narrow_ready, 1)
            logits(6, 0, 1)
            pe.wait_ge(mix_ready, 2)
            pe.wait_ge(step_read, 6)
            up("up0", 0, 5)
            positions(0, 7)
            up("up0", 5, 7)
            gate_rows(0, 6)
            up("up0", 7, 8)
            gate_spread(0, (4, 5, 7, 6))
            for t in range(T):
                down("down0", t, bank[t][:, :], 8, 0, False)

            xT_made(2, xn, (2, 3))
            pe.wait_ge(wa_ready, 2)

            def node_terms(g, b, i):
                n2 = 2 if g else 2 * H
                w = slice(2 * H, A2) if g else slice(0, 2 * H)
                for t in range(T):
                    pe.wait_ge(xT_ready, T * i + t + 1)
                    ins = split_product(bank[b][:, t * n2:(t + 1) * n2], lambda c: xT_at(c, t),
                                        lambda c: (wa_hi[:, c, w], wa_lo[:, c, w]), C)
                ins.then_inc(al_full, 1)

            def node_rows(g, b):
                hh = 1 if g else H
                pe.wait_ge(al_ready, g + 1)
                for a in range(2):
                    for t in range(T):
                        ins = nc.tensor.transpose(bank[b][0:hh, a * N + t * P:a * N + (t + 1) * P],
                                                  al[:, t, a * hh:(a + 1) * hh], ident[:, :])
                ins.then_inc(alT_full, 1)

            node_terms(0, 4, 2)
            node_rows(0, 5)
            PAIR = (0, 1, 6, 7)

            def broadcast(rows_hi, rows_lo, full, read):
                for h in range(H):
                    if read and h % 2 == 0:
                        pe.wait_ge(*read(h // 2))
                    ins = selected(half(PAIR[h // 2], h % 2), pick[:, h, :], rows_hi, rows_lo)
                    if h % 2:
                        ins.then_inc(full, 1)

            pe.wait_ge(alT_ready, 1)
            pe.wait_ge(xn_ready, 6)
            broadcast(alT_hi[:, 0, :], alT_lo[:, 0, :], src_full, None)
            rows_of("gat1", (2, 3), hx_full, 2)
            k_of("k1", k_full)
            broadcast(alT_hi[:, 1, :], alT_lo[:, 1, :], dst_full, lambda j: (max_ready, j + 1))
            pe.wait_ge(hx_ready, 2)
            rows_of("q1", (2, 3), q_full, 2)
            pe.wait_ge(max_ready, 5)
            pe.wait_ge(ekT_ready, 8)
            for t in range(T):
                ins = nc.tensor.transpose(bank[4][0:H, t * P:(t + 1) * P], mz[:, t, :], ident[:, :])
            ins.then_inc(mT_full, 1)
            rows_of("v1", (5, 4), v_full, 2, lambda t: (mT_ready, 1) if t else None)
            broadcast(mT_hi[:, :], mT_lo[:, :], max_full, lambda j: (z_ready, 4 * j + 4))
            pe.wait_ge(q_shifted, 4)
            ek_made(1, (2, 3))
            pe.wait_ge(q_ready, 4)
            pe.wait_ge(v_ready, 4)
            qT_made((4, 5))
            pe.wait_ge(ek_ready, 4)
            context(3)
            AGG = ((0, 6), (1, 7))

            def aggregate(u):
                pe.wait_ge(weight_ready, 4 * u + 4)
                for t in range(T):
                    for h in range(4 * u, 4 * u + 4):
                        o = (h % 4) * (HD + 1)
                        ins = product(bank[AGG[t][u]][:, o:o + HD + 1],
                                      lambda s: logit[:, s, h, t * P:(t + 1) * P], lambda s: hx[:, s, h, :], T)
                    ins.then_inc(agg_full, 1)

            aggregate(0)
            pe.wait_ge(ctx_ready, 4)
            pe.wait_ge(qT_ready, 4)
            yT_made(1, (5, 2))
            aggregate(1)
            pe.wait_ge(yT_ready, 4)
            attn_out("out1", (3, 4))
            xT_made(3, x1g, (0, 1))
            node_terms(1, 6, 3)
            node_rows(1, 7)
            pe.wait_ge(alT_ready, 2)
            for a in range(2):
                ins = selected(half((2, 6)[a], 0), pick[0:1, 0, :], alT_hi[0:1, a, :], alT_lo[0:1, a, :])
            ins.then_inc(src_full, 1)
            pe.wait_ge(mix_ready, 4)
            w = Weight("gat2")
            weights_in(w)
            split_product(bank[3][:, :], lambda c: xT_at(c, 0), w.at, C).then_inc(hx_full, 1)
            pe.wait_ge(max_ready, 6)
            for t in range(T):
                ins = nc.tensor.transpose(bank[5][0:1, t * P:(t + 1) * P], mz[:, t, 0:1], ident[:, :])
            ins.then_inc(mT_full, 1)
            split_product(bank[4][:, :], lambda c: xT_at(c, 1), w.at, C).then_inc(hx_full, 1)
            pe.wait_ge(mT_ready, 2)
            selected(half(7, 0), pick[0:1, 0, :], mT_hi[0:1, :], mT_lo[0:1, :]).then_inc(max_full, 1)
            pe.wait_ge(hx_ready, 4)
            pe.wait_ge(weight_ready, 10)
            for t in range(T):
                product(bank[t][:, :], lambda s: logit[:, s, 0, t * P:(t + 1) * P], lambda s: h2[:, s, :], T)
                product(bank[(2, 5)[t]][:, 0:1], lambda s: logit[:, s, 0, t * P:(t + 1) * P],
                        lambda s: ones[:, 0:1], T).then_inc(agg_full, 1)
            xT_made(4, xn, (3, 4))
            pe.wait_ge(narrow_ready, 3)
            logits(5, 1, 4)
            up("up1", 0, 3)
            positions(1, 6)
            up("up1", 3, C)
            gate_rows(1, 7)
            gate_spread(1, (2, 5))
            for t in range(T):
                dst = bank[3 + t][:, :]
                cols = slice(t * P, (t + 1) * P)
                g_hi, g_lo = gateT_hi[0:EXPERTS[1], cols], gateT_lo[0:EXPERTS[1], cols]
                mm(dst, g_hi, b_down_hi[:, :], start=True, stop=False)
                mm(dst, g_hi, b_down_lo[:, :], start=False, stop=False)
                mm(dst, g_lo, b_down_hi[:, :], start=False, stop=False)
                down("down1", t, dst, C, 1, True)


def _chunks(a):
    c = a.shape[0] // 128
    return a.reshape(c, 128, -1).transpose(1, 0, 2)


def kernel(**inputs):
    import numpy as np
    import concourse.bacc as bacc
    from concourse import mybir
    from concourse.bass_utils import run_bass_kernel_spmd

    a = {k: np.asarray(v) for k, v in inputs.items()}
    hidden = 512
    wq0, wk0, wv0 = (a["L0_mix_w_qkv"][i * hidden:(i + 1) * hidden].T for i in range(3))
    wq1, wk1, wv1 = (a["L1_mix_W_qkv"][:, i * hidden:(i + 1) * hidden] for i in range(3))

    def experts_in(w):
        return _chunks(w.transpose(1, 0, 2).reshape(w.shape[1], -1))

    def experts_out(w):
        return _chunks(w.reshape(-1, w.shape[2]))

    def column(v):
        return v.reshape(-1, 128).T

    arrays = {
        "x": a["x"], "src": a["src"], "dst": a["dst"],
        "k0": _chunks(wk0), "q0": _chunks(wq0), "v0": _chunks(wv0),
        "gnn0": _chunks(a["L0_gnn_W"]), "out0": _chunks(a["L0_mix_w_out"].T),
        "b_gnn0": a["L0_gnn_b"], "diffusion": a["L0_gnn_diffusion_weights"], "gamma0": a["L0_mix_gamma"],
        "gate": _chunks(a["L0_ffn_w_gating"]), "up0": experts_in(a["L0_ffn_w1"]),
        "down0": experts_out(a["L0_ffn_w2"]),
        "gat1": _chunks(a["L1_gnn_W1"]), "w1t": _chunks(a["L1_gnn_W1"].T),
        "gat2": _chunks(a["L1_gnn_W2"]), "w2t": _chunks(a["L1_gnn_W2"].T),
        "a_src1": column(a["L1_gnn_a_src1"]), "a_dst1": column(a["L1_gnn_a_dst1"]),
        "a_src2": column(a["L1_gnn_a_src2"]), "a_dst2": column(a["L1_gnn_a_dst2"]),
        "b1": a["L1_gnn_b1"], "g1": a["L1_gnn_g1"], "beta1": a["L1_gnn_beta1"],
        "b2": a["L1_gnn_b2"], "g2": a["L1_gnn_g2"], "beta2": a["L1_gnn_beta2"],
        "k1": _chunks(wk1), "q1": _chunks(wq1), "v1": _chunks(wv1),
        "out1": _chunks(a["L1_mix_W_out"]), "b_out1": a["L1_mix_b_out"],
        "router": _chunks(a["L1_ffn_Wr"]), "b_router": a["L1_ffn_br"],
        "up1": experts_in(a["L1_ffn_W1"]), "b_up1": column(a["L1_ffn_b1"]),
        "down1": experts_out(a["L1_ffn_W2"]), "b_down1": a["L1_ffn_b2"],
    }
    arrays = {k: np.ascontiguousarray(v) for k, v in arrays.items()}
    nc = bacc.Bacc("TRN2", target_bir_lowering=False, num_devices=1)
    aps = {k: nc.dram_tensor("in_" + k, v.shape, mybir.dt.from_np(v.dtype), kind="ExternalInput").ap()
           for k, v in arrays.items()}
    out = nc.dram_tensor("out", a["x"].shape, mybir.dt.from_np(a["x"].dtype), kind="ExternalOutput").ap()
    gps_two_layers(nc, aps, out)
    r = run_bass_kernel_spmd(nc, [{"in_" + k: v for k, v in arrays.items()}], core_ids=[0])
    return r.results[0]["out"]
```

```python
import concourse.bass as bass
from concourse import mybir
from contextlib import ExitStack



def gps_two_layers(nc, A, out):
    f32, bf16, f32r = mybir.dt.float32, mybir.dt.bfloat16, mybir.dt.float32r
    i32, u32 = mybir.dt.int32, mybir.dt.uint32
    ALU, ACT, AX = mybir.AluOpType, mybir.ActivationFunctionType, mybir.AxisListType

    P = 128
    N, D = A["x"].shape
    T = N // P
    C = D // P
    EDGES = A["src"].shape[0]
    ET = EDGES // P
    H, HD = 8, 64
    STEPS = A["diffusion"].shape[0] - 1
    EXPERTS = (16, 8)
    FF = 64
    CAP0 = max(min(N, int(N * 2 * 2.0 / EXPERTS[0])), 4)
    CAP1 = max(1, -int(-1.25 * N * 2 // EXPERTS[1]))
    EPS, GATE_EPS = 1e-5, 1e-9
    SLOPE = 0.2
    BIG = 3.0e38
    FAR = 1.0e30

    ctx = ExitStack()
    with ctx:
        def sb(name, shape, dt=f32):
            return ctx.enter_context(nc.sbuf_tensor(name, shape, dt))

        def sem(name):
            return ctx.enter_context(nc.semaphore(name))

        UNIT, RAWS, SLOTS = 2 * D, 4, 6
        raw = sb("raw", [P, RAWS, UNIT])
        w_hi = sb("w_hi", [P, SLOTS, UNIT], f32r)
        w_lo = sb("w_lo", [P, SLOTS, UNIT], f32r)
        ORDER = ["k0", "q0", "v0", "gnn0", "out0", "up0", "down0",
                 "gat1", "k1", "q1", "v1", "out1", "gat2", "up1", "down1"]
        unit_of, units = {}, []
        for name in ORDER:
            unit_of[name] = len(units)
            parts = A[name].shape[1] * A[name].shape[2] // UNIT
            flat = A[name].rearrange("p c n -> p (c n)")
            units += [(name, flat[:, i * UNIT:(i + 1) * UNIT]) for i in range(parts)]
        U = len(units)
        VECTOR_LO = (1, 16, 19)

        class Weight:

            def __init__(self, name):
                self.first, self.width = unit_of[name], A[name].shape[2]
                self.units = A[name].shape[1] * self.width // UNIT

            def at(self, c, c0=0, c1=None):
                o = c * self.width + c0
                slot = (self.first + o // UNIT) % SLOTS
                n = (self.width if c1 is None else c1) - c0
                return tuple(w[:, slot, o % UNIT:o % UNIT + n] for w in (w_hi, w_lo))

        ring = sb("ring", [P, 4 * 1024])
        RING = 16
        onehot = ring[:, :].bitcast(bf16).rearrange("p (j a n) -> p j a n", j=RING, a=2)
        w1t = ring[:, 2048:4096].rearrange("p (c n) -> p c n", c=C)
        w2t = ring[:, 0:2048].rearrange("p (c n) -> p c n", c=C)
        hid = ring[:, 0:2048].rearrange("p (c n) -> p c n", c=8)
        logit = ring[:, :].rearrange("p (s h n) -> p s h n", s=T, h=H)
        w_gate = sb("w_gate", [P, C, EXPERTS[0]])
        w_router = sb("w_router", [P, C, EXPERTS[1]])
        narrow_hi = sb("narrow_hi", [P, 2, C, EXPERTS[0]], f32r)
        narrow_lo = sb("narrow_lo", [P, 2, C, EXPERTS[0]], f32r)

        row_names = ["b_gnn0", "gamma0", "b1", "g1", "beta1", "b2", "g2", "beta2", "b_out1"]
        rows = sb("rows", [P, len(row_names), D])
        row = {n: rows[:, i, :] for i, n in enumerate(row_names)}
        diffusion = sb("diffusion", [P, STEPS + 1])
        b_router = sb("b_router", [P, EXPERTS[1]])
        b_up1 = sb("b_up1", [P, C])
        b_down_hi = sb("b_down_hi", [EXPERTS[1], D], f32r)
        b_down_lo = sb("b_down_lo", [EXPERTS[1], D], f32r)
        att1 = sb("att1", [P, 2, C])
        att2 = sb("att2", [P, 2, C])

        ident = sb("ident", [P, P])
        ones = sb("ones", [P, P])
        before = sb("before", [P, P])
        pick = sb("pick", [2 * H, 2 * H, P], f32r)
        spread = sb("spread", [EXPERTS[0], 8, 2, FF], f32r)
        headmask = sb("headmask", [P, C, H])
        iota_bf = sb("iota_bf", [P, N], bf16)
        iota_f = sb("iota_f", [P, EXPERTS[0]])
        minus_half = sb("minus_half", [P, T])
        edges = sb("edges", [P, 2, ET])

        xa = sb("xa", [P, T, D])
        xb = sb("xb", [P, T, D])
        xn = sb("xn", [P, T, D])
        xT_hi = sb("xT_hi", [P, C, N], f32r)
        xT_lo = sb("xT_lo", [P, C, N], f32r)
        q = sb("q", [P, T, D])
        v = sb("v", [P, T, D])
        ek = sb("ek", [P, T, D])
        ekT = sb("ekT", [P, C, N])
        qT = ekT
        yT_hi = sb("yT_hi", [P, C, N], f32r)
        yT_lo = sb("yT_lo", [P, C, N], f32r)
        yT = q[:, :, :].rearrange("p t (c n) -> p (t c) n", n=N)
        ctxbd = sb("ctxbd", [P, C, P])
        hr = sb("hr", [P, T, D])
        both_hi = sb("both_hi", [P, 2, T * D], f32r)
        both_lo = sb("both_lo", [P, 2, T * D], f32r)
        cur_hi = both_hi[:, :, :].rearrange("p i (t n) -> p i t n", t=T)
        cur_lo = both_lo[:, :, :].rearrange("p i (t n) -> p i t n", t=T)
        hid_hi = both_hi[:, :, :].rearrange("p i (c n) -> p (i c) n", n=N)
        hid_lo = both_lo[:, :, :].rearrange("p i (c n) -> p (i c) n", n=N)
        diffused = sb("diffused", [P, T, D])
        b_down1 = diffused[0:EXPERTS[1], 0, :]
        mixed = v
        count = sb("count", [P, T, N])
        countT = sb("countT", [P, T, N])
        linked = sb("linked", [P, T, N], f32r)
        far = sb("far", [P, T, N])
        iota_i = far[:, 0, :].bitcast(i32)
        edges_i = far[:, 1, 0:2 * ET].bitcast(i32).rearrange("p (a j) -> p a j", a=2)
        hx = sb("hx", [P, T, H, HD + 1])
        h2 = ek
        g_a = hr
        g_b = diffused
        x1g = xn
        A2 = 2 * H + 2
        wa = sb("wa", [P, C, A2])
        wa_hi = sb("wa_hi", [P, C, A2], f32r)
        wa_lo = sb("wa_lo", [P, C, A2], f32r)
        al = sb("al", [P, T, 2 * H])
        rows_hi = sb("rows_hi", [EXPERTS[0], 2, N], f32r)
        rows_lo = sb("rows_lo", [EXPERTS[0], 2, N], f32r)
        alT_hi, alT_lo = rows_hi[:, 1, :], rows_lo[:, 1, :]
        mT_hi, mT_lo = rows_hi[:, 0, :], rows_lo[:, 0, :]
        gateT_hi, gateT_lo = rows_hi[:, 1, :], rows_lo[:, 1, :]
        lgT = ekT[0:EXPERTS[0], 0, :]
        mx = sb("mx", [P, T, H])
        less = sb("less", [P, T, 2 * H])
        mz = less[:, :, 0:H]
        junk = [g[:, :, :].rearrange("p t (a n) -> p (t a) n", a=2) for g in (g_a, g_b)]
        attblk = sb("attblk", [P, C, 2 * H])
        stats = sb("stats", [P, T, 6])
        mv = sb("mv", [P, T, 2])
        veps = sb("veps", [P, T])
        rstd = sb("rstd", [P, T])
        kmax = sb("kmax", [P, C])
        ksum = sb("ksum", [P, C])
        kinv = sb("kinv", [P, C])
        qmax = sb("qmax", [P, T, H])
        qsum = sb("qsum", [P, T, H])
        degree = sb("degree", [P, T])
        degree_w = sb("degree_w", [P, STEPS, T])
        E0 = EXPERTS[0]
        lg = sb("lg", [P, T, E0])
        al_slope = lg[:, :, 0:H]
        prob = sb("prob", [P, T, E0])
        prob2 = sb("prob2", [P, T, E0])
        peak, total = sb("peak", [P, T]), sb("total", [P, T])
        weight, flag = sb("weight", [P, T, 2]), sb("flag", [P, T, 2])
        top = sb("top", [P, 2, T, 8])
        top_i = sb("top_i", [P, 2, T, 8], u32)
        top_f = sb("top_f", [P, T, 2])
        mask = sb("mask", [P, T, 2 * E0])
        kept = sb("kept", [P, T, 2 * E0])
        poss = sb("poss", [P, T, 2 * E0])
        gate = sb("gate", [P, T, E0])

        bank = [ctx.enter_context(nc.psum_tensor(f"bank{i}", [P, 512], f32)) for i in range(8)]

        x_in, edges_in, small_in, b_down_in = sem("x_in"), sem("edges_in"), sem("small_in"), sem("b_down_in")
        raw_in = [sem(f"raw_in{i}") for i in range(RAWS)]
        hi_ready, lo_ready = sem("hi_ready"), sem("lo_ready")
        w1t_in, w2t_in, narrow_ready = sem("w1t_in"), sem("w2t_in"), sem("narrow_ready")
        consts, iota_ready = sem("consts"), sem("iota_ready")
        var_ready, rstd_ready, xn_ready = sem("var_ready"), sem("rstd_ready"), sem("xn_ready")
        xT_full, xT_rounded, xT_ready = sem("xT_full"), sem("xT_rounded"), sem("xT_ready")
        k_full, kmax_ready, ekT_ready, ek_full, ek_ready = (sem(n) for n in
            ["k_full", "kmax_ready", "ekT_ready", "ek_full", "ek_ready"])
        q_full, q_shifted, q_exp, q_ready, qT_full, qT_ready = (sem(n) for n in
            ["q_full", "q_shifted", "q_exp", "q_ready", "qT_full", "qT_ready"])
        v_full, v_ready, ctx_full, ctx_ready = (sem(n) for n in
            ["v_full", "v_ready", "ctx_full", "ctx_ready"])
        yT_full, yT_rounded, yT_ready, o_full, mix_ready = (sem(n) for n in
            ["yT_full", "yT_rounded", "yT_ready", "o_full", "mix_ready"])
        onehot_used = sem("onehot_used")
        onehot_ready, count_full, count_ready, countT_full, linked_ready, countT_ready = (sem(n) for n in
            ["onehot_ready", "count_full", "count_ready", "countT_full", "linked_ready", "countT_ready"])
        h_full, hr_ready, cur_rounded, cur_ready, step_full, step_read = (sem(n) for n in
            ["h_full", "hr_ready", "cur_rounded", "cur_ready", "step_full", "step_read"])
        lgT_full, lgT_ready = sem("lgT_full"), sem("lgT_ready")
        logits_full, shift_ready, gexp_ready, masks_ready, pos_full = (sem(n) for n in
            ["logits_full", "shift_ready", "gexp_ready", "masks_ready", "pos_full"])
        gate_ready, gateT_full, gateT_rounded, gateT_ready, spread_full = (sem(n) for n in
            ["gate_ready", "gateT_full", "gateT_rounded", "gateT_ready", "spread_full"])
        up_full, up_ready, gated, hid_rounded, hid_ready, down_full = (sem(n) for n in
            ["up_full", "up_ready", "gated", "hid_rounded", "hid_ready", "down_full"])
        wa_full, wa_read, wa_ready, al_full, al_ready, alT_full, alT_rounded, alT_ready = (sem(n) for n in
            ["wa_full", "wa_read", "wa_ready", "al_full", "al_ready", "alT_full", "alT_rounded", "alT_ready"])
        src_full, max_ready, mT_full, mT_rounded, mT_ready, hx_full, hx_ready = (sem(n) for n in
            ["src_full", "max_ready", "mT_full", "mT_rounded", "mT_ready", "hx_full", "hx_ready"])
        dst_full, z_ready, max_full, shifted, exp_ready, weight_ready = (sem(n) for n in
            ["dst_full", "z_ready", "max_full", "shifted", "exp_ready", "weight_ready"])
        agg_full, y_ready, elu_exp, out_ready, stored = (sem(n) for n in
            ["agg_full", "y_ready", "elu_exp", "out_ready", "stored"])
        degree_ready = sem("degree_ready")
        kinv_ready, yT_copied = sem("kinv_ready"), sem("yT_copied")
        xn_less_one, sum_full, vector_lo = sem("xn_less_one"), sem("sum_full"), sem("vector_lo")
        dve_step, pool_step = sem("dve_step"), sem("pool_step")

        xT_read = {1: (h_full, 2), 2: (up_full, 4), 3: (v_full, 4), 4: (hx_full, 4)}
        last_read = {"k0": (k_full, 2), "q0": (q_full, 2), "v0": (v_full, 2), "gnn0": (h_full, 2),
                     "out0": (o_full, 2), "up0": (up_full, 4), "down0": (down_full, 2), "gat1": (hx_full, 2),
                     "k1": (k_full, 4), "q1": (q_full, 4), "v1": (v_full, 4), "out1": (o_full, 4),
                     "gat2": (hx_full, 4)}

        def lo_done(u):
            v = sum(x <= u for x in VECTOR_LO)
            return (vector_lo, v) if u in VECTOR_LO else (lo_ready, u + 1 - v)

        block = ctx.enter_context(nc.Block())

        def half(b, i, n=N):
            return bank[b][:, i * n:(i + 1) * n]

        @block.sync
        def _(sp):
            for t in range(T):
                sp.dma_start(xa[:, t, :], A["x"][t * P:(t + 1) * P, :]).then_inc(x_in, 16)

            def load(u0, u1):
                for u in range(u0, u1):
                    if u >= RAWS:
                        sp.wait_ge(*lo_done(u - RAWS))
                    sp.dma_start(raw[:, u % RAWS, :], units[u][1]).then_inc(raw_in[u % RAWS], 16)

            load(0, 2)
            for a, n in enumerate(("src", "dst")):
                sp.dma_start(edges_i[:, a, :], A[n].rearrange("(p j) -> p j", p=P)).then_inc(edges_in, 16)
            load(2, 8)
            sp.dma_start(b_down1, A["b_down1"]).then_inc(b_down_in, 16)
            sp.dma_start(w_gate[:, :, :], A["gate"]).then_inc(small_in, 16)
            sp.dma_start(diffusion[:, :], A["diffusion"].partition_broadcast(P)).then_inc(small_in, 16)
            for n in row_names:
                sp.dma_start(row[n], A[n].partition_broadcast(P)).then_inc(small_in, 16)
            sp.dma_start(b_router[:, :], A["b_router"].partition_broadcast(P)).then_inc(small_in, 16)
            sp.dma_start(b_up1[:, :], A["b_up1"]).then_inc(small_in, 16)
            sp.dma_start(w_router[:, :, :], A["router"]).then_inc(small_in, 16)
            for a, n in enumerate(("a_src1", "a_dst1")):
                sp.dma_start(att1[:, a, :], A[n]).then_inc(small_in, 16)
            for a, n in enumerate(("a_src2", "a_dst2")):
                sp.dma_start(att2[:, a, :], A[n]).then_inc(small_in, 16)
            load(8, 14)
            sp.wait_ge(count_full, 1)
            sp.dma_start(w1t, A["w1t"]).then_inc(w1t_in, 16)
            sp.dma_start(w2t, A["w2t"]).then_inc(w2t_in, 16)
            load(14, U)
            for t in range(T):
                sp.wait_ge(out_ready, t + 1)
                sp.dma_start(out[t * P:(t + 1) * P, :], xa[:, t, :]).then_inc(stored, 16)
            sp.wait_ge(stored, 16 * T)

        SMALLS = 16 * (2 + len(row_names) + 7)

        @block.gpsimd
        def _(pool):
            n = [0]

            def then(ins):
                n[0] += 1
                ins.then_inc(pool_step, 1)
                pool.wait_ge(pool_step, n[0])

            def fill(dst, base, pattern, cm):
                then(nc.gpsimd.affine_select(out=dst, in_=dst.bitcast(f32), compare_op=ALU.not_equal, fill=1.0,
                                             base=base, pattern=pattern, channel_multiplier=cm))

            nc.gpsimd.iota(iota_i[:, :], pattern=[[1, N]], base=0, channel_multiplier=0).then_inc(iota_ready, 1)
            then(nc.gpsimd.memset(minus_half[:, :], -0.5))
            then(nc.gpsimd.memset(ident[:, :], 0.0))
            fill(ident[:, :], 0, [[-1, P]], 1)
            nc.gpsimd.memset(ctxbd[:, :, :], 0.0).then_inc(consts, 1)

            def roots(i):
                for t in range(T):
                    pool.wait_ge(var_ready, T * i + t + 1)
                    nc.gpsimd.tensor_tensor(rstd[:, t:t + 1], veps[:, t:t + 1], minus_half[:, t:t + 1], ALU.pow)\
                        .then_inc(rstd_ready, 1)

            def split(u0, u1):
                for u in range(u0, u1):
                    if u in VECTOR_LO:
                        continue
                    pool.wait_ge(hi_ready, u + 1)
                    nc.gpsimd.tensor_tensor(w_lo[:, u % SLOTS, :], raw[:, u % RAWS, :],
                                            w_hi[:, u % SLOTS, :].bitcast(f32), ALU.subtract)\
                        .then_inc(lo_ready, 1)

            roots(0)
            split(0, 8)
            then(nc.gpsimd.memset(ones[:, :], 1.0))
            then(nc.gpsimd.affine_select(out=before[:, :], in_=ones[:, :], compare_op=ALU.is_gt, fill=0.0,
                                         base=0, pattern=[[1, P]], channel_multiplier=-1))
            then(nc.gpsimd.memset(pick[:, :, :].bitcast(f32), 0.0))
            fill(pick[:, :, :], 0, [[-1, 2 * H], [0, P]], 1)
            then(nc.gpsimd.memset(spread[:, :, :, :].bitcast(f32), 0.0))
            fill(spread[:, :, :, :], 0, [[-2, 8], [-1, 2], [0, FF]], 1)
            then(nc.gpsimd.memset(headmask[:, :, :], 0.0))
            fill(headmask[0:64, :, :], 0, [[2, C], [-1, H]], 0)
            fill(headmask[64:128, :, :], 1, [[2, C], [-1, H]], 0)
            pool.wait_ge(small_in, SMALLS)
            for a in range(2):
                then(nc.gpsimd.tensor_tensor(attblk[:, :, a * H:(a + 1) * H], headmask[:, :, :],
                                             att1[:, a, :].unsqueeze(2).broadcast_to([P, C, H]), ALU.mult))
            nc.gpsimd.memset(hx[:, :, :, HD:HD + 1], 1.0).then_inc(consts, 1)
            split(8, 14)
            roots(1)
            split(14, 16)
            roots(2)
            split(16, 19)
            roots(3)
            split(20, 26)
            pool.wait_ge(xT_full, 6)
            nc.gpsimd.tensor_scalar(xn[:, :, :], xn[:, :, :], -1.0, None, ALU.add).then_inc(xn_less_one, 1)
            split(26, 30)
            roots(4)
            for j in range(2):
                pool.wait_ge(yT_rounded, 2 + j + 1)
                pool.wait_ge(yT_copied, j + 1)
                nc.gpsimd.tensor_tensor(yT_lo[:, 2 * j:2 * j + 2, :], yT[:, 2 * j:2 * j + 2, :],
                                        yT_hi[:, 2 * j:2 * j + 2, :].bitcast(f32), ALU.subtract).then_inc(yT_ready, 1)
            split(30, 32)
            roots(5)
            roots(6)
            split(32, 34)

        @block.scalar
        def _(act):
            def copy(dst, src):
                return nc.scalar.activation(dst, src, ACT.Copy)

            def hi(u0, u1):
                for u in range(u0, u1):
                    act.wait_ge(raw_in[u % RAWS], 16 * (u // RAWS + 1))
                    if u >= SLOTS:
                        act.wait_ge(*last_read[units[u - SLOTS][0]])
                    copy(w_hi[:, u % SLOTS, :], raw[:, u % RAWS, :]).then_inc(hi_ready, 1)

            def xT_part(i, banks, tiles=range(T)):
                for t in tiles:
                    act.wait_ge(xT_full, T * i + t + 1)
                    if i and t == 0:
                        act.wait_ge(*xT_read[i])
                    copy(xT_hi[:, :, t * P:(t + 1) * P], bank[banks[t]][:, :].rearrange("p (c n) -> p c n", c=C))\
                        .then_inc(xT_rounded, 1)

            def mix_exps(L):
                for m in range(C):
                    act.wait_ge(kmax_ready, 2 * L + m // 2 + 1)
                    if L:
                        act.wait_ge(yT_full, 2)
                    nc.scalar.activation(ekT[:, m, :], half(4 + m // 2, m % 2), ACT.Exp,
                                         bias=kmax[:, m:m + 1], accum_out=ksum[:, m:m + 1]).then_inc(ekT_ready, 1)

            def mix_q(L):
                for t in range(T):
                    act.wait_ge(q_shifted, 2 * L + t + 1)
                    nc.scalar.activation(q[:, t, :], q[:, t, :], ACT.Exp).then_inc(q_exp, 1)

            def mix_v(L, banks, tiles=range(T)):
                for t in tiles:
                    act.wait_ge(v_full, 2 * L + t + 1)
                    if L:
                        act.wait_ge(ctx_full, 1)
                    copy(v[:, t, :], bank[banks[t]][:, :]).then_inc(v_ready, 1)

            def yT_part(L, banks, parts=range(2)):
                for j in parts:
                    act.wait_ge(yT_full, 2 * L + j + 1)
                    if L:
                        act.wait_ge(o_full, 2)
                    copy(yT_hi[:, 2 * j:2 * j + 2, :], bank[banks[j]][:, :].rearrange("p (c n) -> p c n", c=2))\
                        .then_inc(yT_rounded, 1)

            def lgT_part(L, b):
                act.wait_ge(lgT_full, L + 1)
                copy(lgT[0:EXPERTS[L], :], bank[b][0:EXPERTS[L], 0:N]).then_inc(lgT_ready, 1)

            def gate_exp(L):
                act.wait_ge(shift_ready, L + 1)
                nc.scalar.activation(prob[:, :, 0:EXPERTS[L]], lg[:, :, 0:EXPERTS[L]], ACT.Exp)\
                    .then_inc(gexp_ready, 1)

            def elu(g, tiles=range(T)):
                for t in tiles:
                    act.wait_ge(y_ready, T * g + t + 1)
                    nc.scalar.activation(g_b[:, t, :], g_a[:, t, :], ACT.Exp).then_inc(elu_exp, 1)

            def diffuse(i, banks):
                for t in range(T):
                    act.wait_ge(step_full, T * i + t + 1)
                    nc.scalar.activation(cur_hi[:, (i + 1) % 2, t, :], bank[banks[t]][:, :], ACT.Copy,
                                         scale=degree[:, t:t + 1]).then_inc(cur_rounded, 1)

            def gateT_part(L, b):
                act.wait_ge(gateT_full, L + 1)
                copy(gateT_hi[0:EXPERTS[L], :], bank[b][0:EXPERTS[L], 0:N]).then_inc(gateT_rounded, 1)

            def hid_part(L, pairs):
                for j in pairs:
                    act.wait_ge(gated, 4 * L + j + 1)
                    copy(hid_hi[:, 2 * j:2 * j + 2, :], hid[:, 2 * j:2 * j + 2, :]).then_inc(hid_rounded, 1)

            def wa_part(g, b):
                act.wait_ge(wa_full, g + 1)
                w = slice(0, 2 * H) if g == 0 else slice(2 * H, A2)
                copy(wa[:, :, w], bank[b][:, 0:C * A2].rearrange("p (c n) -> p c n", c=C)[:, :, w]).then_inc(wa_read, 1)

            hi(0, 2)
            xT_part(0, (0, 1))
            hi(2, 6)
            mix_exps(0)
            hi(6, 8)
            mix_q(0)
            hi(8, 10)
            mix_v(0, (6, 7))
            hi(10, 12)
            for t in range(T):
                act.wait_ge(hr_ready, t + 1)
                copy(cur_hi[:, 0, t, :], hr[:, t, :]).then_inc(cur_rounded, 1)
            hi(12, 14)
            for t in range(T):
                act.wait_ge(ek_full, t + 1)
                copy(ek[:, t, :], bank[4 + t][:, :]).then_inc(ek_ready, 1)
            for j in range(2):
                act.wait_ge(qT_full, j + 1)
                copy(qT[:, 2 * j:2 * j + 2, :], bank[j][:, :].rearrange("p (c n) -> p c n", c=2)).then_inc(qT_ready, 1)
            for t in range(T):
                act.wait_ge(count_full, 1)
                copy(count[:, t, :], half(2 + t, 0)).then_inc(count_ready, 1)
            yT_part(0, (4, 5))
            act.wait_ge(linked_ready, 2)
            copy(countT[:, :, :], bank[7][:, :].rearrange("p (c n) -> p c n", c=T)).then_inc(countT_ready, 1)
            act.wait_ge(degree_ready, 1)
            diffuse(0, (2, 3))
            diffuse(1, (7, 4))
            hi(14, 16)
            wa_part(0, 6)
            wa_part(1, 5)
            xT_part(1, (4, 5))
            lgT_part(0, 6)
            gate_exp(0)
            act.wait_ge(wa_full, 2)
            for m in range(8):
                if m == 6:
                    gateT_part(0, 6)
                    hid_part(0, (0, 1, 2))
                act.wait_ge(up_full, m // 2 + 1)
                nc.scalar.activation(hid[:, m, :], half(m // 2, m % 2), ACT.Relu).then_inc(up_ready, 1)
            hi(16, 17)
            hid_part(0, (3,))
            hi(17, 18)
            hi(18, 20)

            def hx_part(t):
                act.wait_ge(hx_full, t + 1)
                copy(hx[:, t, :, 0:HD], bank[2 + t][:, :].rearrange("p (h n) -> p h n", h=H)).then_inc(hx_ready, 1)

            def alT_part(g, b):
                k = (2 * H, 2)[g]
                act.wait_ge(alT_full, g + 1)
                copy(alT_hi[0:k, :], bank[b][0:k, 0:N]).then_inc(alT_rounded, 1)

            def exp_weights(j):
                for s in range(T):
                    act.wait_ge(shifted, 2 * j + s + 1)
                    nc.scalar.activation(logit[:, s, 2 * j:2 * j + 2, :], logit[:, s, 2 * j:2 * j + 2, :],
                                         ACT.Exp).then_inc(exp_ready, 1)

            def edge_logits(j):
                act.wait_ge(dst_full, j + 1)
                for s in range(T):
                    for h in range(2):
                        hh = 2 * j + h
                        nc.scalar.activation(logit[:, s, hh, :], half((0, 6)[j % 2], h), ACT.Identity,
                                             bias=al[:, s, hh:hh + 1]).then_inc(z_ready, 1)

            xT_part(2, (4, 5), (0,))
            hi(20, 22)
            xT_part(2, (4, 5), (1,))
            alT_part(0, 6)
            hx_part(0)
            act.wait_ge(al_full, 1)
            copy(al[:, :, :], bank[4][:, N:N + T * 2 * H].rearrange("p (t n) -> p t n", t=T)).then_inc(al_ready, 1)
            hi(22, 24)
            hx_part(1)
            hi(24, 26)
            act.wait_ge(mT_full, 1)
            copy(mT_hi[:, :], bank[2][0:2 * H, 0:N]).then_inc(mT_rounded, 1)
            act.wait_ge(al_ready, 1)
            act.wait_ge(hid_ready, 4)
            act.wait_ge(wa_full, 2)
            edge_logits(0)
            edge_logits(1)
            exp_weights(0)
            edge_logits(2)
            exp_weights(1)
            edge_logits(3)
            mix_exps(1)
            exp_weights(2)
            exp_weights(3)
            hi(26, 28)
            mix_q(1)
            mix_v(1, (5, 4), (0,))
            hi(28, 30)
            mix_v(1, (5, 4), (1,))
            for t in range(T):
                act.wait_ge(ek_full, 2 + t + 1)
                copy(ek[:, t, :], bank[2 + t][:, :]).then_inc(ek_ready, 1)
            act.wait_ge(kinv_ready, 1)
            for m in range(C):
                act.wait_ge(qT_full, 2 + m // 2 + 1)
                nc.scalar.activation(qT[:, m, :], half(4 + m // 2, m % 2), ACT.Copy,
                                     scale=kinv[:, m:m + 1]).then_inc(qT_ready, 1)
            elu(0, (0,))
            act.wait_ge(ctx_full, 2)
            for r in range(2):
                p0, p1 = r * HD, (r + 1) * HD
                copy(ctxbd[p0:p1, :, p0:p1], bank[3][p0:p1, :].rearrange("p (m n) -> p m n", m=C)[:, :, p0:p1])\
                    .then_inc(ctx_ready, 1)
            elu(0, (1,))
            yT_part(1, (5, 2))
            xT_part(3, (4, 3))
            for j in range(2):
                copy(yT[:, 2 * j:2 * j + 2, :], bank[(5, 2)[j]][:, :].rearrange("p (c n) -> p c n", c=2))\
                    .then_inc(yT_copied, 1)
            alT_part(1, 7)
            act.wait_ge(al_full, 2)
            copy(al[:, :, 0:2], bank[7][:, N:N + T * 2].rearrange("p (t a) -> p t a", t=T))\
                .then_inc(al_ready, 1)
            act.wait_ge(al_ready, 2)
            act.wait_ge(src_full, 5)
            for s in range(T):
                nc.scalar.activation(logit[:, s, 0, :], half(3, 0), ACT.Identity,
                                     bias=al[:, s, 0:1]).then_inc(z_ready, 1)
            act.wait_ge(mT_full, 2)
            copy(mT_hi[0:1, :], bank[6][0:1, 0:N]).then_inc(mT_rounded, 1)
            for s in range(T):
                act.wait_ge(shifted, 8 + s + 1)
                nc.scalar.activation(logit[:, s, 0, :], logit[:, s, 0, :], ACT.Exp).then_inc(exp_ready, 1)
            for t in range(T):
                act.wait_ge(hx_full, 2 + t + 1)
                copy(h2[:, t, :], bank[5 - t][:, :]).then_inc(hx_ready, 1)
            hi(30, 32)
            elu(1)
            hi(32, 34)
            xT_part(4, (3, 4))
            lgT_part(1, 5)
            gate_exp(1)
            act.wait_ge(gexp_ready, 2)
            for m in range(C):
                if m == 2:
                    gateT_part(1, 7)
                act.wait_ge(up_full, 4 + m // 2 + 1)
                nc.scalar.activation(hid[:, m, :], half(m // 2, m % 2), ACT.Gelu, bias=b_up1[:, m:m + 1])\
                    .then_inc(up_ready, 1)
            hid_part(1, (0, 1))

        @block.vector
        def _(dve):
            n = [0]
            V = nc.vector

            def go(ins):
                n[0] += 1
                ins.then_inc(dve_step, 1)
                return ins

            def settle(but=0):
                dve.wait_ge(dve_step, n[0] - but)

            def variance(i, t, src):
                go(V.bn_stats(stats[:, t, :], src))
                settle()
                go(V.bn_aggr(mv[:, t, :], stats[:, t, :]))
                settle()
                if i:
                    dve.wait_ge(rstd_ready, T * (i - 1) + t + 1)
                V.tensor_scalar(veps[:, t:t + 1], mv[:, t, 1:2], EPS, None, ALU.add).then_inc(var_ready, 1)

            def variances(i, src):
                for t in range(T):
                    if i:
                        settle(T - 1)
                    go(V.bn_stats(stats[:, t, :], src(t)))
                for t in range(T):
                    settle(T - 1)
                    go(V.bn_aggr(mv[:, t, :], stats[:, t, :]))
                for t in range(T):
                    settle(T - 1 - t)
                    if i:
                        dve.wait_ge(rstd_ready, T * (i - 1) + t + 1)
                    V.tensor_scalar(veps[:, t:t + 1], mv[:, t, 1:2], EPS, None, ALU.add).then_inc(var_ready, 1)

            def norm_rows(i, dst, src, t):
                dve.wait_ge(rstd_ready, T * i + t + 1)
                V.tensor_scalar(dst, src, mv[:, t, 0:1], rstd[:, t:t + 1], ALU.subtract, ALU.mult)\
                    .then_inc(xn_ready, 1)

            def xT_part(i, banks, tiles=range(T)):
                for t in tiles:
                    dve.wait_ge(xT_rounded, T * i + t + 1)
                    cols = slice(t * P, (t + 1) * P)
                    V.tensor_tensor(xT_lo[:, :, cols], bank[banks[t]][:, :].rearrange("p (c n) -> p c n", c=C),
                                    xT_hi[:, :, cols].bitcast(f32), ALU.subtract).then_inc(xT_ready, 1)

            def weight_lo(u):
                dve.wait_ge(hi_ready, u + 1)
                V.tensor_tensor(w_lo[:, u % SLOTS, :], raw[:, u % RAWS, :], w_hi[:, u % SLOTS, :].bitcast(f32),
                                ALU.subtract).then_inc(vector_lo, 1)

            def yT_part(banks):
                for j in range(2):
                    dve.wait_ge(yT_rounded, j + 1)
                    V.tensor_tensor(yT_lo[:, 2 * j:2 * j + 2, :],
                                    bank[banks[j]][:, :].rearrange("p (c n) -> p c n", c=2),
                                    yT_hi[:, 2 * j:2 * j + 2, :].bitcast(f32), ALU.subtract).then_inc(yT_ready, 1)

            def small_split(hi, lo, src):
                go(V.tensor_copy(hi, src))
                settle()
                V.tensor_tensor(lo, src, hi.bitcast(f32), ALU.subtract).then_inc(narrow_ready, 1)

            def k_max(L, parts=range(2)):
                for j in parts:
                    dve.wait_ge(k_full, 2 * L + j + 1)
                    V.tensor_reduce(kmax[:, 2 * j:2 * j + 2], bank[4 + j][:, :].rearrange("p (c n) -> p c n", c=2),
                                    AX.X, ALU.max, negate=True).then_inc(kmax_ready, 1)

            def bc(a, shape):
                return a.unsqueeze(len(a.shape)).broadcast_to(shape)

            def q_shift(L, banks):
                def src(t):
                    return bank[banks[t]][:, :].rearrange("p (h n) -> p h n", h=H)

                for t in range(T):
                    dve.wait_ge(q_full, 2 * L + t + 1)
                    go(V.tensor_reduce(qmax[:, t, :], src(t), AX.X, ALU.max))
                for t in range(T):
                    settle(T - 1 - t)
                    V.tensor_tensor(q[:, t, :].rearrange("p (h n) -> p h n", h=H), src(t),
                                    bc(qmax[:, t, :], [P, H, HD]), ALU.subtract).then_inc(q_shifted, 1)

            def q_norm(L):
                qh = q[:, :, :].rearrange("p t (h n) -> p t h n", h=H)
                for t in range(T):
                    dve.wait_ge(q_exp, 2 * L + t + 1)
                    go(V.tensor_reduce(qsum[:, t, :], qh[:, t], AX.X, ALU.add))
                settle()
                go(V.reciprocal(qsum[:, :, :], qsum[:, :, :]))
                settle()
                if L == 0:
                    go(V.tensor_scalar(qsum[:, :, :], qsum[:, :, :], float(HD) ** -0.5, None, ALU.mult))
                    settle()
                for t in range(T):
                    V.tensor_tensor(qh[:, t], qh[:, t], bc(qsum[:, t, :], [P, H, HD]), ALU.mult).then_inc(q_ready, 1)

            def context(b):
                dve.wait_ge(ekT_ready, 4)
                go(V.reciprocal(kinv[:, :], ksum[:, :]))
                settle()
                dve.wait_ge(ctx_full, 1)
                dve.wait_ge(consts, 1)
                for r in range(2):
                    p0, p1 = r * HD, (r + 1) * HD
                    src = bank[b][p0:p1, :].rearrange("p (m n) -> p m n", m=C)[:, :, p0:p1]
                    V.tensor_tensor(ctxbd[p0:p1, :, p0:p1], src, bc(kinv[p0:p1, :], [HD, C, HD]), ALU.mult)\
                        .then_inc(ctx_ready, 1)

            def gates(L, b, pb):
                E = EXPERTS[L]
                dve.wait_ge(logits_full, L + 1)
                x = bank[b][:, N:N + T * E].rearrange("p (t e) -> p t e", t=T)
                lgE, pE = lg[:, :, 0:E], prob[:, :, 0:E]

                def pairs(a):
                    return a[:, :, 0:2 * E].rearrange("p t (a e) -> p t a e", a=2)

                if L:
                    go(V.tensor_tensor(lgE, x, b_router[:, :].unsqueeze(1).broadcast_to([P, T, E]), ALU.add))
                    settle()
                    x = lgE
                go(V.tensor_reduce(peak[:, :], x, AX.X, ALU.max))
                settle()
                V.tensor_tensor(lgE, x, bc(peak[:, :], [P, T, E]), ALU.subtract).then_inc(shift_ready, 1)
                dve.wait_ge(gexp_ready, L + 1)
                go(V.tensor_reduce(total[:, :], pE, AX.X, ALU.add))
                settle()
                go(V.reciprocal(total[:, :], total[:, :]))
                settle()
                go(V.tensor_tensor(pE, pE, bc(total[:, :], [P, T, E]), ALU.mult))

                def largest(k, p):
                    settle()
                    for t in range(T):
                        go(V.max(top[:, k, t, :], p(t)))
                    for t in range(T):
                        settle(T - 1)
                        go(V.max_index(top_i[:, k, t, :], top[:, k, t, :], p(t)))
                    settle()

                largest(0, lambda t: prob[:, t, 0:E])
                io = iota_f[:, 0:E].unsqueeze(1).broadcast_to([P, T, E])
                m1, m2 = mask[:, :, 0:E], mask[:, :, E:2 * E]
                if L == 0:
                    go(V.tensor_copy(top_f[:, :, 0], top_i[:, 0, :, 0]))
                    settle()
                    go(V.tensor_tensor(m1, io, bc(top_f[:, :, 0], [P, T, E]), ALU.is_equal))
                    settle()
                    go(V.scalar_tensor_tensor(prob2[:, :, :], m1, 0.0, pE, ALU.is_equal, ALU.mult))
                    largest(1, lambda t: prob2[:, t, :])
                    go(V.tensor_copy(top_f[:, :, 1], top_i[:, 1, :, 0]))
                    settle()
                    V.tensor_tensor(m2, io, bc(top_f[:, :, 1], [P, T, E]), ALU.is_equal).then_inc(masks_ready, 1)
                    value = top[:, :, :, 0].rearrange("p a t -> p t a")
                else:
                    go(V.tensor_copy(top_f[:, :, :], top_i[:, 0, :, 0:2]))
                    settle()
                    V.tensor_tensor(pairs(mask), iota_f[:, 0:E].unsqueeze(1).unsqueeze(1).broadcast_to([P, T, 2, E]),
                                    bc(top_f[:, :, :], [P, T, 2, E]), ALU.is_equal).then_inc(masks_ready, 1)
                    value = top[:, 0, :, 0:2]

                def normed(dst, src):
                    go(V.scalar_tensor_tensor(total[:, :], src[:, :, 0], GATE_EPS, src[:, :, 1], ALU.add, ALU.add))
                    settle()
                    go(V.reciprocal(total[:, :], total[:, :]))
                    settle()
                    go(V.tensor_tensor(dst, src, bc(total[:, :], [P, T, 2]), ALU.mult))

                normed(weight[:, :, :], value)
                dve.wait_ge(masks_ready, L + 1)
                dve.wait_ge(pos_full, L + 1)
                pos = bank[pb][:, 0:T * 2 * E].rearrange("p (t e) -> p t e", t=T)
                if L == 0:
                    go(V.tensor_scalar(poss[:, 0, 0:E], bank[pb][:, T * 2 * E:T * 2 * E + E], float(CAP0), None,
                                       ALU.min))
                    go(V.scalar_tensor_tensor(kept[:, :, 0:E], pos[:, :, 0:E], float(CAP0), m1, ALU.is_lt, ALU.mult))
                    settle(1)
                    go(V.tensor_tensor(poss[:, :, E:2 * E], pos[:, :, E:2 * E],
                                       poss[:, 0:1, 0:E].broadcast_to([P, T, E]), ALU.add))
                    settle()
                    go(V.scalar_tensor_tensor(kept[:, :, E:2 * E], poss[:, :, E:2 * E], float(CAP0), m2,
                                              ALU.is_lt, ALU.mult))
                else:
                    go(V.tensor_reduce(poss[:, :, 0:E], pos.rearrange("p t (a e) -> p t e a", a=2), AX.X, ALU.add))
                    settle()
                    for a, m in enumerate((m1, m2)):
                        go(V.scalar_tensor_tensor(kept[:, :, a * E:(a + 1) * E], poss[:, :, 0:E], float(CAP1), m,
                                                  ALU.is_lt, ALU.mult))
                    settle()
                    go(V.tensor_reduce(flag[:, :, :], pairs(kept), AX.X, ALU.add))
                    settle()
                    go(V.tensor_tensor(weight[:, :, :], weight[:, :, :], flag[:, :, :], ALU.mult))
                    settle()
                    normed(weight[:, :, :], weight[:, :, :])
                settle()
                go(V.tensor_tensor(pairs(kept), pairs(kept), bc(weight[:, :, :], [P, T, 2, E]), ALU.mult))
                settle()
                V.tensor_tensor(gate[:, :, 0:E], kept[:, :, 0:E], kept[:, :, E:2 * E], ALU.add).then_inc(gate_ready, 1)

            def gateT_part(L, b):
                E = EXPERTS[L]
                dve.wait_ge(gateT_rounded, L + 1)
                V.tensor_tensor(gateT_lo[0:E, :], bank[b][0:E, 0:N], gateT_hi[0:E, :].bitcast(f32), ALU.subtract)\
                    .then_inc(gateT_ready, 1)

            def gate_hidden(L, banks):
                pairs = 4 if L == 0 else 2

                def lo(j):
                    dve.wait_ge(hid_rounded, 4 * L + j + 1)
                    two = slice(2 * j, 2 * j + 2)
                    V.tensor_tensor(hid_lo[:, two, :], hid[:, two, :], hid_hi[:, two, :].bitcast(f32), ALU.subtract)\
                        .then_inc(hid_ready, 1)

                def scaled(j):
                    dve.wait_ge(up_ready, 8 * L + 2 * j + 2)
                    dve.wait_ge(spread_full, 4 * L + j + 1)
                    two = slice(2 * j, 2 * j + 2)
                    V.tensor_tensor(hid[:, two, :], hid[:, two, :],
                                    bank[banks[j]][:, :].rearrange("p (c n) -> p c n", c=2), ALU.mult)\
                        .then_inc(gated, 1)

                ahead = 3 if L == 0 else 2
                for j in range(ahead):
                    scaled(j)
                for j in range(ahead):
                    lo(j)
                for j in range(ahead, pairs):
                    scaled(j)
                    weight_lo(16)
                    lo(j)

            dve.wait_ge(x_in, 16 * T)
            variances(0, lambda t: xa[:, t, :])
            for t in range(T):
                norm_rows(0, xn[:, t, :], xa[:, t, :], t)
            dve.wait_ge(iota_ready, 1)
            go(V.tensor_copy(iota_bf[:, :], iota_i[:, :]))
            go(V.tensor_copy(iota_f[:, :], iota_i[:, 0:E0]))
            weight_lo(1)
            xT_part(0, (0, 1))
            dve.wait_ge(edges_in, 32)
            go(V.tensor_copy(edges[:, :, :], edges_i[:, :, :]))
            settle()

            def onehots(j0, j1):
                for j in range(j0, j1):
                    if j >= RING:
                        dve.wait_ge(onehot_used, j - RING + 1)
                    for a in range(2):
                        ins = V.tensor_scalar(onehot[:, j % RING, a, :], iota_bf[:, :], edges[:, a, j:j + 1], None,
                                              ALU.is_equal)
                    ins.then_inc(onehot_ready, 1)

            onehots(0, 16)
            k_max(0)
            dve.wait_ge(b_down_in, 16)
            small_split(b_down_hi[:, :], b_down_lo[:, :], b_down1)
            onehots(16, 32)
            q_shift(0, (0, 1))
            onehots(32, 48)
            q_norm(0)
            dve.wait_ge(small_in, SMALLS)
            for t in range(T):
                dve.wait_ge(h_full, t + 1)
                V.tensor_tensor(hr[:, t, :], bank[t][:, :], row["b_gnn0"], ALU.add).then_inc(hr_ready, 1)
            onehots(48, 64)
            dve.wait_ge(narrow_ready, 1)
            for t in range(T):
                dve.wait_ge(cur_rounded, t + 1)
                V.tensor_tensor(cur_lo[:, 0, t, :], hr[:, t, :], cur_hi[:, 0, t, :].bitcast(f32), ALU.subtract)\
                    .then_inc(cur_ready, 1)
                go(V.tensor_scalar(diffused[:, t, :], hr[:, t, :], diffusion[:, 0:1], None, ALU.mult))
            context(6)
            dve.wait_ge(count_ready, 2)
            go(V.tensor_scalar(far[:, :, :], count[:, :, :], 1.0, None, ALU.min))
            settle()
            dve.wait_ge(countT_full, 1)
            go(V.scalar_tensor_tensor(linked[:, :, :], bank[7][:, :].rearrange("p (c n) -> p c n", c=T), 1.0,
                                      far[:, :, :], ALU.min, ALU.max))
            settle()
            for t in range(T):
                sl = linked[:, t, t * P:(t + 1) * P]
                V.tensor_tensor(sl, sl.bitcast(f32), ident[:, :], ALU.add).then_inc(linked_ready, 1)
            dve.wait_ge(linked_ready, 2)
            go(V.tensor_reduce(degree[:, :], linked[:, :, :].bitcast(f32), AX.X, ALU.add))
            settle()
            go(V.tensor_scalar(degree[:, :], degree[:, :], 1.0, None, ALU.max))
            settle()
            V.reciprocal(degree[:, :], degree[:, :]).then_inc(degree_ready, 1)
            dve.wait_ge(degree_ready, 1)
            small_split(narrow_hi[:, 0, :, :], narrow_lo[:, 0, :, :], w_gate[:, :, :])
            for i in range(STEPS):
                go(V.tensor_scalar(degree_w[:, i, :], degree[:, :], diffusion[:, i + 1:i + 2], None, ALU.mult))
            yT_part((4, 5))
            STEPB = ((2, 3), (7, 4), (2, 3))

            def diffuse(i):
                settle()
                for t in range(T):
                    src = bank[STEPB[i][t]][:, :]
                    if i < STEPS - 1:
                        dve.wait_ge(cur_rounded, T * (i + 1) + t + 1)
                        V.scalar_tensor_tensor(cur_lo[:, (i + 1) % 2, t, :], src, degree[:, t:t + 1],
                                               cur_hi[:, (i + 1) % 2, t, :].bitcast(f32), ALU.mult, ALU.subtract)\
                            .then_inc(cur_ready, 1)
                for t in range(T):
                    add_step(i, t)

            def add_step(i, t):
                dve.wait_ge(step_full, T * i + t + 1)
                V.scalar_tensor_tensor(diffused[:, t, :], bank[STEPB[i][t]][:, :], degree_w[:, i, t:t + 1],
                                       diffused[:, t, :], ALU.mult, ALU.add).then_inc(step_read, 1)

            diffuse(0)
            def centred(t):
                go(V.scalar_tensor_tensor(mixed[:, t, :], bank[t][:, :], mv[:, t, 0:1], row["gamma0"],
                                          ALU.subtract, ALU.mult))

            for t in range(T):
                dve.wait_ge(o_full, t + 1)
                variance(1, t, bank[t][:, :])
                if t == 0:
                    centred(0)
            dve.wait_ge(step_read, 2)
            diffuse(1)
            centred(1)
            settle()
            for t in range(T):
                dve.wait_ge(rstd_ready, T + t + 1)
                V.scalar_tensor_tensor(mixed[:, t, :], mixed[:, t, :], rstd[:, t:t + 1], xa[:, t, :],
                                       ALU.mult, ALU.add).then_inc(mix_ready, 1)
            dve.wait_ge(step_read, 4)
            dve.wait_ge(mix_ready, 2)
            for t in range(T):
                add_step(2, t)
            for t in range(T):
                dve.wait_ge(step_read, 4 + t + 1)
                go(V.scalar_tensor_tensor(xb[:, t, :], diffused[:, t, :], 0.0, mixed[:, t, :], ALU.max, ALU.add))
            variances(2, lambda t: xb[:, t, :])
            dve.wait_ge(xT_full, 2)
            for t in range(T):
                norm_rows(2, xn[:, t, :], xb[:, t, :], t)
            for g in range(2):
                w = slice(0, 2 * H) if g == 0 else slice(2 * H, A2)
                dve.wait_ge(wa_read, g + 1)
                go(V.tensor_copy(wa_hi[:, :, w], wa[:, :, w]))
                settle()
                V.tensor_tensor(wa_lo[:, :, w], wa[:, :, w], wa_hi[:, :, w].bitcast(f32), ALU.subtract)\
                    .then_inc(wa_ready, 1)
            xT_part(1, (4, 5))
            gates(0, 6, 7)
            gateT_part(0, 6)
            gate_hidden(0, (4, 5, 7, 6))
            small_split(narrow_hi[:, 1, :, 0:EXPERTS[1]], narrow_lo[:, 1, :, 0:EXPERTS[1]], w_router[:, :, :])
            dve.wait_ge(countT_ready, 1)
            for t in range(T):
                for m in (count, countT):
                    sl = m[:, t, t * P:(t + 1) * P]
                    go(V.tensor_tensor(sl, sl, ident[:, :], ALU.add))
            settle()
            go(V.tensor_scalar(far[:, :, :], count[:, :, :], 0.0, -FAR, ALU.is_equal, ALU.mult))
            weight_lo(19)
            dve.wait_ge(xT_full, 4)
            for t in range(T):
                dve.wait_ge(down_full, t + 1)
                go(V.tensor_tensor(xa[:, t, :], bank[t][:, :], xb[:, t, :], ALU.add))
                settle()
                variance(3, t, xa[:, t, :])
                if t:
                    xT_part(2, (4, 5), (0,))
                norm_rows(3, xn[:, t, :], xa[:, t, :], t)
            xT_part(2, (4, 5), (1,))

            def alT_part(g, b):
                k = (2 * H, 2)[g]
                dve.wait_ge(alT_rounded, g + 1)
                V.tensor_tensor(alT_lo[0:k, :], bank[b][0:k, 0:N], alT_hi[0:k, :].bitcast(f32), ALU.subtract)\
                    .then_inc(alT_ready, 1)

            alT_part(0, 6)
            PAIR = (0, 1, 6, 7)
            for j in range(4):
                dve.wait_ge(src_full, j + 1)
                settle(3 if j else 0)
                if j > 1:
                    dve.wait_ge(max_ready, j - 1)
                for h in range(2):
                    for t in range(T):
                        if h or t:
                            go(ins)
                        ins = V.tensor_tensor_reduce(out=junk[j % 2][:, 2 * h + t, :], in0=half(PAIR[j], h),
                                                     in1=far[:, t, :], scale=1.0, scalar=-BIG, op0=ALU.add, op1=ALU.max,
                                                     accum_out=mx[:, t, 2 * j + h:2 * j + h + 1])
                ins.then_inc(max_ready, 1)
            dve.wait_ge(max_ready, 4)
            dve.wait_ge(al_ready, 1)
            go(V.tensor_tensor(mx[:, :, :], mx[:, :, :], al[:, :, H:2 * H], ALU.add))
            settle()
            go(V.scalar_tensor_tensor(mx[:, :, :], mx[:, :, :], SLOPE, mx[:, :, :], ALU.mult, ALU.max))
            settle()
            go(V.tensor_tensor(less[:, :, 0:H], al[:, :, H:2 * H], mx[:, :, :], ALU.subtract))
            V.scalar_tensor_tensor(less[:, :, H:2 * H], al[:, :, H:2 * H], SLOPE, mx[:, :, :],
                                   ALU.mult, ALU.subtract).then_inc(max_ready, 1)
            go(V.tensor_scalar(al_slope[:, :, :], al[:, :, 0:H], SLOPE, None, ALU.mult))

            def less_max(j):
                dve.wait_ge(max_full, j + 1)
                for s in range(T):
                    for h in range(2):
                        dve.wait_ge(z_ready, 4 * j + 2 * s + h + 1)
                        hh = 2 * j + h
                        z = logit[:, s, hh, :]
                        ins = V.scalar_tensor_tensor(z, half((1, 7)[j % 2], h), al_slope[:, s, hh:hh + 1], z,
                                                     ALU.add, ALU.max)
                    ins.then_inc(shifted, 1)

            def edge_weights(j):
                for s in range(T):
                    dve.wait_ge(exp_ready, 2 * j + s + 1)
                    z = logit[:, s, 2 * j:2 * j + 2, :]
                    V.scalar_tensor_tensor(z, z, BIG, countT[:, s:s + 1, :].broadcast_to([P, 2, N]), ALU.min, ALU.mult)\
                        .then_inc(weight_ready, 1)

            k_max(1, (0,))
            dve.wait_ge(mT_rounded, 1)
            V.tensor_tensor(mT_lo[:, :], bank[2][0:2 * H, 0:N], mT_hi[:, :].bitcast(f32), ALU.subtract)\
                .then_inc(mT_ready, 1)
            settle()
            less_max(0)
            less_max(1)
            k_max(1, (1,))
            less_max(2)
            edge_weights(0)
            less_max(3)
            edge_weights(1)
            dve.wait_ge(ekT_ready, 8)
            V.reciprocal(kinv[:, :], ksum[:, :]).then_inc(kinv_ready, 1)
            q_shift(1, (2, 3))
            edge_weights(2)
            edge_weights(3)

            def gat_norm(g, i):
                gg, beta = (("g1", "beta1"), ("g2", "beta2"))[g]
                variances(i, lambda t: g_a[:, t, :])
                for t in range(T):
                    go(V.scalar_tensor_tensor(g_a[:, t, :], g_a[:, t, :], mv[:, t, 0:1], row[gg],
                                              ALU.subtract, ALU.mult))
                for t in range(T):
                    settle(T - 1 - t)
                    dve.wait_ge(rstd_ready, T * i + t + 1)
                    V.scalar_tensor_tensor(g_a[:, t, :], g_a[:, t, :], rstd[:, t:t + 1], row[beta],
                                           ALU.mult, ALU.add).then_inc(y_ready, 1)

            def elu(g, dst, base, work, then):
                for t in range(T):
                    dve.wait_ge(y_ready, T * g + t + 1)
                    go(V.scalar_tensor_tensor(work[:, t, :], g_a[:, t, :], 0.0, base(t), ALU.max, ALU.add))
                for t in range(T):
                    settle()
                    dve.wait_ge(elu_exp, T * g + t + 1)
                    then(V.scalar_tensor_tensor(dst[:, t, :], g_b[:, t, :], 1.0, work[:, t, :], ALU.min, ALU.add))

            AGG = ((0, 6), (1, 7))

            def divided(u):
                def src(t):
                    return bank[AGG[t][u]][:, 0:4 * (HD + 1)].rearrange("p (h n) -> p h n", h=4)

                heads, cols = slice(4 * u, 4 * u + 4), slice(4 * u * HD, 4 * (u + 1) * HD)
                for t in range(T):
                    dve.wait_ge(agg_full, 2 * u + t + 1)
                    go(V.reciprocal(mx[:, t, heads], src(t)[:, :, HD]))
                for t in range(T):
                    settle(T - 1)
                    go(V.tensor_tensor(g_a[:, t, cols].rearrange("p (h n) -> p h n", h=4), src(t)[:, :, 0:HD],
                                       bc(mx[:, t, heads], [P, 4, HD]), ALU.mult))
                for t in range(T):
                    settle(T - 1)
                    go(V.tensor_tensor(g_a[:, t, cols], g_a[:, t, cols], row["b1"][:, cols], ALU.add))

            q_norm(1)
            divided(0)
            divided(1)
            gat_norm(0, 4)
            dve.wait_ge(xn_less_one, 1)
            elu(0, x1g, lambda t: xn[:, t, :], xn, lambda ins: ins.then_inc(xn_ready, 1))
            xT_part(3, (4, 3))
            alT_part(1, 7)
            dve.wait_ge(src_full, 5)
            for t in range(T):
                go(V.tensor_tensor_reduce(out=junk[0][:, t, :], in0=half(2, 0), in1=far[:, t, :],
                                          scale=1.0, scalar=-BIG, op0=ALU.add, op1=ALU.max, accum_out=mx[:, t, 0:1]))
            dve.wait_ge(al_ready, 2)
            settle()
            go(V.tensor_tensor(mx[:, :, 0:1], mx[:, :, 0:1], al[:, :, 1:2], ALU.add))
            settle()
            V.scalar_tensor_tensor(mz[:, :, 0:1], mx[:, :, 0:1], SLOPE, mx[:, :, 0:1], ALU.mult, ALU.max)\
                .then_inc(max_ready, 1)
            dve.wait_ge(z_ready, 18)
            z = logit[:, :, 0, :]
            go(V.scalar_tensor_tensor(z, z, SLOPE, z, ALU.mult, ALU.max))
            settle()
            dve.wait_ge(mT_rounded, 2)
            V.tensor_tensor(mT_lo[0:1, :], bank[6][0:1, 0:N], mT_hi[0:1, :].bitcast(f32), ALU.subtract)\
                .then_inc(mT_ready, 1)
            dve.wait_ge(max_full, 5)
            for s in range(T):
                V.tensor_tensor(logit[:, s, 0, :], logit[:, s, 0, :], half(7, 0), ALU.subtract).then_inc(shifted, 1)
            for s in range(T):
                dve.wait_ge(exp_ready, 8 + s + 1)
                V.scalar_tensor_tensor(logit[:, s, 0, :], logit[:, s, 0, :], BIG, countT[:, s, :], ALU.min, ALU.mult)\
                    .then_inc(weight_ready, 1)
            go(V.scalar_tensor_tensor(mixed[:, :, :], x1g[:, :, :], -1.0, xa[:, :, :], ALU.add, ALU.add))
            settle()
            V.tensor_tensor(mixed[:, :, :], mixed[:, :, :], row["b_out1"].unsqueeze(1).broadcast_to([P, T, D]),
                            ALU.add).then_inc(mix_ready, 1)
            dve.wait_ge(sum_full, 1)
            for t in range(T):
                go(V.reciprocal(mx[:, t, 1:2], bank[(2, 6)[t]][:, 0:1]))
            settle()
            for t in range(T):
                dve.wait_ge(agg_full, 4 + t + 1)
                go(V.scalar_tensor_tensor(g_a[:, t, :], bank[(3, 7)[t]][:, :], mx[:, t, 1:2], row["b2"],
                                          ALU.mult, ALU.add))
            gat_norm(1, 5)
            def summed(t):
                dve.wait_ge(o_full, 2 + t + 1)
                return bank[t][:, :]

            elu(1, xb, summed, mixed, go)
            variances(6, lambda t: xb[:, t, :])
            for t in range(T):
                norm_rows(6, xn[:, t, :], xb[:, t, :], t)
            xT_part(4, (3, 4))
            gates(1, 5, 6)
            gateT_part(1, 7)
            gate_hidden(1, (2, 5))
            for t in range(T):
                dve.wait_ge(down_full, 2 + t + 1)
                V.tensor_tensor(xa[:, t, :], bank[3 + t][:, :], xb[:, t, :], ALU.add).then_inc(out_ready, 1)

        @block.tensor
        def _(pe):
            mm = nc.tensor.matmul

            def product(dst, lhs, rhs, k):
                for c in range(k):
                    ins = mm(dst, lhs(c), rhs(c), start=c == 0, stop=c == k - 1)
                return ins

            def split_product(dst, lhs, rhs, k, part=None, late=None, open_end=False):
                if late:
                    first_products(dst, lhs, rhs, k, late[0])
                    pe.wait_ge(*late[1])
                    return last_products(dst, lhs, rhs, k, late[0])
                for c in part or range(k):
                    (l_hi, l_lo), (r_hi, r_lo) = lhs(c), rhs(c)
                    mm(dst, l_hi, r_hi, start=c == 0, stop=False)
                    mm(dst, l_hi, r_lo, start=False, stop=False)
                    ins = mm(dst, l_lo, r_hi, start=False, stop=c == k - 1 and not open_end)
                return ins

            def first_products(dst, lhs, rhs, k, side):
                for c in range(k):
                    (l_hi, l_lo), (r_hi, r_lo) = lhs(c), rhs(c)
                    mm(dst, l_hi, r_hi, start=c == 0, stop=False)
                    if side == "lhs":
                        mm(dst, l_hi, r_lo, start=False, stop=False)
                    else:
                        mm(dst, l_lo, r_hi, start=False, stop=False)

            def last_products(dst, lhs, rhs, k, side, open_end=False):
                for c in range(k):
                    (l_hi, l_lo), (r_hi, r_lo) = lhs(c), rhs(c)
                    l, r = (l_lo, r_hi) if side == "lhs" else (l_hi, r_lo)
                    ins = mm(dst, l, r, start=False, stop=c == k - 1 and not open_end)
                return ins

            def xT_at(c, t=None):
                cols = slice(0, N) if t is None else slice(t * P, (t + 1) * P)
                return xT_hi[:, c, cols], xT_lo[:, c, cols]

            def weights_in(w):
                for s, n in dict(lo_done(u) for u in range(w.first, w.first + w.units)).items():
                    pe.wait_ge(s, n)

            def xT_made(i, src, banks, tiles=range(T)):
                for t in tiles:
                    pe.wait_ge(xn_ready, T * i + t + 1)
                    for c in range(C):
                        ins = nc.tensor.transpose(bank[banks[t]][:, c * P:(c + 1) * P], src[:, t, c * P:(c + 1) * P],
                                                  ident[:, :])
                    ins.then_inc(xT_full, 1)

            def rows_of(name, banks, full, i, tiles=range(T)):
                w = Weight(name)
                weights_in(w)
                for t in tiles:
                    pe.wait_ge(xT_ready, T * i + t + 1)
                    split_product(bank[banks[t]][:, :], lambda c: xT_at(c, t), w.at, C).then_inc(full, 1)

            def k_of(name, full, parts=range(C), late=None):
                w = Weight(name)
                weights_in(w)
                for m in parts:
                    ins = split_product(half(4 + m // 2, m % 2), lambda c: w.at(c, m * P, (m + 1) * P), xT_at, C,
                                        late=None if m else late)
                    if m % 2:
                        ins.then_inc(full, 1)

            def ek_made(L, banks):
                for t in range(T):
                    for m in range(C):
                        ins = nc.tensor.transpose(bank[banks[t]][:, m * P:(m + 1) * P], ekT[:, m, t * P:(t + 1) * P],
                                                  ident[:, :])
                    ins.then_inc(ek_full, 1)

            def qT_made(banks):
                for j in range(2):
                    for m in (2 * j, 2 * j + 1):
                        for t in range(T):
                            o = (m % 2) * N + t * P
                            ins = nc.tensor.transpose(bank[banks[j]][:, o:o + P], q[:, t, m * P:(m + 1) * P],
                                                      ident[:, :])
                    ins.then_inc(qT_full, 1)

            def context(b):
                for m in range(C):
                    cols = slice(m * P, (m + 1) * P)
                    ins = product(bank[b][:, cols], lambda t: ek[:, t, cols], lambda t: v[:, t, cols], T)
                ins.then_inc(ctx_full, 1)

            def yT_made(L, banks):
                for m in range(C):
                    ins = mm(half(banks[m // 2], m % 2), ctxbd[:, m, :], qT[:, m, :], start=True, stop=True)
                    if m % 2:
                        ins.then_inc(yT_full, 1)

            def attn_out(name, banks, tiles):
                w = Weight(name)
                weights_in(w)
                for t in tiles:
                    cols = slice(t * P, (t + 1) * P)
                    ins = split_product(bank[banks[t]][:, :], lambda m: (yT_hi[:, m, cols], yT_lo[:, m, cols]),
                                        w.at, C)
                    ins.then_inc(o_full, 1)

            def selected(dst, selector, rows_hi, rows_lo):
                mm(dst, selector, rows_hi, start=True, stop=False)
                return mm(dst, selector, rows_lo, start=False, stop=True)

            def positions(L, b):
                E2 = 2 * EXPERTS[L]
                E = EXPERTS[L]
                pe.wait_ge(masks_ready, L + 1)
                mm(bank[b][:, 0:E2], before[:, :], mask[:, 0, 0:E2], start=True, stop=True)
                mm(bank[b][:, E2:2 * E2], ones[:, :], mask[:, 0, 0:E2], start=True, stop=False)
                mm(bank[b][:, E2:2 * E2], before[:, :], mask[:, 1, 0:E2], start=False, stop=True)
                mm(bank[b][:, 2 * E2:2 * E2 + E], ones[:, :], mask[:, 0, 0:E], start=True, stop=False)
                mm(bank[b][:, 2 * E2:2 * E2 + E], ones[:, :], mask[:, 1, 0:E], start=False, stop=True)\
                    .then_inc(pos_full, 1)

            def gate_rows(L, b):
                E = EXPERTS[L]
                pe.wait_ge(gate_ready, L + 1)
                for t in range(T):
                    ins = nc.tensor.transpose(bank[b][0:E, t * P:(t + 1) * P], gate[:, t, 0:E], ident[:, :])
                ins.then_inc(gateT_full, 1)

            def gate_spread(L, banks):
                E = EXPERTS[L]
                pe.wait_ge(gateT_ready, L + 1)
                for m in range(len(banks) * 2):
                    ins = selected(half(banks[m // 2], m % 2), spread[0:E, m, :, :].rearrange("p a f -> p (a f)"),
                                   gateT_hi[0:E, :], gateT_lo[0:E, :])
                    if m % 2:
                        ins.then_inc(spread_full, 1)

            def up(name, m0, m1, part=range(C)):
                w = Weight(name)
                weights_in(w)
                for m in range(m0, m1):
                    ins = split_product(half(m // 2, m % 2), lambda c: w.at(c, m * P, (m + 1) * P), xT_at, C, part)
                    if m % 2 and C - 1 in part:
                        ins.then_inc(up_full, 1)

            def down(name, t, dst, k, L, opened, part=None):
                w = Weight(name)
                cols = slice(t * P, (t + 1) * P)
                for m in part or range(k):
                    if t == 0:
                        pe.wait_ge(hid_ready, 4 * L + m // 2 + 1)
                        if m % 2 == 0:
                            pe.wait_ge(*lo_done(w.first + m // 2))
                    h_hi, h_lo = hid_hi[:, m, cols], hid_lo[:, m, cols]
                    r_hi, r_lo = w.at(m)
                    mm(dst, h_hi, r_hi, start=m == 0 and not opened, stop=False)
                    mm(dst, h_hi, r_lo, start=False, stop=False)
                    ins = mm(dst, h_lo, r_hi, start=False, stop=m == k - 1)
                if m == k - 1:
                    ins.then_inc(down_full, 1)

            def narrow_rows(dst, hi, lo, cols, i):
                pe.wait_ge(xT_rounded, T * i + T)
                return split_product(dst, lambda c: (hi[:, c, cols], lo[:, c, cols]), xT_at, C,
                                     late=("rhs", (xT_ready, T * i + T)))

            def logit_rows(b, L, i):
                E = EXPERTS[L]
                narrow_rows(bank[b][0:E, 0:N], narrow_hi[:, L, :, :], narrow_lo[:, L, :, :], slice(0, E), i)\
                    .then_inc(lgT_full, 1)

            def logits(b, L):
                E = EXPERTS[L]
                pe.wait_ge(lgT_ready, L + 1)
                for t in range(T):
                    ins = nc.tensor.transpose(bank[b][:, N + t * E:N + (t + 1) * E], lgT[0:E, t * P:(t + 1) * P],
                                              ident[0:E, 0:E])
                ins.then_inc(logits_full, 1)

            def attention_weights(g, b, parts=range(C)):
                wt = w2t if g else w1t
                pe.wait_ge(w2t_in if g else w1t_in, 16)
                for kc in parts:
                    o = kc * A2 + (2 * H if g else 0)
                    ins = product(bank[b][:, o:o + (2 if g else 2 * H)], lambda m: wt[:, m, kc * P:(kc + 1) * P],
                                  (lambda m: att2[:, :, m]) if g else (lambda m: attblk[:, m, :]), C)
                if kc == C - 1:
                    ins.then_inc(wa_full, 1)

            pe.wait_ge(consts, 1)
            xT_made(0, xn, (0, 1))
            pe.wait_ge(xT_rounded, 2)
            k_of("k0", k_full, late=("rhs", (xT_ready, 2)))

            def counts(j0, j1):
                for j in range(j0, j1):
                    pe.wait_ge(onehot_ready, j + 1)
                    for t in range(T):
                        ins = mm(half(COUNTB[t], 0), onehot[:, j % RING, 1, t * P:(t + 1) * P],
                                 onehot[:, j % RING, 0, :], start=j == 0, stop=j == ET - 1)
                    if j < ET - 1:
                        ins.then_inc(onehot_used, 1)
                return ins

            COUNTB = (2, 3)
            rows_of("q0", (0, 1), q_full, 0)
            counts(0, 16)
            rows_of("v0", (6, 7), v_full, 0)
            counts(16, 32)
            pe.wait_ge(q_shifted, 2)
            rows_of("gnn0", (0, 1), h_full, 0)
            counts(32, 48)
            pe.wait_ge(ekT_ready, 4)
            ek_made(0, (4, 5))
            pe.wait_ge(hr_ready, 2)
            pe.wait_ge(q_ready, 2)
            qT_made((0, 1))
            pe.wait_ge(v_ready, 2)
            pe.wait_ge(ek_ready, 2)
            context(6)
            counts(48, 64).then_inc(count_full, 1)
            pe.wait_ge(ctx_ready, 2)
            pe.wait_ge(qT_ready, 2)
            yT_made(0, (4, 5))
            pe.wait_ge(count_ready, 2)
            for s in range(T):
                for t in range(T):
                    ins = nc.tensor.transpose(bank[7][:, s * N + t * P:s * N + (t + 1) * P],
                                              count[:, t, s * P:(s + 1) * P], ident[:, :])
            ins.then_inc(countT_full, 1)

            def diffuse(i, banks):
                for t in range(T):
                    for s in range(T):
                        adj = linked[:, s, t * P:(t + 1) * P]
                        mm(bank[banks[t]][:, :], adj, cur_hi[:, i % 2, s, :], start=s == 0, stop=False)
                        ins = mm(bank[banks[t]][:, :], adj, cur_lo[:, i % 2, s, :], start=False, stop=s == T - 1)
                    ins.then_inc(step_full, 1)

            out0 = Weight("out0")
            weights_in(out0)
            pe.wait_ge(yT_rounded, 2)
            first_products(bank[0][:, :], lambda m: (yT_hi[:, m, 0:P], yT_lo[:, m, 0:P]), out0.at, C, "lhs")
            pe.wait_ge(linked_ready, 2)
            pe.wait_ge(cur_ready, 2)
            diffuse(0, (2, 3))
            pe.wait_ge(consts, 2)
            attention_weights(0, 6, (0, 1))
            pe.wait_ge(yT_ready, 2)
            last_products(bank[0][:, :], lambda m: (yT_hi[:, m, 0:P], yT_lo[:, m, 0:P]), out0.at, C, "lhs")\
                .then_inc(o_full, 1)
            attn_out("out0", (0, 1), (1,))
            pe.wait_ge(cur_ready, 4)
            diffuse(1, (7, 4))
            attention_weights(0, 6, (2, 3))
            pe.wait_ge(cur_ready, 6)
            pe.wait_ge(step_read, 2)
            diffuse(2, (2, 3))
            attention_weights(1, 5)
            pe.wait_ge(wa_read, 2)
            pe.wait_ge(step_read, 4)
            xT_made(1, xn, (4, 5))
            pe.wait_ge(narrow_ready, 2)
            logit_rows(6, 0, 1)
            pe.wait_ge(mix_ready, 2)
            pe.wait_ge(step_read, 6)
            up("up0", 0, 1, (0, 1))
            logits(6, 0)
            up("up0", 0, 1, (2, 3))
            up("up0", 1, 4)
            positions(0, 7)
            up("up0", 4, 6)
            gate_rows(0, 6)
            up("up0", 6, 7)
            gate_spread(0, (4, 5, 7, 6))
            up("up0", 7, 8)
            for part in (range(0, 4), range(4, 8)):
                for t in range(T):
                    down("down0", t, bank[t][:, :], 8, 0, False, part)

            xT_made(2, xn, (4, 5), (0,))
            gat1 = Weight("gat1")
            weights_in(gat1)
            pe.wait_ge(xT_rounded, 5)
            first_products(bank[2][:, :], lambda c: xT_at(c, 0), gat1.at, C, "lhs")
            xT_made(2, xn, (4, 5), (1,))
            pe.wait_ge(xT_ready, 5)
            last_products(bank[2][:, :], lambda c: xT_at(c, 0), gat1.at, C, "lhs").then_inc(hx_full, 1)
            pe.wait_ge(wa_ready, 2)

            def node_rows(g, b, i):
                k, o = ((2 * H, 0), (2, 2 * H))[g]
                narrow_rows(bank[b][0:k, 0:N], wa_hi, wa_lo, slice(o, o + k), i).then_inc(alT_full, 1)

            def node_terms(g, b):
                k = (2 * H, 2)[g]
                for t in range(T):
                    dst, cols = bank[b][:, N + t * k:N + (t + 1) * k], slice(t * P, (t + 1) * P)
                    mm(dst, alT_hi[0:k, cols], pick[0:k, 0:k, 0], start=True, stop=False)
                    ins = mm(dst, alT_lo[0:k, cols], pick[0:k, 0:k, 0], start=False, stop=True)
                ins.then_inc(al_full, 1)

            node_rows(0, 6, 2)
            PAIR = (0, 1, 6, 7)

            def broadcast(b, row, rows_hi, rows_lo, full):
                for h in range(2):
                    ins = selected(half(b, h), pick[:, row + h, :], rows_hi, rows_lo)
                ins.then_inc(full, 1)

            pe.wait_ge(alT_ready, 1)
            for j in range(4):
                broadcast(PAIR[j], 2 * j, alT_hi, alT_lo, src_full)
            node_terms(0, 4)
            rows_of("gat1", (2, 3), hx_full, 2, (1,))
            pe.wait_ge(al_ready, 1)
            k_of("k1", k_full, (0, 1))
            pe.wait_ge(max_ready, 5)
            pe.wait_ge(hx_ready, 1)
            for t in range(T):
                ins = nc.tensor.transpose(bank[2][0:2 * H, t * P:(t + 1) * P], less[:, t, :], ident[:, :])
            ins.then_inc(mT_full, 1)
            k_of("k1", k_full, (2,))

            def target_rows(j):
                if j >= 2:
                    pe.wait_ge(shifted, 2 * (j - 2) + 2)
                broadcast((0, 6)[j % 2], 2 * j, mT_hi, mT_lo, dst_full)
                broadcast((1, 7)[j % 2], H + 2 * j, mT_hi, mT_lo, max_full)

            pe.wait_ge(mT_ready, 1)
            target_rows(0)
            target_rows(1)
            k_of("k1", k_full, (3,))
            target_rows(2)
            q1 = Weight("q1")
            weights_in(q1)
            split_product(bank[2][:, :], lambda c: xT_at(c, 0), q1.at, C, (0, 1))
            target_rows(3)
            split_product(bank[2][:, :], lambda c: xT_at(c, 0), q1.at, C, (2, 3)).then_inc(q_full, 1)
            pe.wait_ge(hx_ready, 2)
            rows_of("q1", (2, 3), q_full, 2, (1,))
            pe.wait_ge(ekT_ready, 8)
            rows_of("v1", (5, 4), v_full, 2, (0,))
            AGG = ((0, 6), (1, 7))

            def aggregate(u):
                pe.wait_ge(weight_ready, 4 * u + 4)
                pe.wait_ge(shifted, 2 * u + 6)
                for t in range(T):
                    for h in range(4 * u, 4 * u + 4):
                        o = (h % 4) * (HD + 1)
                        ins = product(bank[AGG[t][u]][:, o:o + HD + 1],
                                      lambda s: logit[:, s, h, t * P:(t + 1) * P], lambda s: hx[:, s, h, :], T)
                    ins.then_inc(agg_full, 1)

            aggregate(0)
            aggregate(1)
            rows_of("v1", (5, 4), v_full, 2, (1,))
            pe.wait_ge(q_shifted, 4)
            ek_made(1, (2, 3))
            pe.wait_ge(q_ready, 4)
            pe.wait_ge(v_ready, 4)
            qT_made((4, 5))
            pe.wait_ge(ek_ready, 4)
            context(3)
            pe.wait_ge(ctx_ready, 4)
            pe.wait_ge(qT_ready, 2 + C)
            yT_made(1, (5, 2))
            xT_made(3, x1g, (4, 3))
            out1 = Weight("out1")
            weights_in(out1)
            pe.wait_ge(yT_rounded, 4)
            first_products(bank[0][:, :], lambda m: (yT_hi[:, m, 0:P], yT_lo[:, m, 0:P]), out1.at, C, "lhs")
            node_rows(1, 7, 3)
            pe.wait_ge(yT_copied, 2)
            gat2 = Weight("gat2")
            weights_in(gat2)
            split_product(bank[5][:, :], lambda c: xT_at(c, 0), gat2.at, C, (0,))
            pe.wait_ge(alT_ready, 2)
            for a in range(2):
                ins = selected(half((2, 3)[a], 0), pick[0:2, a, :], alT_hi[0:2, :], alT_lo[0:2, :])
            ins.then_inc(src_full, 1)
            node_terms(1, 7)
            split_product(bank[5][:, :], lambda c: xT_at(c, 0), gat2.at, C, (1,))
            pe.wait_ge(max_ready, 6)
            for t in range(T):
                ins = nc.tensor.transpose(bank[6][0:1, t * P:(t + 1) * P], mz[:, t, 0:1], ident[:, :])
            ins.then_inc(mT_full, 1)
            split_product(bank[5][:, :], lambda c: xT_at(c, 0), gat2.at, C, (2, 3)).then_inc(hx_full, 1)
            pe.wait_ge(mT_ready, 2)
            selected(half(7, 0), pick[0:1, 0, :], mT_hi[0:1, :], mT_lo[0:1, :]).then_inc(max_full, 1)
            rows_of("gat2", (5, 4), hx_full, 3, (1,))
            pe.wait_ge(weight_ready, 10)
            for t in range(T):
                ins = product(bank[(2, 6)[t]][:, 0:1], lambda s: logit[:, s, 0, t * P:(t + 1) * P],
                              lambda s: ones[:, 0:1], T)
            ins.then_inc(sum_full, 1)
            pe.wait_ge(hx_ready, 4)
            for t in range(T):
                product(bank[(3, 7)[t]][:, :], lambda s: logit[:, s, 0, t * P:(t + 1) * P], lambda s: h2[:, s, :], T)\
                    .then_inc(agg_full, 1)
            pe.wait_ge(yT_ready, 4)
            last_products(bank[0][:, :], lambda m: (yT_hi[:, m, 0:P], yT_lo[:, m, 0:P]), out1.at, C, "lhs",
                          open_end=True)
            pe.wait_ge(mix_ready, 3)
            for t in range(T):
                if t:
                    split_product(bank[t][:, :], lambda m: (yT_hi[:, m, P:2 * P], yT_lo[:, m, P:2 * P]), out1.at, C,
                                  open_end=True)
                mm(bank[t][:, :], ident[:, :], mixed[:, t, :], start=False, stop=True).then_inc(o_full, 1)
            xT_made(4, xn, (3, 4))
            pe.wait_ge(narrow_ready, 3)
            logit_rows(5, 1, 4)
            up("up1", 0, 1, (0,))
            logits(5, 1)
            up("up1", 0, 1, (1, 2, 3))
            up("up1", 1, 2)
            up("up1", 2, 3, (0, 1))
            positions(1, 6)
            up("up1", 2, 3, (2, 3))
            up("up1", 3, C, (0, 1))
            gate_rows(1, 7)
            up("up1", 3, C, (2, 3))
            gate_spread(1, (2, 5))
            for t in range(T):
                dst = bank[3 + t][:, :]
                cols = slice(t * P, (t + 1) * P)
                g_hi, g_lo = gateT_hi[0:EXPERTS[1], cols], gateT_lo[0:EXPERTS[1], cols]
                mm(dst, g_hi, b_down_hi[:, :], start=True, stop=False)
                mm(dst, g_hi, b_down_lo[:, :], start=False, stop=False)
                mm(dst, g_lo, b_down_hi[:, :], start=False, stop=False)
            for part in (range(0, 2), range(2, C)):
                for t in range(T):
                    down("down1", t, bank[3 + t][:, :], C, 1, True, part)


def _chunks(a):
    c = a.shape[0] // 128
    return a.reshape(c, 128, -1).transpose(1, 0, 2)


def kernel(**inputs):
    import numpy as np
    import concourse.bacc as bacc
    from concourse import mybir
    from concourse.bass_utils import run_bass_kernel_spmd

    a = {k: np.asarray(v) for k, v in inputs.items()}
    hidden = 512
    wq0, wk0, wv0 = (a["L0_mix_w_qkv"][i * hidden:(i + 1) * hidden].T for i in range(3))
    wq1, wk1, wv1 = (a["L1_mix_W_qkv"][:, i * hidden:(i + 1) * hidden] for i in range(3))

    def experts_in(w):
        return _chunks(w.transpose(1, 0, 2).reshape(w.shape[1], -1))

    def experts_out(w):
        return _chunks(w.reshape(-1, w.shape[2]))

    def column(v):
        return v.reshape(-1, 128).T

    arrays = {
        "x": a["x"], "src": a["src"], "dst": a["dst"],
        "k0": _chunks(wk0), "q0": _chunks(wq0), "v0": _chunks(wv0),
        "gnn0": _chunks(a["L0_gnn_W"]), "out0": _chunks(a["L0_mix_w_out"].T),
        "b_gnn0": a["L0_gnn_b"], "diffusion": a["L0_gnn_diffusion_weights"], "gamma0": a["L0_mix_gamma"],
        "gate": _chunks(a["L0_ffn_w_gating"]), "up0": experts_in(a["L0_ffn_w1"]),
        "down0": experts_out(a["L0_ffn_w2"]),
        "gat1": _chunks(a["L1_gnn_W1"]), "w1t": _chunks(a["L1_gnn_W1"].T),
        "gat2": _chunks(a["L1_gnn_W2"]), "w2t": _chunks(a["L1_gnn_W2"].T),
        "a_src1": column(a["L1_gnn_a_src1"]), "a_dst1": column(a["L1_gnn_a_dst1"]),
        "a_src2": column(a["L1_gnn_a_src2"]), "a_dst2": column(a["L1_gnn_a_dst2"]),
        "b1": a["L1_gnn_b1"], "g1": a["L1_gnn_g1"], "beta1": a["L1_gnn_beta1"],
        "b2": a["L1_gnn_b2"], "g2": a["L1_gnn_g2"], "beta2": a["L1_gnn_beta2"],
        "k1": _chunks(wk1), "q1": _chunks(wq1), "v1": _chunks(wv1),
        "out1": _chunks(a["L1_mix_W_out"]), "b_out1": a["L1_mix_b_out"],
        "router": _chunks(a["L1_ffn_Wr"]), "b_router": a["L1_ffn_br"],
        "up1": experts_in(a["L1_ffn_W1"]), "b_up1": column(a["L1_ffn_b1"]),
        "down1": experts_out(a["L1_ffn_W2"]), "b_down1": a["L1_ffn_b2"],
    }
    arrays = {k: np.ascontiguousarray(v) for k, v in arrays.items()}
    nc = bacc.Bacc("TRN2", target_bir_lowering=False, num_devices=1)
    aps = {k: nc.dram_tensor("in_" + k, v.shape, mybir.dt.from_np(v.dtype), kind="ExternalInput").ap()
           for k, v in arrays.items()}
    out = nc.dram_tensor("out", a["x"].shape, mybir.dt.from_np(a["x"].dtype), kind="ExternalOutput").ap()
    gps_two_layers(nc, aps, out)
    r = run_bass_kernel_spmd(nc, [{"in_" + k: v for k, v in arrays.items()}], core_ids=[0])
    return r.results[0]["out"]
```
